# Optimizing a Trainium2 kernel written in Bass

```python
import numpy as np
import jax
import jax.numpy as jnp

def _softmax(x, axis=-1):
    return jax.nn.softmax(x, axis=axis)
def _gelu(x):
    return jax.nn.gelu(x, approximate=True)
def _silu(x):
    return jax.nn.silu(x)
def _sigmoid(x):
    return jax.nn.sigmoid(x)
def _layernorm(x, axis=-1, eps=1e-5):
    m = jnp.mean(x, axis=axis, keepdims=True)
    v = jnp.var(x, axis=axis, keepdims=True)
    return (x - m) / jnp.sqrt(v + eps)
def _scatter_add(tgt, idx, src, axis=0):
    return tgt.at[idx].add(src)
def _segment_sum(src, seg, n):
    return jax.ops.segment_sum(src, seg, n)

kernel_name = 'mk_adj_seq_d4_adj_128_a8b0b7'

def setup_inputs(seed: int = 0):
    np.random.seed(seed)
    _w = jnp.asarray
    def _rec_inputs():
        import jax
        import jax.numpy as jnp
        _gk = jax.random.key(seed)
        x = -0.0002928 + 1 * jax.random.normal(jax.random.fold_in(_gk, 1), (8, 2048, 128), jnp.float32)
        _w = (1.0 + jnp.arange(2048, dtype=jnp.float32)) ** -0.5
        _w = _w / _w.mean()
        _pij = jnp.clip(0.00390625 * _w[:, None] * _w[None, :], 0.0, 1.0)
        _a = jax.random.uniform(jax.random.fold_in(_gk, 2), (2048, 2048)) < _pij
        _a = jnp.logical_or(_a, jnp.eye(2048, dtype=bool))
        adj = _a.astype(jnp.int32)
        return x, adj
    x, adj = _rec_inputs()
    def _L0_gnn_setup():
        import jax, jax.numpy as jnp
        import numpy as np
        B, K, D = (16, 2048, 128)
        NEG_SLOPE = 0.2
        LN_EPS = 1e-05
        key = jax.random.key(seed)
        k0, k1, k2, k3, k4 = jax.random.split(key, 5)
        x = jax.random.normal(k0, (B, K, D), dtype=jnp.float32)
        adj = jax.random.randint(k1, (K, K), 0, 2, dtype=jnp.int32)
        adj = jnp.maximum(adj, jnp.eye(K, dtype=jnp.int32))
        W = jax.random.normal(k2, (D, D), dtype=jnp.float32) / np.sqrt(D)
        a_src = jax.random.normal(k3, (D,), dtype=jnp.float32) / np.sqrt(2 * D)
        a_dst = jax.random.normal(k4, (D,), dtype=jnp.float32) / np.sqrt(2 * D)
        ln_gamma = jnp.ones((D,), dtype=jnp.float32)
        ln_beta = jnp.zeros((D,), dtype=jnp.float32)
        return {'x': x, 'adj': adj, 'W': W, 'a_src': a_src, 'a_dst': a_dst, 'ln_gamma': ln_gamma, 'ln_beta': ln_beta}
    _L0_gnn_all = _L0_gnn_setup()
    _L0_gnn_in = {k: v for k, v in _L0_gnn_all.items() if k in ('W', 'a_src', 'a_dst', 'ln_gamma', 'ln_beta', )}
    del _L0_gnn_all

    def _L1_gnn_setup():
        import jax, jax.numpy as jnp
        import numpy as np
        IN_DIM = 128
        OUT_DIM = 128
        NUM_HEADS = 8
        HEAD_DIM = OUT_DIM // NUM_HEADS
        FFN_DIM = OUT_DIM * 2
        LN_EPS = 1e-05

        def _layer_norm(x, g, b):
            mu = jnp.mean(x, axis=-1, keepdims=True)
            var = jnp.var(x, axis=-1, keepdims=True)
            return (x - mu) * jax.lax.rsqrt(var + LN_EPS) * g + b
        key = jax.random.key(seed)
        ks = jax.random.split(key, 12)
        B, N = (4, 2048)
        s_in = 1.0 / np.sqrt(IN_DIM)
        s_out = 1.0 / np.sqrt(OUT_DIM)
        s_ffn = 1.0 / np.sqrt(FFN_DIM)
        return {'adj_matrix': jax.random.randint(ks[0], (N, N), 0, 2, dtype=jnp.int32), 'h': jax.random.normal(ks[1], (B, N, IN_DIM), dtype=jnp.float32), 'Wq': jax.random.uniform(ks[2], (IN_DIM, OUT_DIM), jnp.float32, -s_in, s_in), 'Wk': jax.random.uniform(ks[3], (IN_DIM, OUT_DIM), jnp.float32, -s_in, s_in), 'Wv': jax.random.uniform(ks[4], (IN_DIM, OUT_DIM), jnp.float32, -s_in, s_in), 'Wo': jax.random.uniform(ks[5], (OUT_DIM, OUT_DIM), jnp.float32, -s_out, s_out), 'bo': jnp.zeros((OUT_DIM,), jnp.float32), 'ln1_g': jnp.ones((OUT_DIM,), jnp.float32), 'ln1_b': jnp.zeros((OUT_DIM,), jnp.float32), 'W1': jax.random.uniform(ks[6], (OUT_DIM, FFN_DIM), jnp.float32, -s_out, s_out), 'b1': jnp.zeros((FFN_DIM,), jnp.float32), 'W2': jax.random.uniform(ks[7], (FFN_DIM, OUT_DIM), jnp.float32, -s_ffn, s_ffn), 'b2': jnp.zeros((OUT_DIM,), jnp.float32), 'ln2_g': jnp.ones((OUT_DIM,), jnp.float32), 'ln2_b': jnp.zeros((OUT_DIM,), jnp.float32)}
    _L1_gnn_all = _L1_gnn_setup()
    _L1_gnn_in = {k: v for k, v in _L1_gnn_all.items() if k in ('Wq', 'Wk', 'Wv', 'Wo', 'bo', 'ln1_g', 'ln1_b', 'W1', 'b1', 'W2', 'b2', 'ln2_g', 'ln2_b', )}
    del _L1_gnn_all

    def _L2_gnn_setup():
        import jax, jax.numpy as jnp
        import numpy as np
        IN_DIM = 128
        OUT_DIM = 128
        NUM_HEADS = 8
        HEAD_DIM = OUT_DIM // NUM_HEADS
        FFN_DIM = OUT_DIM * 2
        LN_EPS = 1e-05

        def _layer_norm(x, g, b):
            mu = jnp.mean(x, axis=-1, keepdims=True)
            var = jnp.var(x, axis=-1, keepdims=True)
            return (x - mu) * jax.lax.rsqrt(var + LN_EPS) * g + b
        key = jax.random.key(seed)
        ks = jax.random.split(key, 12)
        B, N = (4, 2048)
        s_in = 1.0 / np.sqrt(IN_DIM)
        s_out = 1.0 / np.sqrt(OUT_DIM)
        s_ffn = 1.0 / np.sqrt(FFN_DIM)
        return {'adj_matrix': jax.random.randint(ks[0], (N, N), 0, 2, dtype=jnp.int32), 'h': jax.random.normal(ks[1], (B, N, IN_DIM), dtype=jnp.float32), 'Wq': jax.random.uniform(ks[2], (IN_DIM, OUT_DIM), jnp.float32, -s_in, s_in), 'Wk': jax.random.uniform(ks[3], (IN_DIM, OUT_DIM), jnp.float32, -s_in, s_in), 'Wv': jax.random.uniform(ks[4], (IN_DIM, OUT_DIM), jnp.float32, -s_in, s_in), 'Wo': jax.random.uniform(ks[5], (OUT_DIM, OUT_DIM), jnp.float32, -s_out, s_out), 'bo': jnp.zeros((OUT_DIM,), jnp.float32), 'ln1_g': jnp.ones((OUT_DIM,), jnp.float32), 'ln1_b': jnp.zeros((OUT_DIM,), jnp.float32), 'W1': jax.random.uniform(ks[6], (OUT_DIM, FFN_DIM), jnp.float32, -s_out, s_out), 'b1': jnp.zeros((FFN_DIM,), jnp.float32), 'W2': jax.random.uniform(ks[7], (FFN_DIM, OUT_DIM), jnp.float32, -s_ffn, s_ffn), 'b2': jnp.zeros((OUT_DIM,), jnp.float32), 'ln2_g': jnp.ones((OUT_DIM,), jnp.float32), 'ln2_b': jnp.zeros((OUT_DIM,), jnp.float32)}
    _L2_gnn_all = _L2_gnn_setup()
    _L2_gnn_in = {k: v for k, v in _L2_gnn_all.items() if k in ('Wq', 'Wk', 'Wv', 'Wo', 'bo', 'ln1_g', 'ln1_b', 'W1', 'b1', 'W2', 'b2', 'ln2_g', 'ln2_b', )}
    del _L2_gnn_all

    def _L3_gnn_setup():
        import jax, jax.numpy as jnp
        import numpy as np
        B, K, D = (16, 2048, 128)
        NEG_SLOPE = 0.2
        LN_EPS = 1e-05
        key = jax.random.key(seed)
        k0, k1, k2, k3, k4 = jax.random.split(key, 5)
        x = jax.random.normal(k0, (B, K, D), dtype=jnp.float32)
        adj = jax.random.randint(k1, (K, K), 0, 2, dtype=jnp.int32)
        adj = jnp.maximum(adj, jnp.eye(K, dtype=jnp.int32))
        W = jax.random.normal(k2, (D, D), dtype=jnp.float32) / np.sqrt(D)
        a_src = jax.random.normal(k3, (D,), dtype=jnp.float32) / np.sqrt(2 * D)
        a_dst = jax.random.normal(k4, (D,), dtype=jnp.float32) / np.sqrt(2 * D)
        ln_gamma = jnp.ones((D,), dtype=jnp.float32)
        ln_beta = jnp.zeros((D,), dtype=jnp.float32)
        return {'x': x, 'adj': adj, 'W': W, 'a_src': a_src, 'a_dst': a_dst, 'ln_gamma': ln_gamma, 'ln_beta': ln_beta}
    _L3_gnn_all = _L3_gnn_setup()
    _L3_gnn_in = {k: v for k, v in _L3_gnn_all.items() if k in ('W', 'a_src', 'a_dst', 'ln_gamma', 'ln_beta', )}
    del _L3_gnn_all

    return {
        "x": x,
        "adj": adj,
        "L0_gnn_W": _L0_gnn_in["W"],
        "L0_gnn_a_src": _L0_gnn_in["a_src"],
        "L0_gnn_a_dst": _L0_gnn_in["a_dst"],
        "L0_gnn_ln_gamma": _L0_gnn_in["ln_gamma"],
        "L0_gnn_ln_beta": _L0_gnn_in["ln_beta"],
        "L1_gnn_Wq": _L1_gnn_in["Wq"],
        "L1_gnn_Wk": _L1_gnn_in["Wk"],
        "L1_gnn_Wv": _L1_gnn_in["Wv"],
        "L1_gnn_Wo": _L1_gnn_in["Wo"],
        "L1_gnn_bo": _L1_gnn_in["bo"],
        "L1_gnn_ln1_g": _L1_gnn_in["ln1_g"],
        "L1_gnn_ln1_b": _L1_gnn_in["ln1_b"],
        "L1_gnn_W1": _L1_gnn_in["W1"],
        "L1_gnn_b1": _L1_gnn_in["b1"],
        "L1_gnn_W2": _L1_gnn_in["W2"],
        "L1_gnn_b2": _L1_gnn_in["b2"],
        "L1_gnn_ln2_g": _L1_gnn_in["ln2_g"],
        "L1_gnn_ln2_b": _L1_gnn_in["ln2_b"],
        "L2_gnn_Wq": _L2_gnn_in["Wq"],
        "L2_gnn_Wk": _L2_gnn_in["Wk"],
        "L2_gnn_Wv": _L2_gnn_in["Wv"],
        "L2_gnn_Wo": _L2_gnn_in["Wo"],
        "L2_gnn_bo": _L2_gnn_in["bo"],
        "L2_gnn_ln1_g": _L2_gnn_in["ln1_g"],
        "L2_gnn_ln1_b": _L2_gnn_in["ln1_b"],
        "L2_gnn_W1": _L2_gnn_in["W1"],
        "L2_gnn_b1": _L2_gnn_in["b1"],
        "L2_gnn_W2": _L2_gnn_in["W2"],
        "L2_gnn_b2": _L2_gnn_in["b2"],
        "L2_gnn_ln2_g": _L2_gnn_in["ln2_g"],
        "L2_gnn_ln2_b": _L2_gnn_in["ln2_b"],
        "L3_gnn_W": _L3_gnn_in["W"],
        "L3_gnn_a_src": _L3_gnn_in["a_src"],
        "L3_gnn_a_dst": _L3_gnn_in["a_dst"],
        "L3_gnn_ln_gamma": _L3_gnn_in["ln_gamma"],
        "L3_gnn_ln_beta": _L3_gnn_in["ln_beta"],
    }

def reference(x, adj, L0_gnn_W, L0_gnn_a_src, L0_gnn_a_dst, L0_gnn_ln_gamma, L0_gnn_ln_beta, L1_gnn_Wq, L1_gnn_Wk, L1_gnn_Wv, L1_gnn_Wo, L1_gnn_bo, L1_gnn_ln1_g, L1_gnn_ln1_b, L1_gnn_W1, L1_gnn_b1, L1_gnn_W2, L1_gnn_b2, L1_gnn_ln2_g, L1_gnn_ln2_b, L2_gnn_Wq, L2_gnn_Wk, L2_gnn_Wv, L2_gnn_Wo, L2_gnn_bo, L2_gnn_ln1_g, L2_gnn_ln1_b, L2_gnn_W1, L2_gnn_b1, L2_gnn_W2, L2_gnn_b2, L2_gnn_ln2_g, L2_gnn_ln2_b, L3_gnn_W, L3_gnn_a_src, L3_gnn_a_dst, L3_gnn_ln_gamma, L3_gnn_ln_beta):
    import jax
    import jax.numpy as jnp
    def _L0_gnn_ref(x, adj, W, a_src, a_dst, ln_gamma, ln_beta):
        import jax, jax.numpy as jnp
        import numpy as np
        B, K, D = (16, 2048, 128)
        NEG_SLOPE = 0.2
        LN_EPS = 1e-05
        h = x @ W
        s_i = h @ a_src
        s_j = h @ a_dst
        e = s_i[:, :, None] + s_j[:, None, :]
        e = jnp.where(e >= 0, e, NEG_SLOPE * e)
        e = jnp.where(adj[None, :, :] == 0, -jnp.inf, e)
        att = jax.nn.softmax(e, axis=-1)
        att = jnp.nan_to_num(att, nan=0.0)
        out = jnp.einsum('bij,bjd->bid', att, h)
        y = out + x
        mu = jnp.mean(y, axis=-1, keepdims=True)
        var = jnp.mean((y - mu) ** 2, axis=-1, keepdims=True)
        return ln_gamma * (y - mu) * jax.lax.rsqrt(var + LN_EPS) + ln_beta

    def _L1_gnn_ref(adj_matrix, h, Wq, Wk, Wv, Wo, bo, ln1_g, ln1_b, W1, b1, W2, b2, ln2_g, ln2_b):
        import jax, jax.numpy as jnp
        import numpy as np
        IN_DIM = 128
        OUT_DIM = 128
        NUM_HEADS = 8
        HEAD_DIM = OUT_DIM // NUM_HEADS
        FFN_DIM = OUT_DIM * 2
        LN_EPS = 1e-05

        def _layer_norm(x, g, b):
            mu = jnp.mean(x, axis=-1, keepdims=True)
            var = jnp.var(x, axis=-1, keepdims=True)
            return (x - mu) * jax.lax.rsqrt(var + LN_EPS) * g + b
        B, N, _ = h.shape
        Q = (h @ Wq).reshape(B, N, NUM_HEADS, HEAD_DIM)
        K = (h @ Wk).reshape(B, N, NUM_HEADS, HEAD_DIM)
        V = (h @ Wv).reshape(B, N, NUM_HEADS, HEAD_DIM)
        scores = jnp.einsum('bnhd,bmhd->bhnm', Q, K) / jnp.sqrt(jnp.asarray(HEAD_DIM, jnp.float32))
        mask = (adj_matrix == 0)[None, None, :, :]
        scores = jnp.where(mask, -jnp.inf, scores)
        attn = jax.nn.softmax(scores, axis=-1)
        attn_out = jnp.einsum('bhnm,bmhd->bnhd', attn, V).reshape(B, N, OUT_DIM)
        x = h + (attn_out @ Wo + bo)
        x = _layer_norm(x, ln1_g, ln1_b)
        y = jax.nn.relu(x @ W1 + b1) @ W2 + b2
        x = _layer_norm(x + y, ln2_g, ln2_b)
        return x

    def _L2_gnn_ref(adj_matrix, h, Wq, Wk, Wv, Wo, bo, ln1_g, ln1_b, W1, b1, W2, b2, ln2_g, ln2_b):
        import jax, jax.numpy as jnp
        import numpy as np
        IN_DIM = 128
        OUT_DIM = 128
        NUM_HEADS = 8
        HEAD_DIM = OUT_DIM // NUM_HEADS
        FFN_DIM = OUT_DIM * 2
        LN_EPS = 1e-05

        def _layer_norm(x, g, b):
            mu = jnp.mean(x, axis=-1, keepdims=True)
            var = jnp.var(x, axis=-1, keepdims=True)
            return (x - mu) * jax.lax.rsqrt(var + LN_EPS) * g + b
        B, N, _ = h.shape
        Q = (h @ Wq).reshape(B, N, NUM_HEADS, HEAD_DIM)
        K = (h @ Wk).reshape(B, N, NUM_HEADS, HEAD_DIM)
        V = (h @ Wv).reshape(B, N, NUM_HEADS, HEAD_DIM)
        scores = jnp.einsum('bnhd,bmhd->bhnm', Q, K) / jnp.sqrt(jnp.asarray(HEAD_DIM, jnp.float32))
        mask = (adj_matrix == 0)[None, None, :, :]
        scores = jnp.where(mask, -jnp.inf, scores)
        attn = jax.nn.softmax(scores, axis=-1)
        attn_out = jnp.einsum('bhnm,bmhd->bnhd', attn, V).reshape(B, N, OUT_DIM)
        x = h + (attn_out @ Wo + bo)
        x = _layer_norm(x, ln1_g, ln1_b)
        y = jax.nn.relu(x @ W1 + b1) @ W2 + b2
        x = _layer_norm(x + y, ln2_g, ln2_b)
        return x

    def _L3_gnn_ref(x, adj, W, a_src, a_dst, ln_gamma, ln_beta):
        import jax, jax.numpy as jnp
        import numpy as np
        B, K, D = (16, 2048, 128)
        NEG_SLOPE = 0.2
        LN_EPS = 1e-05
        h = x @ W
        s_i = h @ a_src
        s_j = h @ a_dst
        e = s_i[:, :, None] + s_j[:, None, :]
        e = jnp.where(e >= 0, e, NEG_SLOPE * e)
        e = jnp.where(adj[None, :, :] == 0, -jnp.inf, e)
        att = jax.nn.softmax(e, axis=-1)
        att = jnp.nan_to_num(att, nan=0.0)
        out = jnp.einsum('bij,bjd->bid', att, h)
        y = out + x
        mu = jnp.mean(y, axis=-1, keepdims=True)
        var = jnp.mean((y - mu) ** 2, axis=-1, keepdims=True)
        return ln_gamma * (y - mu) * jax.lax.rsqrt(var + LN_EPS) + ln_beta

    x = _L0_gnn_ref(x, adj, L0_gnn_W, L0_gnn_a_src, L0_gnn_a_dst, L0_gnn_ln_gamma, L0_gnn_ln_beta)
    x = _L1_gnn_ref(adj, x, L1_gnn_Wq, L1_gnn_Wk, L1_gnn_Wv, L1_gnn_Wo, L1_gnn_bo, L1_gnn_ln1_g, L1_gnn_ln1_b, L1_gnn_W1, L1_gnn_b1, L1_gnn_W2, L1_gnn_b2, L1_gnn_ln2_g, L1_gnn_ln2_b)
    x = _L2_gnn_ref(adj, x, L2_gnn_Wq, L2_gnn_Wk, L2_gnn_Wv, L2_gnn_Wo, L2_gnn_bo, L2_gnn_ln1_g, L2_gnn_ln1_b, L2_gnn_W1, L2_gnn_b1, L2_gnn_W2, L2_gnn_b2, L2_gnn_ln2_g, L2_gnn_ln2_b)
    x = _L3_gnn_ref(x, adj, L3_gnn_W, L3_gnn_a_src, L3_gnn_a_dst, L3_gnn_ln_gamma, L3_gnn_ln_beta)
    return x


_drawn_inputs = setup_inputs


def setup_inputs(seed=0):
    import zlib

    import numpy as np

    out = dict(_drawn_inputs(seed))
    spreads = {'L0_gnn_ln_gamma': (1.0, 0.2),
     'L0_gnn_ln_beta': (0.0, 0.1),
     'L1_gnn_bo': (0.0, 0.1),
     'L1_gnn_ln1_g': (1.0, 0.2),
     'L1_gnn_ln1_b': (0.0, 0.1),
     'L1_gnn_b1': (0.0, 0.1),
     'L1_gnn_b2': (0.0, 0.1),
     'L1_gnn_ln2_g': (1.0, 0.2),
     'L1_gnn_ln2_b': (0.0, 0.1),
     'L2_gnn_bo': (0.0, 0.1),
     'L2_gnn_ln1_g': (1.0, 0.2),
     'L2_gnn_ln1_b': (0.0, 0.1),
     'L2_gnn_b1': (0.0, 0.1),
     'L2_gnn_b2': (0.0, 0.1),
     'L2_gnn_ln2_g': (1.0, 0.2),
     'L2_gnn_ln2_b': (0.0, 0.1),
     'L3_gnn_ln_gamma': (1.0, 0.2),
     'L3_gnn_ln_beta': (0.0, 0.1)}
    factors = {}
    for name, (base, spread) in spreads.items():
        noise = np.random.default_rng([zlib.crc32(name.encode()), seed]).standard_normal(out[name].shape)
        drawn = base * np.exp(spread * noise) if base else spread * noise
        out[name] = jnp.asarray(drawn.astype(out[name].dtype))
    for name, factor in factors.items():
        out[name] = (out[name] * factor).astype(out[name].dtype)
    return out
```

```python
import concourse.bass as bass
from concourse import mybir
from contextlib import ExitStack

F32 = mybir.dt.float32
I32 = mybir.dt.int32
ALU = mybir.AluOpType
ACT = mybir.ActivationFunctionType
AX = mybir.AxisListType

P = 128
B, N, D = 8, 2048, 128
RT = N // P
BD = B * D
HEADS, HD = 8, 16
FFN = 2 * D
FC = FFN // P
CMAX = 11
CREST = 10
EMAX = CMAX * P
BLK = 64
NBLK = N // BLK
COL_OFS, COL_ROW, COL_LOC = NBLK, NBLK + 1, NBLK + 2
TABW = NBLK + 3
RING = 5
BIG = 1.0e30
TINY = 1.0e-30
SLOPE = 0.2
EPS = 1e-5
KINDS = ("gat", "tf", "tf", "gat")


class Chain:

    def __init__(self, eng, sem):
        self.eng, self.sem, self.base, self.n = eng, sem, 0, 0

    def link(self, ins):
        ins.then_inc(self.sem, 1)
        self.n += 1
        self.eng.wait_ge(self.sem, self.base + self.n)

    def loop(self, i, per):
        self.start, self.per = self.base + self.n, per
        self.base, self.n = self.start + i * per, 0

    def end(self, turns):
        assert self.n == self.per, (self.n, self.per)
        self.base, self.n = self.start + turns * self.per, 0


class Semaphores:

    def __init__(self, nc):
        self.nc, self.made = nc, {}

    def get(self, name):
        if name not in self.made:
            self.made[name] = self.nc.alloc_semaphore(name)
        return self.made[name]

    def renew(self):
        if self.made:
            self.nc.clear_and_free_semaphores(list(self.made.values()))
            self.nc.all_engine_barrier()
        self.made = {}


def hold(eng, sem, value):
    eng.wait_ge(sem, value)
    eng.nop(nofuse=True)


def first_edge_tile(t):
    return 0 if isinstance(t, int) and t == 0 else CMAX + CREST * (t - 1)


def edge_tiles(t):
    return CMAX if isinstance(t, int) and t == 0 else CREST


def build(nc, a, out, layers=4):
    ctx = ExitStack()
    with ctx:
        def sb(name, shape, dt=F32):
            return ctx.enter_context(nc.sbuf_tensor(name, shape, dt))

        def ps(name, shape):
            return ctx.enter_context(nc.psum_tensor(name, shape, F32))

        sems = Semaphores(nc)
        sem = sems.get

        xs = nc.dram_tensor("xs", (RT, P, BD), F32).ap()
        ao = nc.dram_tensor("ao", (RT, P, BD), F32).ap()
        qq = nc.dram_tensor("qq", (RT, P, BD), F32).ap()
        si = nc.dram_tensor("si", (RT, P, B), F32).ap()
        kk = nc.dram_tensor("kk", (N, BD), F32).ap()
        vv = nc.dram_tensor("vv", (N, BD), F32).ap()
        sj = nc.dram_tensor("sj", (N, B), F32).ap()
        starts = nc.dram_tensor("starts", (RT, EMAX + P), F32).ap()

        ident = sb("ident", [P, P])
        ones = sb("ones", [P, P])
        below = sb("below", [P, P])
        lane = sb("lane", [P, P])
        edge_id = sb("edge_id", [P, CMAX])
        tile_start = sb("tile_start", [P, CMAX])
        capacity = sb("capacity", [P, RT])
        fits = sb("fits", [P, 1], I32)
        neighbour = sb("neighbour", [P, RT, CMAX], I32)
        local_row = sb("local_row", [P, RT, CMAX])
        row_from = sb("row_from", [P, RT, CMAX])
        row_to = sb("row_to", [P, RT, CMAX])
        w = {}
        for L, kind in enumerate(KINDS):
            if kind == "tf":
                w[L] = dict(qkv=sb(f"wqkv{L}", [P, 3 * D]), wo=sb(f"wo{L}", [P, D]), w1=sb(f"w1{L}", [P, FFN]),
                            w2=sb(f"w2{L}", [P, FC, D]), b1=sb(f"b1{L}", [P, FC]), bias=sb(f"bias{L}", [P, 2, D]),
                            gb=sb(f"gb{L}", [P, 4, D]))
            else:
                w[L] = dict(w=sb(f"w{L}", [P, D + 2]), av=sb(f"av{L}", [P, 2]), gb=sb(f"gb{L}", [P, 2, D]))
        eps_col = sb("eps_col", [P, 1])

        arena = sb("arena", [P, 30208])

        def carve(*shapes):
            at, views = 0, []
            for shape in shapes:
                size = 1
                for s in shape:
                    size *= s
                v = arena[:, at:at + size]
                if len(shape) == 2:
                    v = v.rearrange("p (a b) -> p a b", a=shape[0])
                if len(shape) == 3:
                    v = v.rearrange("p (a b c) -> p a b c", a=shape[0], b=shape[1])
                views.append(v)
                at += size
            assert at <= 30208, at
            return views

        bank = [ps(f"bank{i}", [P, 4 * P]) if i in (6, 7) else None for i in range(8)]
        pair = [ps(f"pair{i}", [P, 8 * P]) for i in range(3)]
        bank[0], bank[1] = pair[0][:, 0:512], pair[0][:, 512:1024]
        bank[2], bank[3] = pair[1][:, 0:512], pair[1][:, 512:1024]
        bank[4], bank[5] = pair[2][:, 0:512], pair[2][:, 512:1024]

        x_by_row = a["x"].rearrange("b (q r) d -> r q b d", r=RT)
        out_by_row = out.rearrange("b (q r) d -> r q b d", r=RT)
        adj_by_row = a["adj"].rearrange("(q r) n -> r q n", r=RT)
        kk_by_row = kk.rearrange("(q r) n -> r q n", r=RT)
        vv_by_row = vv.rearrange("(q r) n -> r q n", r=RT)
        sj_by_row = sj.rearrange("(q r) n -> r q n", r=RT)

        def tile_rows(view, t):
            return (view[bass.ds(t, 1), 0:1], view[bass.ds(RT - 1 - t, 1), 1:P])

        row_count, = carve((1,))
        nz, adj_rows, block_sum, cum, keep32, table, deg, before, total, over = carve(
            (N,), (2, N), (RT, NBLK), (RT * NBLK,), (RT * NBLK,), (RT, TABW), (RT,), (RT,), (RT,), (RT,))
        adj_rows = adj_rows.bitcast(I32)
        with nc.Block() as block:
            w_in, x_in = sem("w_in"), sem("x_in")
            adj_in = [sem("adj_in0"), sem("adj_in1")]
            adj_read, const_made, counts, dv = sem("adj_read"), sem("const_made"), sem("counts"), sem("dv0")
            prefix = sem("prefix")

            @block.sync
            def _(sp):
                def load(t, slot):
                    for src, lo, hi in zip(tile_rows(adj_by_row, t), (0, 1), (1, P)):
                        sp.dma_start(adj_rows[lo:hi, slot:slot + 1, :], src.rearrange("r q n -> q r n")
                                     ).then_inc(adj_in[slot], 16)

                load(0, 0)
                load(1, 1)
                with sp.Fori(1, RT // 2) as i:
                    for slot in range(2):
                        sp.wait_ge(adj_read, 2 * i - 1 + slot)
                        load(2 * i + slot, slot)

            @block.scalar
            def _(act):
                n = 0
                for L, kind in enumerate(KINDS):
                    pre = f"L{L}_gnn_"
                    if kind == "tf":
                        loads = [(w[L]["qkv"][:, k * D:(k + 1) * D], a[pre + m]) for k, m in enumerate(("Wq", "Wk", "Wv"))]
                        loads += [(w[L]["wo"][:], a[pre + "Wo"]), (w[L]["w1"][:], a[pre + "W1"]),
                                  (w[L]["w2"][:], a[pre + "W2"].rearrange("(c p) n -> p c n", p=P)),
                                  (w[L]["bias"][:, 0, :], a[pre + "bo"].rearrange("(a n) -> a n", a=1).broadcast_to([P, D])),
                                  (w[L]["bias"][:, 1, :], a[pre + "b2"].rearrange("(a n) -> a n", a=1).broadcast_to([P, D]))]
                        loads += [(w[L]["b1"][:, c:c + 1], a[pre + "b1"][c * P:(c + 1) * P].rearrange("(p a) -> p a", a=1))
                                  for c in range(FC)]
                        gb = ("ln1_g", "ln1_b", "ln2_g", "ln2_b")
                    else:
                        loads = [(w[L]["w"][:, 0:D], a[pre + "W"])]
                        loads += [(w[L]["av"][:, k:k + 1], a[pre + m].rearrange("(p a) -> p a", a=1))
                                  for k, m in enumerate(("a_src", "a_dst"))]
                        gb = ("ln_gamma", "ln_beta")
                    loads += [(w[L]["gb"][:, k, :], a[pre + m].rearrange("(a n) -> a n", a=1).broadcast_to([P, D]))
                              for k, m in enumerate(gb)]
                    for dst, src in loads:
                        act.dma_start(dst, src).then_inc(w_in, 16)
                        n += 16
                act.wait_ge(w_in, n)
                with act.Fori(0, RT) as t:
                    for src, lo, hi in zip(tile_rows(x_by_row, t), (0, 1), (1, P)):
                        act.dma_start(xs[bass.ds(t, 1), lo:hi, :].rearrange("r q (b d) -> (r q) b d", b=B),
                                      src.rearrange("r q b d -> (r q) b d")).then_inc(x_in, 16)
                act.wait_ge(x_in, 32 * RT)

            @block.gpsimd
            def _(g):
                g.memset(ones[:], 1.0)
                g.memset(eps_col[:], EPS)
                g.memset(capacity[:], float(CREST * P)).then_inc(const_made, 1)
                g.wait_ge(const_made, 1)
                g.memset(capacity[:, 0:1], float(CMAX * P))
                g.affine_select(out=ident[:], in_=ones[:], compare_op=ALU.is_equal, fill=0.0, base=0,
                                pattern=[[-1, P]], channel_multiplier=1)
                g.affine_select(out=below[:], in_=ones[:], compare_op=ALU.is_gt, fill=0.0, base=0,
                                pattern=[[1, P]], channel_multiplier=-1)
                g.affine_select(out=keep32.rearrange("p (t b) -> p t b", b=NBLK), in_=ones[:, 0:1].broadcast_to([P, RT * NBLK]).rearrange("p (t b) -> p t b", b=NBLK),
                                compare_op=ALU.is_gt, fill=0.0, base=0, pattern=[[0, RT], [1, NBLK]],
                                channel_multiplier=0)
                any_dt = dict(allow_small_or_imprecise_dtypes=True)
                g.iota(lane[:], pattern=[[1, P]], base=0, channel_multiplier=0, **any_dt)
                g.iota(edge_id[:], pattern=[[P, CMAX]], base=0, channel_multiplier=1, **any_dt)
                g.iota(tile_start[:], pattern=[[P, CMAX]], base=0, channel_multiplier=0, **any_dt)
                g.iota(table[:, :, COL_LOC:COL_LOC + 1], pattern=[[0, RT], [0, 1]], base=1, channel_multiplier=1, **any_dt)
                g.iota(table[:, :, COL_ROW:COL_ROW + 1], pattern=[[-1, RT], [0, 1]], base=RT - 1,
                       channel_multiplier=RT, **any_dt).then_inc(const_made, 1)
                g.wait_ge(const_made, 2)
                g.iota(table[0:1, :, COL_ROW:COL_ROW + 1], pattern=[[1, RT], [0, 1]], base=0,
                       channel_multiplier=0, **any_dt).then_inc(const_made, 1)

            @block.vector
            def _(v):
                ch = Chain(v, dv)
                def count(t, slot, times):
                    v.wait_ge(adj_in[slot], 32 * times + 32)
                    if not (isinstance(t, int) and t == 0):
                        v.wait_ge(adj_read, t)
                    ch.link(v.tensor_scalar(nz, adj_rows[:, slot, :], 0, None, ALU.not_equal))
                    v.tensor_reduce(block_sum[:, bass.ds(t, 1), :],
                                    nz.rearrange("p (a k j) -> p a k j", a=1, j=BLK), AX.X, ALU.add).then_inc(adj_read, 1)

                count(0, 0, 0)
                count(1, 1, 0)
                with v.Fori(1, RT // 2) as i:
                    ch.loop(i - 1, 2)
                    count(2 * i, 0, i)
                    count(2 * i + 1, 1, i)
                ch.end(RT // 2 - 1)
                v.wait_ge(adj_read, RT)
                v.wait_ge(const_made, 3)
                ch.link(v.tensor_tensor_scan(cum, keep32, block_sum.rearrange("p t k -> p (t k)"), 0.0, ALU.mult, ALU.add))
                cum3 = cum.rearrange("p (t k) -> p t k", t=RT)
                ch.link(v.tensor_copy(table[:, :, 0:NBLK], cum3))
                v.tensor_copy(deg, cum3[:, :, NBLK - 1]).then_inc(counts, 1)
                v.wait_ge(prefix, 1)
                v.tensor_copy(before, bank[0][:, 0:RT]).then_inc(dv, 1)
                ch.link(v.tensor_copy(total, bank[1][:, 0:RT]))
                ch.n += 1
                v.wait_ge(dv, ch.base + ch.n)
                v.tensor_copy(table[:, :, COL_OFS], before)
                bc = lambda x: x.rearrange("p (t a) -> p t a", a=1).broadcast_to([P, RT, CMAX])
                cc = tile_start[:].rearrange("p (a c) -> p a c", a=1).broadcast_to([P, RT, CMAX])
                ch.link(v.tensor_tensor(row_from[:], bc(before), cc, ALU.subtract))
                v.tensor_tensor(row_to[:], row_from[:], bc(deg), ALU.add)
                ch.link(v.tensor_tensor(over, total, capacity[:], ALU.subtract))
                ch.link(v.tensor_reduce(row_count, over, AX.X, ALU.max))
                ch.link(v.tensor_scalar(fits[:], row_count, 0.0, None, ALU.is_le))

            @block.tensor
            def _(pe):
                pe.wait_ge(counts, 1)
                pe.matmul(bank[0][:, 0:RT], below[:], deg, start=True, stop=True)
                pe.matmul(bank[1][:, 0:RT], ones[:], deg, start=True, stop=True).then_inc(prefix, 1)

        _, _, _, _, _, table, deg = carve((N,), (2, N), (RT, NBLK), (RT * NBLK,), (RT * NBLK,), (RT, TABW), (RT,))
        deg_end = (N + 2 * N + 3 * RT * NBLK + RT * TABW + RT)
        skip = arena[:, 0:1]
        views = carve((deg_end,), (4, P), (2, P), (CMAX, TABW), (CMAX,), (CMAX, NBLK), (CMAX, NBLK), (CMAX,),
                      (CMAX,), (2, CMAX), (2, CMAX), (2, CMAX), (2, CMAX, BLK), (CMAX, BLK), (CMAX, BLK), (CMAX, BLK),
                      (CMAX,), (CMAX,), (CMAX * BLK,), (EMAX,), (2, EMAX + P))
        (_, onehot, ge, tab, rank, le, part, blk, base, gidx, rank2, blk_base, ablk, nzb, cumb, leb, inner, col,
         keep64, iota_e, start_row) = views
        gidx, ablk = gidx.bitcast(I32), ablk.bitcast(I32)
        adj_blocks = a["adj"].rearrange("n (k j) -> (n k) j", j=BLK)
        with nc.Block() as block:
            oh_made, tab_ready, tab_read, gidx_ready = sem("oh_made"), sem("tab_ready"), sem("tab_read"), sem("gidx_ready")
            blk_in = [sem("blk_in0"), sem("blk_in1")]
            blk_read, dv, k64_made = sem("blk_read"), sem("dv1"), sem("k64_made")
            end_made, start_ready, start_out = sem("end_made"), sem("start_ready"), [sem("start_out0"), sem("start_out1")]

            @block.gpsimd
            def _(g):
                g.affine_select(out=keep64.rearrange("p (t b) -> p t b", b=BLK), in_=ones[:, 0:1].broadcast_to([P, CMAX * BLK]).rearrange("p (t b) -> p t b", b=BLK),
                                compare_op=ALU.is_gt, fill=0.0, base=0, pattern=[[0, CMAX], [1, BLK]],
                                channel_multiplier=0)
                g.iota(iota_e, pattern=[[1, EMAX]], base=0, channel_multiplier=0,
                       allow_small_or_imprecise_dtypes=True).then_inc(k64_made, 1)
                with g.Fori(0, RT // 2) as i:
                    for slot in range(2):
                        hold(g, gidx_ready, 2 * i + slot + 1)
                        for c in range(CMAX):
                            g.indirect_dma_start(out=ablk[:, slot, c, :], out_offset=None, in_=adj_blocks,
                                                 in_offset=bass.IndirectOffsetOnAxis(ap=gidx[:, slot, c:c + 1], axis=0)
                                                 ).then_inc(blk_in[slot], 16)

            @block.tensor
            def _(pe):
                def step(t):
                    for c in range(CMAX):
                        pe.wait_ge(oh_made, CMAX * t + c + 1)
                        if c == 0 and not isinstance(t, int):
                            pe.wait_ge(tab_read, t)
                        pe.matmul(bank[0][:, c * TABW:(c + 1) * TABW], onehot[:, c % 4, :],
                                  table[:, bass.ds(t, 1), :].rearrange("p a n -> p (a n)"),
                                  start=True, stop=True).then_inc(tab_ready, 1)
                    pe.wait_ge(end_made, t + 1)
                    for k in range(3):
                        lo, hi = k * 512, min((k + 1) * 512, EMAX)
                        mm = pe.matmul(bank[1 + k][0:1, 0:hi - lo], ones[:, 0:1], nz[:, lo:hi], start=True, stop=True)
                    mm.then_inc(start_ready, 1)

                step(0)
                with pe.Fori(1, RT) as t:
                    step(t)

            @block.sync
            def _(sp):
                for slot in range(2):
                    sp.sem_inc(start_out[slot], 16)
                with sp.Fori(0, RT // 2) as i:
                    for slot in range(2):
                        sp.wait_ge(sem("start_made"), 2 * i + slot + 1)
                        sp.dma_start(starts[bass.ds(2 * i + slot, 1), :], start_row[0:1, slot, :]).then_inc(start_out[slot], 16)
                for slot in range(2):
                    sp.wait_ge(start_out[slot], 16 * (RT // 2) + 16)

            @block.vector
            def _(v):
                ch = Chain(v, dv)
                v.wait_ge(k64_made, 1)
                ch.link(v.memset(start_row[0:1, :, :], -BIG))

                def find_block(t, slot, half):
                    for c in range(CMAX):
                        if c >= 2:
                            v.wait_ge(tab_ready, CMAX * t + c - 1)
                        ch.link(v.tensor_scalar(ge[:, c % 2, :], lane[:], row_from[:, bass.ds(t, 1), c], None, ALU.is_ge))
                        v.scalar_tensor_tensor(onehot[:, c % 4, :], lane[:], row_to[:, bass.ds(t, 1), c], ge[:, c % 2, :],
                                               ALU.is_lt, ALU.mult).then_inc(oh_made, 1)
                    v.tensor_scalar(nz[:, 0:EMAX], iota_e, row_to[:, bass.ds(t, 1), 0], None, ALU.is_equal).then_inc(end_made, 1)
                    v.wait_ge(tab_ready, CMAX * t + CMAX)
                    v.tensor_copy(tab, bank[0][:, 0:CMAX * TABW].rearrange("p (c n) -> p c n", c=CMAX)).then_inc(tab_read, 1)
                    v.wait_ge(tab_read, t + 1)
                    ch.link(v.tensor_tensor(rank, edge_id[:], tab[:, :, COL_OFS], ALU.subtract))
                    over32 = lambda x: x.rearrange("p (c a) -> p c a", a=1).broadcast_to([P, CMAX, NBLK])
                    ch.link(v.tensor_tensor(le, tab[:, :, 0:NBLK], over32(rank), ALU.is_le))
                    ch.link(v.tensor_tensor(part, tab[:, :, 0:NBLK], le, ALU.mult))
                    ch.link(v.tensor_reduce(base, part, AX.X, ALU.max))
                    ch.link(v.tensor_reduce(blk, le, AX.X, ALU.add))
                    v.tensor_tensor(rank2[:, slot, :], rank, base, ALU.subtract)
                    v.tensor_scalar(local_row[:, bass.ds(t, 1), :], tab[:, :, COL_LOC].rearrange("p (a c) -> p a c", a=1), -1.0, None, ALU.add)
                    ch.link(v.tensor_scalar(blk, blk, float(NBLK - 1), None, ALU.min))
                    v.tensor_scalar(blk_base[:, slot, :], blk, float(BLK), None, ALU.mult)
                    v.scalar_tensor_tensor(gidx[:, slot, :], tab[:, :, COL_ROW], float(NBLK), blk, ALU.mult, ALU.add
                                           ).then_inc(gidx_ready, 1)
                    v.wait_ge(start_ready, t + 1)
                    v.wait_ge(start_out[slot], 16 * half + 16)
                    for k in range(3):
                        lo, hi = k * 512, min((k + 1) * 512, EMAX)
                        ins = v.tensor_scalar(start_row[0:1, slot, lo:hi], bank[1 + k][0:1, 0:hi - lo], 1.0, -BIG,
                                              ALU.min, ALU.mult)
                    ins.then_inc(sem("start_made"), 1)

                def find_column(t, slot, half):
                    v.wait_ge(blk_in[slot], 16 * CMAX * (half + 1))
                    ch.link(v.tensor_scalar(nzb, ablk[:, slot], 0, None, ALU.not_equal))
                    flat = lambda x: x.rearrange("p c j -> p (c j)")
                    ch.link(v.tensor_tensor_scan(flat(cumb), keep64, flat(nzb), 0.0, ALU.mult, ALU.add))
                    over64 = lambda x: x.rearrange("p (c a) -> p c a", a=1).broadcast_to([P, CMAX, BLK])
                    ch.link(v.tensor_tensor(leb, cumb, over64(rank2[:, slot, :]), ALU.is_le))
                    ch.link(v.tensor_reduce(inner, leb, AX.X, ALU.add))
                    ch.link(v.tensor_tensor(col, inner, blk_base[:, slot, :], ALU.add))
                    v.tensor_scalar(neighbour[:, bass.ds(t, 1), :], col.rearrange("p (a c) -> p a c", a=1), float(N - 1), None, ALU.min)

                find_block(0, 0, 0)
                with v.Fori(0, RT // 2 - 1) as i:
                    ch.loop(i, 2 * (CMAX + 6 + 5))
                    find_block(2 * i + 1, 1, i)
                    find_column(2 * i, 0, i)
                    find_block(2 * i + 2, 0, i + 1)
                    find_column(2 * i + 1, 1, i)
                ch.end(RT // 2 - 1)
                find_block(RT - 1, 1, RT // 2 - 1)
                find_column(RT - 2, 0, RT // 2 - 1)
                find_column(RT - 1, 1, RT // 2 - 1)

        for L in range(layers):
            sems.renew()
            project(nc, sem, carve, bank, pair, w[L], KINDS[L], L, ident, tile_rows, xs, qq, kk_by_row, vv_by_row, si, sj_by_row)
            sems.renew()
            attend(nc, sem, carve, bank, pair, KINDS[L], L, lane, neighbour, local_row, row_from, row_to, ident,
                   starts, qq, kk, vv, si, sj, ao, fits, ones, adj_by_row, tile_rows)
            sems.renew()
            (post_gat if KINDS[L] == "gat" else post_tf)(nc, sem, carve, bank, w[L], L, ident, eps_col, xs, ao)
        sems.renew()
        with nc.Block() as block:
            stored = sem("stored")

            @block.sync
            def _(sp):
                with sp.Fori(0, RT) as t:
                    for dst, lo, hi in zip(tile_rows(out_by_row, t), (0, 1), (1, P)):
                        sp.dma_start(dst.rearrange("r q b d -> (r q) b d"),
                                     xs[bass.ds(t, 1), lo:hi, :].rearrange("r q (b d) -> (r q) b d", b=B)).then_inc(stored, 16)
                sp.wait_ge(stored, 32 * RT)
        sems.renew()
        return nc


def project(nc, sem, carve, bank, pair, w, kind, L, ident, tile_rows, xs, qq, kk_by_row, vv_by_row, si, sj_by_row):
    tf = kind == "tf"
    x_tile, x_turned, stage, small, w_turned = carve((2, BD), (2, 4 * D), (2, 3, BD), (2, 2 * B), (D,))
    x_in = [sem(f"x_in{L}{s}") for s in range(2)]
    turned, x_copied, product = sem(f"turned{L}"), sem(f"x_copied{L}"), sem(f"product{L}")
    evac_v, evac_a, small_v = sem(f"evac_v{L}"), sem(f"evac_a{L}"), sem(f"small_v{L}")
    out_sem = [sem(f"staged_out{L}{s}") for s in range(2)]
    wt, wt_copied, wa = sem(f"wt{L}"), sem(f"wt_copied{L}"), sem(f"wa{L}")
    stores = 5 if tf else 5
    GROUPS = 2 * RT

    with nc.Block() as block:
        @block.sync
        def _(sp):
            def load(t, slot):
                sp.dma_start(x_tile[:, slot:slot + 1, :], xs[bass.ds(t, 1)].rearrange("r q n -> q r n")).then_inc(x_in[slot], 16)

            def store(t, slot):
                sp.wait_ge(evac_v, (4 if tf else 1) * (t + 1))
                sp.wait_ge(evac_a, (4 if tf else 1) * (t + 1))
                if tf:
                    sp.dma_start(qq[bass.ds(t, 1)].rearrange("r q n -> q r n"), stage[:, slot, 0:1, :]).then_inc(out_sem[slot], 16)
                    pieces = [(kk_by_row, stage[:, slot, 1, :]), (vv_by_row, stage[:, slot, 2, :])]
                else:
                    sp.wait_ge(small_v, t + 1)
                    sp.dma_start(si[bass.ds(t, 1)].rearrange("r q n -> q r n"), small[:, slot:slot + 1, 0:B]).then_inc(out_sem[slot], 16)
                    pieces = [(vv_by_row, stage[:, slot, 2, :]), (sj_by_row, small[:, slot, B:2 * B])]
                for view, src in pieces:
                    for dst, lo, hi in zip(tile_rows(view, t), (0, 1), (1, P)):
                        sp.dma_start(dst.rearrange("r q n -> (r q) n"), src[lo:hi]).then_inc(out_sem[slot], 16)

            load(0, 0)
            load(1, 1)
            with sp.Fori(0, RT // 2 - 1) as i:
                for slot in range(2):
                    sp.wait_ge(turned, 2 * (2 * i + slot) + 2)
                    load(2 * i + slot + 2, slot)
                    store(2 * i + slot, slot)
            store(RT - 2, 0)
            store(RT - 1, 1)
            for slot in range(2):
                sp.wait_ge(out_sem[slot], 16 * stores * (RT // 2))

        @block.tensor
        def _(pe):
            if not tf:
                pe.transpose(bank[6][:, 0:D], w["w"][:, 0:D], ident[:]).then_inc(wt, 1)
                pe.wait_ge(wt_copied, 1)
                pe.matmul(bank[7][:, 0:2], w_turned, w["av"][:], start=True, stop=True).then_inc(wt, 1)
                pe.wait_ge(wa, 1)

            def turn(n, k, turn_no):
                slot, half = (k // 2) % 2, k % 2
                if k % 2 == 0:
                    pe.wait_ge(x_in[slot], 16 * turn_no + 16)
                if not (isinstance(n, int) and n < 2):
                    pe.wait_ge(x_copied, n - 1)
                for b in range(4):
                    at = (4 * half + b) * D
                    tr = pe.transpose(bank[half][:, b * P:(b + 1) * P], x_tile[:, slot, at:at + D], ident[:])
                tr.then_inc(turned, 1)

            def multiply(n, k):
                half = k % 2
                pe.wait_ge(x_copied, n + 1)
                for b in range(4):
                    lhs = x_turned[:, half, b * P:(b + 1) * P]
                    if tf:
                        if not (isinstance(n, int) and n == 0):
                            pe.wait_ge(evac_a if b % 2 else evac_v, 2 * n - 1 + b // 2)
                        pe.matmul(bank[2 + b][:, 0:3 * D], lhs, w["qkv"][:], start=True, stop=True).then_inc(product, 1)
                    else:
                        if b == 0 and not (isinstance(n, int) and n < 2):
                            pe.wait_ge(evac_a if half else evac_v, n // 2 if isinstance(n, int) else n_half[0])
                        pe.matmul(bank[2 + half][:, b * D:(b + 1) * D], lhs, w["w"][:, 0:D], start=True, stop=True)
                        if b == 0 and half == 0 and not (isinstance(n, int) and n < 4):
                            pe.wait_ge(small_v, (n // 2 if isinstance(n, int) else n_half[0]) - 1)
                        col = 2 * (4 * half + b)
                        mm = pe.matmul(bank[4 + (k // 2) % 2][:, col:col + 2], lhs, w["w"][:, D:D + 2], start=True, stop=True)
                if not tf:
                    mm.then_inc(product, 1)

            n_half = [0]
            turn(0, 0, 0)
            multiply_now = []
            for k in range(4):
                turn(k + 1, k + 1 if k < 3 else 0, 0 if k < 3 else 1)
                multiply(k, k)
            with pe.Fori(1, RT // 2 - 1) as i:
                for k in range(4):
                    n_half[0] = 2 * i + k // 2
                    turn(4 * i + k + 1, (k + 1) % 4, i if k < 3 else i + 1)
                    multiply(4 * i + k, k)
            for k in range(4):
                n = GROUPS - 4 + k
                if k < 3:
                    turn(n + 1, k + 1, RT // 2 - 1)
                multiply(n, k)

        def evacuate(eng, copy, n, k, done, uses, first):
            slot, half = (k // 2) % 2, k % 2
            mine = 1 if eng is nc.scalar else 0
            if tf:
                for b in (mine, mine + 2):
                    eng.wait_ge(product, 4 * n + b + 1)
                    if not first and half == 0 and b < 2:
                        eng.wait_ge(out_sem[slot], 16 * stores * uses)
                    at = (4 * half + b) * D
                    copy(stage[:, slot, :, at:at + D], bank[2 + b][:, 0:3 * D].rearrange("p (m d) -> p m d", m=3)).then_inc(done, 1)
            elif half == mine:
                eng.wait_ge(product, n + 1)
                if not first:
                    eng.wait_ge(out_sem[slot], 16 * stores * uses)
                copy(stage[:, slot, 2, half * 4 * D:(half + 1) * 4 * D], bank[2 + half]).then_inc(done, 1)

        @block.scalar
        def _(act):
            if not tf:
                act.wait_ge(wt, 1)
                act.copy(w_turned, bank[6][:, 0:D]).then_inc(wt_copied, 1)
                act.wait_ge(wt, 2)
                act.copy(w["w"][:, D:D + 2], bank[7][:, 0:2]).then_inc(wa, 1)

            def copy_turned(n, k):
                act.wait_ge(turned, n + 1)
                if not (isinstance(n, int) and n < 2):
                    act.wait_ge(product, (4 if tf else 1) * (n - 1))
                act.copy(x_turned[:, k % 2, :], bank[k % 2]).then_inc(x_copied, 1)

            copy_turned(0, 0)
            for k in range(4):
                copy_turned(k + 1, k + 1)
                evacuate(act, act.copy, k, k, evac_a, 0, True)
            with act.Fori(1, RT // 2 - 1) as i:
                for k in range(4):
                    copy_turned(4 * i + k + 1, k + 1)
                    evacuate(act, act.copy, 4 * i + k, k, evac_a, i, False)
            for k in range(4):
                n = GROUPS - 4 + k
                if k < 3:
                    copy_turned(n + 1, k + 1)
                evacuate(act, act.copy, n, k, evac_a, RT // 2 - 1, False)

        @block.vector
        def _(v):
            def turn(n, k, t, uses, first):
                evacuate(v, v.tensor_copy, n, k, evac_v, uses, first)
                if not tf and k % 2 == 1:
                    slot = (k // 2) % 2
                    v.wait_ge(product, n + 1)
                    v.tensor_copy(small[:, slot, :].rearrange("p (m b) -> p b m", m=2),
                                  bank[4 + slot][:, 0:2 * B].rearrange("p (b m) -> p b m", m=2)).then_inc(small_v, 1)

            for k in range(4):
                turn(k, k, k // 2, 0, True)
            with v.Fori(1, RT // 2) as i:
                for k in range(4):
                    turn(4 * i + k, k, 2 * i + k // 2, i, False)


def attend(nc, sem, carve, bank, pair, kind, L, lane, neighbour, local_row, row_from, row_to, ident,
           starts, qq, kk, vv, si, sj, ao, fits, ones, adj_by_row, tile_rows):
    by_edge = attend_by_edge(nc, sem, carve, bank, pair, kind, L, lane, neighbour, local_row, row_from, row_to, ident,
                             starts, qq, kk, vv, si, sj, ao)
    dense = attend_dense(nc, sem, carve, bank, pair, kind, L, ident, qq, kk, vv, si, sj, ao, ones, adj_by_row, tile_rows)

    def either(eng, edge_program, dense_program):
        fit = eng.value_load(fits[0:1, 0:1], min_val=0, max_val=1)
        with eng.If(fit == 1):
            edge_program(eng)
        with eng.Else():
            dense_program(eng)

    with nc.Block() as block:
        @block.gpsimd
        def _(g):
            either(g, by_edge[0], dense[0])

        @block.sync
        def _(sp):
            either(sp, by_edge[1], dense[1])

        @block.tensor
        def _(pe):
            either(pe, by_edge[2], dense[2])

        @block.scalar
        def _(act):
            either(act, by_edge[3], dense[3])

        @block.vector
        def _(v):
            either(v, by_edge[4], dense[4])


def attend_dense(nc, sem, carve, bank, pair, kind, L, ident, qq, kk, vv, si, sj, ao, ones, adj_by_row, tile_rows):
    tf = kind == "tf"
    H = HEADS if tf else 1
    W = D // H
    SCALE = float(HD) ** -0.5 if tf else 1.0
    KT = N // P
    (keys, values, keys_turned, masked, probs, probs_turned, bias, adj_rows, q_tile, q_heads, o_stage, head_mask, top,
     shift, den, q_pair, k_pair) = carve((KT, D), (KT, D), (N,), (N,), (N,), (N,), (N,), (N,), (D,), (HEADS, P), (D,),
                                         (HEADS,), (1,), (1,), (1,), (P,), (N,))
    adj_rows = adj_rows.bitcast(I32)
    new = lambda name: sem(f"{name}{L}")
    made, adj_in, kv_in, bias_made = new("d_made"), new("d_adj_in"), new("d_kv_in"), new("d_bias")
    k_tr, k_copied, q_tr, q_masked = new("d_k_tr"), new("d_k_copied"), new("d_q_tr"), new("d_q_masked")
    scored, read, biased, topped, shifted = new("d_scored"), new("d_read"), new("d_biased"), new("d_topped"), new("d_shifted")
    raised, p_tr, p_copied, summed = new("d_exp"), new("d_p_tr"), new("d_p_copied"), new("d_summed")
    den_step, o_made, o_out = new("d_den"), new("d_o"), new("d_o_out")
    loads = 3 if tf else 3

    def tiles(eng, per_tile, per_batch):
        with eng.Fori(0, RT) as t:
            per_tile(t)
            with eng.Fori(0, B) as b:
                per_batch(t, b, B * t + b)

    nothing = lambda t: None

    def gpsimd(g):
        g.affine_select(out=head_mask, in_=ones[:, 0:HEADS], compare_op=ALU.is_ge, fill=0.0, base=0,
                        pattern=[[-HD, HEADS]], channel_multiplier=1).then_inc(made, 1)
        g.wait_ge(made, 1)
        g.affine_select(out=head_mask, in_=head_mask, compare_op=ALU.is_ge, fill=0.0, base=HD - 1,
                        pattern=[[HD, HEADS]], channel_multiplier=-1)
        g.memset(q_pair[0:2, :], 1.0)
        g.memset(k_pair[0:2, :], 1.0).then_inc(made, 1)
        g.sem_inc(o_made, 1)
        g.sem_inc(p_copied, 1)
        g.sem_inc(raised, 1)
        g.sem_inc(o_out, 16)

    def sync(sp):
        sp.wait_ge(made, 2)

        def per_tile(t):
            sp.wait_ge(o_made, H * B * t + 1)
            for src, lo, hi in zip(tile_rows(adj_by_row, t), (0, 1), (1, P)):
                sp.dma_start(adj_rows[lo:hi, :], src.rearrange("r q n -> (r q) n")).then_inc(adj_in, 16)

        def per_batch(t, b, m):
            sp.wait_ge(o_made, H * m + 1)
            cols = bass.ds(b * D, D)
            by_tile = lambda x: x.rearrange("(k p) n -> p k n", p=P)
            sp.dma_start(values, by_tile(vv)[:, :, cols]).then_inc(kv_in, 16)
            if tf:
                sp.dma_start(keys, by_tile(kk)[:, :, cols]).then_inc(kv_in, 16)
                sp.dma_start(q_tile, qq[bass.ds(t, 1), :, cols].rearrange("r q n -> (r q) n")).then_inc(kv_in, 16)
            else:
                sp.dma_start(k_pair[1:2, :], sj.rearrange("n b -> b n")[bass.ds(b, 1), :], allow_slow_non_contiguous=True
                             ).then_inc(kv_in, 16)
                sp.dma_start(q_pair[0:1, :], si.rearrange("r q b -> r b q")[bass.ds(t, 1), bass.ds(b, 1), :].rearrange("r b q -> (r b) q"),
                             allow_slow_non_contiguous=True).then_inc(kv_in, 16)
            sp.wait_ge(o_made, H * (m + 1) + 1)
            sp.dma_start(ao[bass.ds(t, 1), :, cols].rearrange("r q n -> (r q) n"), o_stage).then_inc(o_out, 16)
        tiles(sp, per_tile, per_batch)
        sp.wait_ge(o_out, 16 * RT * B + 16)

    def tensor(pe):
        def per_batch(t, b, m):
            hold(pe, kv_in, 16 * loads * (m + 1))
            if tf:
                hold(pe, p_copied, 2 * H * m + 1)
                for k in range(KT):
                    tr = pe.transpose(bank[k // 4][:, (k % 4) * P:(k % 4 + 1) * P], keys[:, k, :], ident[:])
                tr.then_inc(k_tr, 1)
                pe.transpose(bank[5][:, 0:P], q_tile, ident[:]).then_inc(q_tr, 1)
            for h in range(H):
                n = H * m + h
                if tf:
                    pe.wait_ge(k_copied, 2 * m + 2)
                    pe.wait_ge(q_masked, m + 1)
                hold(pe, p_copied, 2 * n + 1)
                for k in range(4):
                    if tf:
                        mm = pe.matmul(bank[k], q_heads[:, h, :], keys_turned[:, k * 512:(k + 1) * 512], start=True, stop=True)
                    else:
                        mm = pe.matmul(bank[k], q_pair[0:2, :], k_pair[0:2, k * 512:(k + 1) * 512], start=True, stop=True)
                mm.then_inc(scored, 1)
                hold(pe, raised, n + 2)
                for k in range(KT):
                    tr = pe.transpose(bank[k // 4][:, (k % 4) * P:(k % 4 + 1) * P], probs[:, k * P:(k + 1) * P], ident[:])
                tr.then_inc(p_tr, 1)
                pe.wait_ge(o_made, n + 1)
                hold(pe, p_copied, 2 * n + 3)
                for k in range(KT):
                    mm = pe.matmul(bank[4][:, 0:W], probs_turned[:, k * P:(k + 1) * P], values[:, k, h * W:(h + 1) * W],
                                   start=(k == 0), stop=(k == KT - 1))
                mm.then_inc(summed, 1)
        tiles(pe, nothing, per_batch)

    def scalar(act):
        def per_batch(t, b, m):
            if tf:
                act.wait_ge(k_tr, m + 1)
                for k in range(2):
                    act.copy(keys_turned[:, k * 1024:(k + 1) * 1024], pair[k][:]).then_inc(k_copied, 1)
            for h in range(H):
                n = H * m + h
                if not tf:
                    act.wait_ge(scored, n + 1)
                    for k in range(2):
                        act.copy(masked[:, k * 1024:(k + 1) * 1024], pair[k][:]).then_inc(read, 1)
                act.wait_ge(shifted, n + 1)
                act.wait_ge(o_made, n + 1)
                act.activation(probs, masked, ACT.Exp, bias=shift, scale=SCALE, accum_out=den).then_inc(raised, 1)
                act.wait_ge(p_tr, n + 1)
                for k in range(2):
                    act.copy(probs_turned[:, k * 1024:(k + 1) * 1024], pair[k][:]).then_inc(p_copied, 1)
        tiles(act, nothing, per_batch)

    def vector(v):
        v.wait_ge(made, 2)

        def per_tile(t):
            v.wait_ge(adj_in, 32 * t + 32)
            v.wait_ge(o_made, H * B * t + 1)
            v.tensor_scalar(bias, adj_rows, 0, -BIG, ALU.is_equal, ALU.mult).then_inc(bias_made, 1)
            hold(v, bias_made, t + 1)

        def per_batch(t, b, m):
            if tf:
                v.wait_ge(q_tr, m + 1)
                v.tensor_tensor(q_heads, bank[5][:, 0:P].rearrange("p (a q) -> p a q", a=1).broadcast_to([P, HEADS, P]),
                                head_mask.rearrange("p (h a) -> p h a", a=1).broadcast_to([P, HEADS, P]), ALU.mult
                                ).then_inc(q_masked, 1)
            for h in range(H):
                n = H * m + h
                if tf:
                    v.wait_ge(scored, n + 1)
                    v.wait_ge(raised, n + 1)
                    for k in range(2):
                        cols = slice(k * 1024, (k + 1) * 1024)
                        v.tensor_tensor(masked[:, cols], pair[k][:], bias[:, cols], ALU.add).then_inc(biased, 1)
                    v.wait_ge(biased, 2 * n + 2)
                else:
                    v.wait_ge(read, 2 * n + 2)
                    v.scalar_tensor_tensor(masked, masked, SLOPE, masked, ALU.mult, ALU.max).then_inc(biased, 1)
                    v.wait_ge(biased, 2 * n + 1)
                    v.tensor_tensor(masked, masked, bias, ALU.add).then_inc(biased, 1)
                    v.wait_ge(biased, 2 * n + 2)
                v.tensor_reduce(top, masked, AX.X, ALU.max).then_inc(topped, 1)
                v.wait_ge(topped, n + 1)
                v.tensor_scalar(shift, top, -BIG / 2, -SCALE, ALU.max, ALU.mult).then_inc(shifted, 1)
                v.wait_ge(raised, n + 2)
                v.tensor_scalar(den, den, TINY, None, ALU.max).then_inc(den_step, 1)
                v.wait_ge(den_step, 2 * n + 1)
                v.reciprocal(den, den).then_inc(den_step, 1)
                v.wait_ge(den_step, 2 * n + 2)
                v.wait_ge(summed, n + 1)
                if h == 0:
                    v.wait_ge(o_out, 16 * m + 16)
                v.tensor_scalar(o_stage[:, h * W:(h + 1) * W], bank[4][:, 0:W], den, None, ALU.mult).then_inc(o_made, 1)
        tiles(v, per_tile, per_batch)

    return gpsimd, sync, tensor, scalar, vector


def attend_by_edge(nc, sem, carve, bank, pair, kind, L, lane, neighbour, local_row, row_from, row_to, ident,
                   starts, qq, kk, vv, si, sj, ao):
    tf = kind == "tf"
    G = B * HEADS if tf else B
    W = BD // G
    SCALE = float(HD) ** -0.5 if tf else 1.0
    (q_tile, ring, prod, weighted_v, o_stage, ge, spread, select, score, row_start, turned, row_max, prob, den, idx,
     sj_edge, raw) = carve((2, BD), (RING, BD), (2, BD), (2, BD), (2, BD), (2, P), (2, P), (2, P), (CMAX, G),
                           (EMAX + P,), (EMAX,), (EMAX,), (2, CMAX, G), (G,), (2, CMAX), (2, CMAX, B), (CMAX, B))
    idx = idx.bitcast(I32)
    new = lambda name: sem(f"{name}{L}")
    q_in = [new("q_in0_"), new("q_in1_")]
    landed = [new(f"landed{r}_") for r in range(RING)]
    sj_in = [new("sj_in0_"), new("sj_in1_")]
    start_in, idx_made = new("start_in"), new("idx_made")
    ge_made, spread_made, spread_q, prod_made, score_made = new("ge_made"), new("spread_made"), new("spread_q"), new("prod_made"), new("score_made")
    raw_made = new("raw_made")
    tp_full, tp_read = new("tp_full"), new("tp_read")
    scan_fwd, scan_back, shifted, prob_ready = new("scan_fwd"), new("scan_back"), new("shifted"), new("prob_ready")
    select_made, weighted, summed = new("select_made"), new("weighted"), new("summed")
    den_made, o_ready, o_out = new("den_made"), new("o_ready"), [new("o_out0_"), new("o_out1_")]
    den_step = new("den_step")
    zero = lambda t: isinstance(t, int) and t == 0
    GROUP_S, GROUP_P = 4, 8

    def slots_of(t, c, what):
        if tf:
            if isinstance(t, int):
                r = {0: 0, 1: CMAX}.get(t, 2 * CMAX + CREST + 2 * CREST * (t - 2)) + c + (0 if what == "k" or t == RT else edge_tiles(t))
                return r % RING, r // RING
            off = 2 * CMAX + CREST + c + (0 if what == "k" else CREST)
            return off % RING, (2 * CREST // RING) * (t - 2) + off // RING
        if isinstance(t, int):
            r = first_edge_tile(t - 1) + c
            return r % RING, r // RING
        off = CMAX + c
        return off % RING, (CREST // RING) * (t - 2) + off // RING

    def steps(eng, step):
        step(0, 0, 0)
        step(1, 1, 0)
        with eng.Fori(0, RT // 2 - 1) as i:
            step(2 * i + 2, 0, i + 1)
            step(2 * i + 3, 1, i + 1)
        step(RT, 0, RT // 2)

    def gpsimd(g):
        def step(t, par, half):
            last, first = isinstance(t, int) and t == RT, zero(t)
            if not last:
                if not (isinstance(t, int) and t < 2):
                    hold(g, weighted, first_edge_tile(t - 1))
                g.tensor_copy(idx[:, par:par + 1, :], neighbour[:, bass.ds(t, 1), :]).then_inc(idx_made, 1)
                hold(g, idx_made, t + 1)
                for c in range(edge_tiles(t)):
                    where = bass.IndirectOffsetOnAxis(ap=idx[:, par, c:c + 1], axis=0)
                    if not tf:
                        g.indirect_dma_start(out=sj_edge[:, par, c, :], out_offset=None, in_=sj, in_offset=where
                                             ).then_inc(sj_in[par], 16)
                        continue
                    slot, used = slots_of(t, c, "k")
                    if c >= RING:
                        hold(g, prod_made, first_edge_tile(t) + c - RING + 1)
                    elif isinstance(t, int) and t == 1:
                        hold(g, prod_made, CMAX + c - RING + 1)
                    elif not first:
                        hold(g, weighted, first_edge_tile(t - 1) + c - RING + 1)
                    g.indirect_dma_start(out=ring[:, slot, :], out_offset=None, in_=kk, in_offset=where
                                         ).then_inc(landed[slot], 16)
            if not first:
                for c in range(edge_tiles(t - 1)):
                    where = bass.IndirectOffsetOnAxis(ap=idx[:, 1 - par, c:c + 1], axis=0)
                    slot, used = slots_of(t, c, "v")
                    if c >= RING or not tf:
                        if not (isinstance(t, int) and t == 1 and c < RING):
                            hold(g, weighted, first_edge_tile(t - 1) + c - RING + 1)
                    elif not last:
                        hold(g, prod_made, first_edge_tile(t + 1) + c - RING + 1)
                    else:
                        hold(g, weighted, first_edge_tile(t - 1) + c - RING + 1)
                    g.indirect_dma_start(out=ring[:, slot, :], out_offset=None, in_=vv, in_offset=where
                                         ).then_inc(landed[slot], 16)
        steps(g, step)

    def sync(sp):
        def step(t, par, half):
            if not (isinstance(t, int) and t == RT):
                if not (isinstance(t, int) and t < 2):
                    sp.wait_ge(spread_q, first_edge_tile(t - 1))
                if tf:
                    sp.dma_start(q_tile[:, par:par + 1, :], qq[bass.ds(t, 1)].rearrange("r q n -> q r n")).then_inc(q_in[par], 16)
                else:
                    sp.dma_start(q_tile[:, par:par + 1, 0:B], si[bass.ds(t, 1)].rearrange("r q n -> q r n")).then_inc(q_in[par], 16)
                if not zero(t):
                    sp.wait_ge(scan_back, t)
                sp.dma_start(row_start[0:G, :], starts[bass.ds(t, 1), :].broadcast_to([G, EMAX + P])).then_inc(start_in, 16)
            if not (isinstance(t, int) and t < 2):
                sp.wait_ge(o_ready, t - 1)
                sp.dma_start(ao[bass.ds(t - 2, 1)].rearrange("r q n -> q r n"), o_stage[:, par:par + 1, :]).then_inc(o_out[par], 16)
        for s in range(2):
            sp.sem_inc(o_out[s], 16)
        steps(sp, step)
        sp.wait_ge(o_ready, RT)
        sp.dma_start(ao[RT - 1], o_stage[:, 1, :]).then_inc(o_out[1], 16)
        for s in range(2):
            sp.wait_ge(o_out[s], 16 * (RT // 2) + 16)

    def tensor(pe):
        def turn_scores(t, k):
            C = edge_tiles(t)
            lo, hi = k * GROUP_S, min((k + 1) * GROUP_S, C)
            pe.wait_ge(score_made, first_edge_tile(t) + hi if tf else t + 1)
            if not (zero(t) and k == 0):
                hold(pe, tp_read, 5 * t + k)
            for c in range(lo, hi):
                tr = pe.transpose(bank[6][0:G, (c - lo) * P:(c - lo + 1) * P], score[:, c, :], ident[:])
            tr.then_inc(tp_full, 1)

        def turn_probs(t, par, m):
            C = edge_tiles(t)
            lo, hi = m * GROUP_P, min((m + 1) * GROUP_P, C)
            pe.wait_ge(prob_ready, t + 1)
            hold(pe, tp_read, 5 * t + 3 + m)
            for c in range(lo, hi):
                tr = pe.transpose(bank[6][:, (c - lo) * G:(c - lo + 1) * G], turned[0:G, c * P:(c + 1) * P], ident[0:G, 0:G])
            tr.then_inc(tp_full, 1)

        def step(t, par, half):
            last = isinstance(t, int) and t == RT
            if not last:
                C, g0 = edge_tiles(t), first_edge_tile(t)
                pe.wait_ge(q_in[par], 16 * half + 16)
                if not tf and not (isinstance(t, int) and t < 2):
                    pe.wait_ge(raw_made, t - 1)
                for c in range(C):
                    slot = (c + (0 if zero(t) else 1)) % 2
                    pe.wait_ge(spread_made, g0 + c + 1)
                    if tf:
                        if not (zero(t) and c < 2):
                            pe.wait_ge(prod_made, g0 + c - 1)
                        for h in range(2):
                            mm = pe.matmul(pair[slot][:, h * 512:(h + 1) * 512], spread[:, slot, :],
                                           q_tile[:, par, h * 512:(h + 1) * 512], start=True, stop=True)
                        mm.then_inc(spread_q, 1)
                        if c == 6:
                            turn_scores(t, 0)
                        if c == C - 1:
                            turn_scores(t, 1)
                    else:
                        pe.matmul(pair[par][:, c * B:(c + 1) * B], spread[:, slot, :], q_tile[:, par, 0:B],
                                  start=True, stop=True).then_inc(spread_q, 1)
                if not tf:
                    turn_scores(t, 0)
                    turn_scores(t, 1)
                turn_scores(t, 2)
            if zero(t):
                turn_probs(t, par, 0)
                turn_probs(t, par, 1)
                return
            C, h0 = edge_tiles(t - 1), first_edge_tile(t - 1)
            for c in range(C):
                slot = (c + (0 if zero(t - 1) else 1)) % 2
                if c == 0:
                    pe.wait_ge(tp_read, 5 * (t - 1) + 5)
                    if not zero(t - 1):
                        pe.wait_ge(o_ready, t - 1)
                pe.wait_ge(select_made, h0 + c + 1)
                pe.wait_ge(weighted, h0 + c + 1)
                ends = dict(start=(c == 0), stop=(c == C - 1))
                for h in range(2):
                    pe.matmul(pair[2][:, h * 512:(h + 1) * 512], select[:, slot, :],
                              weighted_v[:, slot, h * 512:(h + 1) * 512], **ends)
                pe.matmul(bank[7][:, 0:G], select[:, slot, :], prob[:, 1 - par, c, :], **ends).then_inc(summed, 1)
                if not last and c in (2, 4):
                    turn_probs(t, par, c // 2 - 1)
        steps(pe, step)

    def scalar(act):
        def step(t, par, half):
            if isinstance(t, int) and t == RT:
                return
            C = edge_tiles(t)
            for k in range(3):
                lo, hi = k * GROUP_S, min((k + 1) * GROUP_S, C)
                act.wait_ge(tp_full, 5 * t + k + 1)
                act.copy(turned[0:G, lo * P:hi * P], bank[6][0:G, 0:(hi - lo) * P]).then_inc(tp_read, 1)
            act.wait_ge(shifted, t + 1)
            act.activation(turned[0:G, 0:C * P], turned[0:G, 0:C * P], ACT.Exp, scale=SCALE).then_inc(prob_ready, 1)
            for m in range(2):
                lo, hi = m * GROUP_P, min((m + 1) * GROUP_P, C)
                act.wait_ge(tp_full, 5 * t + 3 + m + 1)
                if m == 0 and not (isinstance(t, int) and t < 2):
                    act.wait_ge(summed, first_edge_tile(t - 1))
                act.copy(prob[:, par, lo:hi, :], bank[6][:, 0:(hi - lo) * G].rearrange("p (c g) -> p c g", g=G)).then_inc(tp_read, 1)
        steps(act, step)

    def vector(v):
        def make_spread(t, c):
            g0 = first_edge_tile(t)
            slot = (c + (0 if zero(t) else 1)) % 2
            if not (zero(t) and c < 2):
                v.wait_ge(spread_q, g0 + c - 1)
            v.tensor_scalar(ge[:, slot, :], lane[:], row_from[:, bass.ds(t, 1), c], None, ALU.is_ge).then_inc(ge_made, 1)
            v.wait_ge(ge_made, g0 + c + 1)
            v.scalar_tensor_tensor(spread[:, slot, :], lane[:], row_to[:, bass.ds(t, 1), c], ge[:, slot, :],
                                   ALU.is_lt, ALU.mult).then_inc(spread_made, 1)

        def scores_tf(t, par):
            C, g0 = edge_tiles(t), first_edge_tile(t)
            make_spread(t, 0)
            make_spread(t, 1)
            for c in range(C):
                slot = (c + (0 if zero(t) else 1)) % 2
                r_slot, used = slots_of(t, c, "k")
                v.wait_ge(landed[r_slot], 16 * used + 16)
                v.wait_ge(spread_q, g0 + c + 1)
                if not (zero(t) and c < 2):
                    v.wait_ge(score_made, g0 + c - 1)
                v.tensor_tensor(prod[:, slot, :], pair[slot][:], ring[:, r_slot, :], ALU.mult).then_inc(prod_made, 1)
                if c + 2 < C:
                    make_spread(t, c + 2)
                v.wait_ge(prod_made, g0 + c + 1)
                if c == 0 and not zero(t):
                    v.wait_ge(tp_full, 5 * (t - 1) + 3)
                v.tensor_reduce(score[:, c, :], prod[:, slot, :].rearrange("p (g w) -> p g w", w=W), AX.X, ALU.add
                                ).then_inc(score_made, 1)

        def scores_gat(t, par, half):
            C = edge_tiles(t)
            for c in range(C):
                make_spread(t, c)
            v.wait_ge(spread_q, first_edge_tile(t) + C)
            v.wait_ge(sj_in[par], 16 * (CREST * (half + 1) + (CMAX - CREST if par == 0 else 0)))
            if not zero(t):
                v.wait_ge(score_made, t)
                v.wait_ge(tp_full, 5 * (t - 1) + 3)
            v.tensor_tensor(raw[:, 0:C, :], pair[par][:, 0:C * B].rearrange("p (c b) -> p c b", b=B),
                            sj_edge[:, par, 0:C, :], ALU.add).then_inc(raw_made, 1)
            v.wait_ge(raw_made, t + 1)
            v.scalar_tensor_tensor(score[:, 0:C, :], raw[:, 0:C, :], SLOPE, raw[:, 0:C, :], ALU.mult, ALU.max
                                   ).then_inc(score_made, 1)

        def shift(t):
            E = edge_tiles(t) * P
            v.wait_ge(tp_read, 5 * t + 3)
            v.wait_ge(start_in, 16 * t + 16)
            if not zero(t):
                v.wait_ge(shifted, t)
            v.tensor_tensor_scan(row_max[0:G, 0:E], row_start[0:G, 0:E], turned[0:G, 0:E], -BIG, ALU.add, ALU.max
                                 ).then_inc(scan_fwd, 1)
            v.wait_ge(scan_fwd, t + 1)
            back = row_max[0:G, 0:E][:, ::-1]
            v.tensor_tensor_scan(back, row_start[0:G, 1:E + 1][:, ::-1], back, -BIG, ALU.add, ALU.max
                                 ).then_inc(scan_back, 1)
            v.wait_ge(scan_back, t + 1)
            v.tensor_tensor(turned[0:G, 0:E], turned[0:G, 0:E], row_max[0:G, 0:E], ALU.subtract).then_inc(shifted, 1)

        def sums(t, step_t, par, uses):
            C, h0 = edge_tiles(t), first_edge_tile(t)
            v.wait_ge(tp_read, 5 * t + 5)
            for c in range(C):
                slot = (c + (0 if zero(t) else 1)) % 2
                r_slot, used = slots_of(step_t, c, "v")
                if not (zero(t) and c < 2):
                    v.wait_ge(summed, h0 + c - 1)
                v.tensor_scalar(select[:, slot, :], lane[:], local_row[:, bass.ds(t, 1), c], None, ALU.is_equal
                                ).then_inc(select_made, 1)
                v.wait_ge(landed[r_slot], 16 * used + 16)
                v.tensor_tensor(weighted_v[:, slot, :].rearrange("p (g w) -> p g w", w=W),
                                ring[:, r_slot, :].rearrange("p (g w) -> p g w", w=W),
                                prob[:, par, c, :].rearrange("p (g a) -> p g a", a=1).broadcast_to([P, G, W]), ALU.mult
                                ).then_inc(weighted, 1)
            v.wait_ge(summed, h0 + C)
            if not zero(t):
                v.wait_ge(o_ready, t)
            v.tensor_scalar(den, bank[7][:, 0:G], TINY, None, ALU.max).then_inc(den_step, 1)
            v.wait_ge(den_step, 2 * t + 1)
            v.reciprocal(den, den).then_inc(den_step, 1)
            v.wait_ge(den_step, 2 * t + 2)
            v.wait_ge(o_out[par], 16 * uses + 16)
            v.tensor_tensor(o_stage[:, par, :].rearrange("p (g w) -> p g w", w=W), pair[2][:].rearrange("p (g w) -> p g w", w=W),
                            den.rearrange("p (g a) -> p g a", a=1).broadcast_to([P, G, W]), ALU.mult).then_inc(o_ready, 1)

        def step(t, par, half):
            if not (isinstance(t, int) and t == RT):
                scores_tf(t, par) if tf else scores_gat(t, par, half)
                shift(t)
            if not zero(t):
                sums(t - 1, t, 1 - par, half if par else half - 1)
        steps(v, step)

    return gpsimd, sync, tensor, scalar, vector


def post_gat(nc, sem, carve, bank, w, L, ident, eps_col, xs, ao):
    x_tile, o_tile, y, z, stats, mv, sd, rs = carve((2, BD), (2, BD), (2, BD), (2, BD), (B, 6), (2, B, 2), (2, B), (2, B))
    new = lambda name: sem(f"{name}{L}")
    x_in, o_in = [new("px0_"), new("px1_")], [new("po0_"), new("po1_")]
    moments, roots, normed, scaled, moved, stored = new("moments"), new("roots"), new("normed"), new("scaled"), new("moved"), [new("st0_"), new("st1_")]
    dv = new("pdv")

    def steps(eng, step):
        step(0, 0, 0)
        step(1, 1, 0)
        with eng.Fori(1, RT // 2) as i:
            step(2 * i, 0, i)
            step(2 * i + 1, 1, i)

    early = lambda t: isinstance(t, int) and t < 2
    with nc.Block() as block:
        @block.sync
        def _(sp):
            def step(t, par, half):
                if not early(t):
                    hold(sp, moments, t - 1)
                    hold(sp, stored[par], 16 * half)
                tile = lambda x: x[bass.ds(t, 1)].rearrange("r q n -> q r n")
                sp.dma_start(x_tile[:, par:par + 1, :], tile(xs)).then_inc(x_in[par], 16)
                sp.dma_start(o_tile[:, par:par + 1, :], tile(ao)).then_inc(o_in[par], 16)
            steps(sp, step)

        @block.scalar
        def _(act):
            def step(t, par, half):
                act.wait_ge(moments, t + 1)
                if not early(t):
                    act.wait_ge(normed, t - 1)
                act.activation(sd[:, par, :], mv[:, par, :, 1], ACT.Sqrt, bias=eps_col[:, 0:1]).then_inc(roots, 1)
                if not zero_int(t):
                    store(t - 1, 1 - par)

            def store(t, par):
                act.wait_ge(moved, t + 1)
                act.dma_start(xs[bass.ds(t, 1)].rearrange("r q n -> q r n"), z[:, par:par + 1, :]).then_inc(stored[par], 16)

            zero_int = lambda t: isinstance(t, int) and t == 0
            steps(act, step)
            store(RT - 1, 1)
            for s in range(2):
                act.wait_ge(stored[s], 16 * (RT // 2))

        @block.vector
        def _(v):
            ch = Chain(v, dv)

            def front(t, par, half):
                v.wait_ge(x_in[par], 16 * half + 16)
                v.wait_ge(o_in[par], 16 * half + 16)
                if not early(t):
                    v.wait_ge(normed, t - 1)
                ch.link(v.tensor_tensor(y[:, par, :], x_tile[:, par, :], o_tile[:, par, :], ALU.add))
                if not (isinstance(t, int) and t == 0):
                    v.wait_ge(moments, t)
                for b in range(B):
                    ins = v.bn_stats(stats[:, b, :], y[:, par, b * D:(b + 1) * D])
                ch.link(ins)
                v.nop(nofuse=True)
                for b in range(B):
                    ins = v.bn_aggr(mv[:, par, b, :], stats[:, b, :])
                ins.then_inc(moments, 1)

            def back(t, par, half):
                v.wait_ge(roots, t + 1)
                ch.link(v.reciprocal(rs[:, par, :], sd[:, par, :]))
                if not early(t):
                    v.wait_ge(scaled, t)
                for b in range(B):
                    ins = v.tensor_scalar(y[:, par, b * D:(b + 1) * D], y[:, par, b * D:(b + 1) * D], mv[:, par, b, 0:1],
                                          rs[:, par, b:b + 1], ALU.subtract, ALU.mult)
                ins.then_inc(normed, 1)

            front(0, 0, 0)
            front(1, 1, 0)
            back(0, 0, 0)
            with v.Fori(1, RT // 2) as i:
                ch.loop(i - 1, 2 * 3)
                front(2 * i, 0, i)
                back(2 * i - 1, 1, i)
                front(2 * i + 1, 1, i)
                back(2 * i, 0, i)
            ch.end(RT // 2 - 1)
            back(RT - 1, 1, 0)

        @block.gpsimd
        def _(g):
            def step(t, par, half):
                g.wait_ge(normed, t + 1)
                row = lambda k: w["gb"][:, k:k + 1, :].broadcast_to([P, B, D])
                as3 = lambda x: x.rearrange("p (b d) -> p b d", b=B)
                if not early(t):
                    g.wait_ge(stored[par], 16 * half)
                g.tensor_tensor(as3(z[:, par, :]), as3(y[:, par, :]), row(0), ALU.mult).then_inc(scaled, 1)
                g.wait_ge(scaled, t + 2)
                g.tensor_tensor(as3(z[:, par, :]), as3(z[:, par, :]), row(1), ALU.add).then_inc(moved, 1)
            g.sem_inc(scaled, 1)
            steps(g, step)


def post_tf(nc, sem, carve, bank, w, L, ident, eps_col, xs, ao):
    GW = 4 * D
    GROUPS = 2 * RT
    (x_tile, o_tile, o_turned, xb, y1, x1, x1_turned, hidden, x1b, y2, x2, stats1, stats2, mv1, mv2, sd1, sd2, rs1,
     rs2) = carve((4, GW), (4, GW), (2, GW), (2, GW), (2, GW), (4, GW), (2, GW), (2, FC, GW), (4, GW), (2, GW), (4, GW),
                  (4, 6), (4, 6), (2, 4, 2), (2, 4, 2), (2, 4), (2, 4), (2, 4), (2, 4))
    new = lambda name: sem(f"{name}{L}")
    x_in, o_in = [new(f"fx{s}_") for s in range(2)], [new(f"fo{s}_") for s in range(2)]
    o_tr, o_copied, o_prod = new("o_tr"), new("o_copied"), new("o_prod")
    x1_tr, x1_copied, h_prod, h_relu, y2_prod = new("x1_tr"), new("x1_copied"), new("h_prod"), new("h_relu"), new("y2_prod")
    xb_made, y1_made, y2_made = new("xb_made"), new("y1_made"), new("y2_made")
    m1, m2, r1, r2, n1, n2 = new("m1"), new("m2"), new("r1"), new("r2"), new("n1"), new("n2")
    g1, x1_made, x1b_made, g2, x2_made = new("g1"), new("x1_made"), new("x1b_made"), new("g2"), new("x2_made")
    stored = [new(f"fst{s}_") for s in range(2)]
    dv = new("fdv")

    def turns(eng, turn):
        for k in range(4):
            turn(k, k, 0)
        with eng.Fori(1, GROUPS // 4) as i:
            for j in range(4):
                turn(4 * i + j, j, i)
        for k in range(GROUPS, GROUPS + 2):
            turn(k, k % 4, GROUPS // 4)

    def has(k, lag=0):
        return not isinstance(k, int) or 0 <= k - lag < GROUPS

    def past(k, lag):
        return not (isinstance(k, int) and k < lag)

    as3 = lambda x: x.rearrange("p (b d) -> p b d", b=4)
    row = lambda r: r.broadcast_to([P, 4, D])

    with nc.Block() as block:
        @block.sync
        def _(sp):
            def turn(k, j, i):
                if past(k, 3) and j % 2 == 1:
                    s4 = (j - 2) % 4
                    t = 2 * (i if j >= 2 else i - 1) + s4 // 2
                    sp.wait_ge(x2_made, k - 1)
                    sp.dma_start(xs[bass.ds(t, 1)].rearrange("r q (h n) -> q (r h) n", h=2), x2[:, s4 - 1:s4 + 1, :]
                                 ).then_inc(stored[s4 // 2], 16)

            for s in range(2):
                sp.sem_inc(stored[s], 16)
            turns(sp, turn)
            for s in range(2):
                sp.wait_ge(stored[s], 16 * (RT // 2) + 16)

        @block.tensor
        def _(pe):
            def turn_o(n, j, i):
                if j % 2 == 0:
                    pe.wait_ge(o_in[j // 2], 16 * i + 16)
                if past(n, 1):
                    pe.wait_ge(o_copied, n)
                for b in range(4):
                    tr = pe.transpose(bank[0][:, b * P:(b + 1) * P], o_tile[:, j, b * D:(b + 1) * D], ident[:])
                tr.then_inc(o_tr, 1)

            def turn(k, j, i):
                if has(k):
                    pe.wait_ge(o_copied, k + 1)
                    if past(k, 1):
                        pe.wait_ge(y1_made, k)
                    for b in range(4):
                        mm = pe.matmul(bank[1][:, b * D:(b + 1) * D], o_turned[:, j % 2, b * P:(b + 1) * P], w["wo"][:],
                                       start=True, stop=True)
                    mm.then_inc(o_prod, 1)
                if has(k, -1):
                    turn_o(k + 1, (j + 1) % 4, i + 1 if j == 3 else i)
                if past(k, 1) and has(k, 1):
                    n, s = k - 1, (j - 1) % 4
                    pe.wait_ge(x1_made, n + 1)
                    if past(n, 1):
                        pe.wait_ge(x1_copied, n)
                    for b in range(4):
                        tr = pe.transpose(bank[2][:, b * P:(b + 1) * P], x1[:, s, b * D:(b + 1) * D], ident[:])
                    tr.then_inc(x1_tr, 1)
                if past(k, 2) and has(k, 2):
                    n, s = k - 2, (j - 2) % 2
                    pe.wait_ge(h_relu, FC * n + FC)
                    if past(n, 1):
                        pe.wait_ge(y2_made, n)
                    for b in range(4):
                        for c in range(FC):
                            mm = pe.matmul(bank[5][:, b * D:(b + 1) * D], hidden[:, s, c, b * P:(b + 1) * P], w["w2"][:, c, :],
                                           start=(c == 0), stop=(c == FC - 1))
                    mm.then_inc(y2_prod, 1)
                if past(k, 1) and has(k, 1):
                    n, s = k - 1, (j - 1) % 2
                    pe.wait_ge(x1_copied, n + 1)
                    for c in range(FC):
                        if past(n, 1):
                            pe.wait_ge(h_relu, FC * (n - 1) + c + 1)
                        pe.matmul(bank[3 + c], w["w1"][:, c * P:(c + 1) * P], x1_turned[:, s, :], start=True, stop=True
                                  ).then_inc(h_prod, 1)

            turn_o(0, 0, 0)
            for k in range(4):
                turn(k, k, 0)
            with pe.Fori(1, GROUPS // 4 - 1) as i:
                for j in range(4):
                    turn(4 * i + j, j, i)
            for k in range(GROUPS - 4, GROUPS + 2):
                turn(k, k % 4, k // 4)

        @block.scalar
        def _(act):
            def load(n, j, i):
                par = j // 2
                if past(n, 4):
                    act.wait_ge(y1_made, n - 2)
                    act.wait_ge(xb_made, n - 2)
                    act.wait_ge(o_tr, n - 2)
                t = 2 * i + par
                tile = lambda x: x[bass.ds(t, 1)].rearrange("r q (h n) -> q (r h) n", h=2)
                act.dma_start(x_tile[:, j:j + 2, :], tile(xs)).then_inc(x_in[par], 16)
                act.dma_start(o_tile[:, j:j + 2, :], tile(ao)).then_inc(o_in[par], 16)

            def copy_o(n, j):
                act.wait_ge(o_tr, n + 1)
                if past(n, 2):
                    act.wait_ge(o_prod, n - 1)
                act.copy(o_turned[:, j % 2, :], bank[0]).then_inc(o_copied, 1)

            def turn(k, j, i):
                if has(k, -2) and past(k, 1) and j % 2 == 0:
                    load(k + 2, (j + 2) % 4, i + 1 if j == 2 else i)
                if has(k, -1):
                    copy_o(k + 1, j + 1)
                if past(k, 1) and has(k, 1):
                    n, s = k - 1, (j - 1) % 2
                    act.wait_ge(x1_tr, n + 1)
                    if past(n, 2):
                        act.wait_ge(h_prod, FC * (n - 1))
                    act.copy(x1_turned[:, s, :], bank[2]).then_inc(x1_copied, 1)
                if past(k, 2) and has(k, 2):
                    n, s = k - 2, (j - 2) % 2
                    act.wait_ge(m2, n + 1)
                    if past(n, 2):
                        act.wait_ge(n2, n - 1)
                    act.activation(sd2[:, s, :], mv2[:, s, :, 1], ACT.Sqrt, bias=eps_col[:, 0:1]).then_inc(r2, 1)
                if has(k):
                    act.wait_ge(m1, k + 1)
                    if past(k, 2):
                        act.wait_ge(n1, k - 1)
                    act.activation(sd1[:, j % 2, :], mv1[:, j % 2, :, 1], ACT.Sqrt, bias=eps_col[:, 0:1]).then_inc(r1, 1)
                if past(k, 1) and has(k, 1):
                    n, s = k - 1, (j - 1) % 2
                    if past(n, 2):
                        act.wait_ge(y2_prod, n - 1)
                    for c in range(FC):
                        act.wait_ge(h_prod, FC * n + c + 1)
                        act.activation(hidden[:, s, c, :], bank[3 + c], ACT.Relu, bias=w["b1"][:, c:c + 1]).then_inc(h_relu, 1)

            load(0, 0, 0)
            load(2, 2, 0)
            copy_o(0, 0)
            for k in range(4):
                turn(k, k, 0)
            with act.Fori(1, GROUPS // 4 - 1) as i:
                for j in range(4):
                    turn(4 * i + j, j, i)
            for k in range(GROUPS - 4, GROUPS + 2):
                turn(k, k % 4, k // 4)

        @block.vector
        def _(v):
            ch = Chain(v, dv)

            def moments(y, stats, mv, sem_m):
                for b in range(4):
                    ins = v.bn_stats(stats[:, b, :], y[:, b * D:(b + 1) * D])
                ch.link(ins)
                v.nop(nofuse=True)
                for b in range(4):
                    ins = v.bn_aggr(mv[:, b, :], stats[:, b, :])
                ins.then_inc(sem_m, 1)

            def normalise(y, mv, sd, rs, sem_n):
                ch.link(v.reciprocal(rs, sd))
                for b in range(4):
                    ins = v.tensor_scalar(y[:, b * D:(b + 1) * D], y[:, b * D:(b + 1) * D], mv[:, b, 0:1], rs[:, b:b + 1],
                                          ALU.subtract, ALU.mult)
                ins.then_inc(sem_n, 1)

            def turn(k, j, i):
                if has(k):
                    s = j % 2
                    v.wait_ge(o_prod, k + 1)
                    v.wait_ge(xb_made, k + 1)
                    if past(k, 2):
                        v.wait_ge(g1, k - 1)
                    if past(k, 1):
                        v.wait_ge(m1, k)
                        v.wait_ge(n1, k)
                    v.tensor_tensor(y1[:, s, :], bank[1], xb[:, s, :], ALU.add).then_inc(y1_made, 1)
                    v.wait_ge(y1_made, k + 1)
                    moments(y1[:, s, :], stats1, mv1[:, s], m1)
                if past(k, 2) and has(k, 2):
                    n, s = k - 2, (j - 2) % 2
                    v.wait_ge(y2_prod, n + 1)
                    v.wait_ge(x1b_made, n + 1)
                    if past(n, 2):
                        v.wait_ge(g2, n - 1)
                    if past(n, 1):
                        v.wait_ge(m2, n)
                        v.wait_ge(n2, n)
                    v.tensor_tensor(y2[:, s, :], bank[5], x1b[:, (j - 2) % 4, :], ALU.add).then_inc(y2_made, 1)
                    v.wait_ge(y2_made, n + 1)
                    moments(y2[:, s, :], stats2, mv2[:, s], m2)
                if has(k):
                    s = j % 2
                    v.wait_ge(r1, k + 1)
                    normalise(y1[:, s, :], mv1[:, s], sd1[:, s, :], rs1[:, s, :], n1)
                if past(k, 2) and has(k, 2):
                    n, s = k - 2, (j - 2) % 2
                    v.wait_ge(r2, n + 1)
                    normalise(y2[:, s, :], mv2[:, s], sd2[:, s, :], rs2[:, s, :], n2)

            for k in range(4):
                turn(k, k, 0)
            with v.Fori(1, GROUPS // 4) as i:
                ch.loop(i - 1, 4 * 2 * 2)
                for j in range(4):
                    turn(4 * i + j, j, i)
            ch.end(GROUPS // 4 - 1)
            for k in range(GROUPS, GROUPS + 2):
                turn(k, k % 4, GROUPS // 4)

        @block.gpsimd
        def _(g):
            def add_bo(n, j, i):
                if j % 2 == 0:
                    g.wait_ge(x_in[j // 2], 16 * i + 16)
                if past(n, 2):
                    g.wait_ge(y1_made, n - 1)
                g.tensor_tensor(as3(xb[:, j % 2, :]), as3(x_tile[:, j, :]), row(w["bias"][:, 0:1, :]), ALU.add).then_inc(xb_made, 1)

            def turn(k, j, i):
                if has(k, -1):
                    add_bo(k + 1, (j + 1) % 4, i + 1 if j == 3 else i)
                if has(k):
                    s = j % 2
                    g.wait_ge(n1, k + 1)
                    if past(k, 4):
                        g.wait_ge(x1_tr, k - 3)
                        g.wait_ge(x1b_made, k - 3)
                    g.tensor_tensor(as3(x1[:, j, :]), as3(y1[:, s, :]), row(w["gb"][:, 0:1, :]), ALU.mult).then_inc(g1, 1)
                    g.wait_ge(g1, k + 1)
                    g.tensor_tensor(as3(x1[:, j, :]), as3(x1[:, j, :]), row(w["gb"][:, 1:2, :]), ALU.add).then_inc(x1_made, 1)
                    g.wait_ge(x1_made, k + 1)
                    if past(k, 4):
                        g.wait_ge(y2_made, k - 3)
                    g.tensor_tensor(as3(x1b[:, j, :]), as3(x1[:, j, :]), row(w["bias"][:, 1:2, :]), ALU.add).then_inc(x1b_made, 1)
                if past(k, 2) and has(k, 2):
                    n, s, s4 = k - 2, (j - 2) % 2, (j - 2) % 4
                    g.wait_ge(n2, n + 1)
                    if past(n, 4) and s4 % 2 == 0:
                        g.wait_ge(stored[s4 // 2], 16 * (i if j >= 2 else i - 1) + 16)
                    g.tensor_tensor(as3(x2[:, s4, :]), as3(y2[:, s, :]), row(w["gb"][:, 2:3, :]), ALU.mult).then_inc(g2, 1)
                    g.wait_ge(g2, n + 1)
                    g.tensor_tensor(as3(x2[:, s4, :]), as3(x2[:, s4, :]), row(w["gb"][:, 3:4, :]), ALU.add).then_inc(x2_made, 1)

            add_bo(0, 0, 0)
            for k in range(4):
                turn(k, k, 0)
            with g.Fori(1, GROUPS // 4 - 1) as i:
                for j in range(4):
                    turn(4 * i + j, j, i)
            for k in range(GROUPS - 4, GROUPS + 2):
                turn(k, k % 4, k // 4)


_INS = ['x', 'adj'] + [f'L{L}_gnn_{n}' for L in (0, 3) for n in ('W', 'a_src', 'a_dst', 'ln_gamma', 'ln_beta')] + \
       [f'L{L}_gnn_{n}' for L in (1, 2) for n in ('Wq', 'Wk', 'Wv', 'Wo', 'bo', 'ln1_g', 'ln1_b', 'W1', 'b1', 'W2', 'b2',
                                                  'ln2_g', 'ln2_b')]


def kernel(**inputs):
    import numpy as _np
    import concourse.bacc as _bacc
    from concourse import mybir as _mybir
    from concourse.bass_utils import run_bass_kernel_spmd as _run

    nc = _bacc.Bacc("TRN2", target_bir_lowering=False, num_devices=1)
    arrays, args = {}, {}
    for name in _INS:
        x = _np.ascontiguousarray(inputs[name])
        arrays[f"in_{name}_dram"] = x
        args[name] = nc.dram_tensor(f"in_{name}_dram", x.shape, _mybir.dt.from_np(x.dtype), kind="ExternalInput").ap()
    out = nc.dram_tensor("out_0_dram", (B, N, D), _mybir.dt.float32, kind="ExternalOutput").ap()
    build(nc, args, out)
    r = _run(nc, [arrays], core_ids=[0])
    return r.results[0]["out_0_dram"]
```

```python
import concourse.bass as bass
from concourse import mybir
from contextlib import ExitStack

F32 = mybir.dt.float32
I32 = mybir.dt.int32
ONE_HOT = mybir.dt.uint8
ALU = mybir.AluOpType
ACT = mybir.ActivationFunctionType
AX = mybir.AxisListType

P = 128
B, N, D = 8, 2048, 128
RT = N // P
BD = B * D
HEADS, HD = 8, 16
FFN = 2 * D
FC = FFN // P
CMAX = 11
CREST = 10
EMAX = CMAX * P
BLK = 64
NBLK = N // BLK
COL_OFS, COL_ROW, COL_LOC = NBLK, NBLK + 1, NBLK + 2
TABW = NBLK + 3
ARENA = 33792
BIG = 1.0e30
TINY = 1.0e-30
SLOPE = 0.2
EPS = 1e-5
KINDS = ("gat", "tf", "tf", "gat")


class Chain:

    def __init__(self, eng, sem):
        self.eng, self.sem, self.base, self.n = eng, sem, 0, 0

    def link(self, ins):
        ins.then_inc(self.sem, 1)
        self.n += 1
        self.eng.wait_ge(self.sem, self.base + self.n)

    def loop(self, i, per):
        self.start, self.per = self.base + self.n, per
        self.base, self.n = self.start + i * per, 0

    def end(self, turns):
        assert self.n == self.per, (self.n, self.per)
        self.base, self.n = self.start + turns * self.per, 0


class Semaphores:

    def __init__(self, nc):
        self.nc, self.made = nc, {}

    def get(self, name):
        if name not in self.made:
            self.made[name] = self.nc.alloc_semaphore(name)
        return self.made[name]

    def renew(self):
        if self.made:
            self.nc.clear_and_free_semaphores(list(self.made.values()))
            self.nc.all_engine_barrier()
        self.made = {}


def hold(eng, sem, value):
    eng.wait_ge(sem, value)
    eng.nop(nofuse=True)


def first_edge_tile(t):
    return 0 if isinstance(t, int) and t == 0 else CMAX + CREST * (t - 1)


def edge_tiles(t):
    return CMAX if isinstance(t, int) and t == 0 else CREST


def build(nc, a, out, layers=4):
    ctx = ExitStack()
    with ctx:
        def sb(name, shape, dt=F32):
            return ctx.enter_context(nc.sbuf_tensor(name, shape, dt))

        def ps(name, shape):
            return ctx.enter_context(nc.psum_tensor(name, shape, F32))

        sems = Semaphores(nc)
        sem = sems.get

        xs = nc.dram_tensor("xs", (RT, P, BD), F32).ap()
        ao = nc.dram_tensor("ao", (RT, P, BD), F32).ap()
        qq = nc.dram_tensor("qq", (RT, P, BD), F32).ap()
        si = nc.dram_tensor("si", (RT, P, B), F32).ap()
        kk = nc.dram_tensor("kk", (N, BD), F32).ap()
        vv = nc.dram_tensor("vv", (N, BD), F32).ap()
        sj = nc.dram_tensor("sj", (N, B), F32).ap()
        starts = nc.dram_tensor("starts", (RT, EMAX + P), F32).ap()

        ident = sb("ident", [P, P])
        ones = sb("ones", [P, P])
        below = sb("below", [P, P])
        lane = sb("lane", [P, P])
        edge_id = sb("edge_id", [P, CMAX])
        tile_start = sb("tile_start", [P, CMAX])
        capacity = sb("capacity", [P, RT])
        fits = sb("fits", [P, 1], I32)
        neighbour = sb("neighbour", [P, RT, CMAX], I32)
        local_row = sb("local_row", [P, RT, CMAX])
        row_from = sb("row_from", [P, RT, CMAX])
        row_to = sb("row_to", [P, RT, CMAX])
        spread_bits = sb("spread_bits", [P, RT, CMAX, P], ONE_HOT)
        select_bits = sb("select_bits", [P, RT, CMAX, P], ONE_HOT)
        w = {}
        for L, kind in enumerate(KINDS):
            if kind == "tf":
                w[L] = dict(qkv=sb(f"wqkv{L}", [P, 3 * D]), wo=sb(f"wo{L}", [P, D]), w1=sb(f"w1{L}", [P, FFN]),
                            w2=sb(f"w2{L}", [P, FC, D]), b1=sb(f"b1{L}", [P, FC]), bias=sb(f"bias{L}", [P, 2, D]),
                            gb=sb(f"gb{L}", [P, 4, D]))
            else:
                w[L] = dict(w=sb(f"w{L}", [P, D + 2]), av=sb(f"av{L}", [P, 2]), gb=sb(f"gb{L}", [P, 2, D]))
        eps_col = sb("eps_col", [P, 1])

        arena = sb("arena", [P, ARENA])

        def carve(*shapes):
            at, views = 0, []
            for shape in shapes:
                size = 1
                for s in shape:
                    size *= s
                v = arena[:, at:at + size]
                if len(shape) == 2:
                    v = v.rearrange("p (a b) -> p a b", a=shape[0])
                if len(shape) == 3:
                    v = v.rearrange("p (a b c) -> p a b c", a=shape[0], b=shape[1])
                views.append(v)
                at += size
            assert at <= ARENA, at
            return views

        bank = [ps(f"bank{i}", [P, 4 * P]) if i in (6, 7) else None for i in range(8)]
        pair = [ps(f"pair{i}", [P, 8 * P]) for i in range(3)]
        bank[0], bank[1] = pair[0][:, 0:512], pair[0][:, 512:1024]
        bank[2], bank[3] = pair[1][:, 0:512], pair[1][:, 512:1024]
        bank[4], bank[5] = pair[2][:, 0:512], pair[2][:, 512:1024]

        x_by_row = a["x"].rearrange("b (q r) d -> r q b d", r=RT)
        out_by_row = out.rearrange("b (q r) d -> r q b d", r=RT)
        adj_by_row = a["adj"].rearrange("(q r) n -> r q n", r=RT)
        kk_by_row = kk.rearrange("(q r) n -> r q n", r=RT)
        vv_by_row = vv.rearrange("(q r) n -> r q n", r=RT)
        sj_by_row = sj.rearrange("(q r) n -> r q n", r=RT)

        def tile_rows(view, t):
            return (view[bass.ds(t, 1), 0:1], view[bass.ds(RT - 1 - t, 1), 1:P])

        row_count, = carve((1,))
        nz, adj_rows, block_sum, cum, keep32, table, deg, before, total, over = carve(
            (N,), (2, N), (RT, NBLK), (RT * NBLK,), (RT * NBLK,), (RT, TABW), (RT,), (RT,), (RT,), (RT,))
        adj_rows = adj_rows.bitcast(I32)
        with nc.Block() as block:
            w_in = sem("w_in")
            adj_in = [sem("adj_in0"), sem("adj_in1")]
            adj_read, const_made, counts, dv = sem("adj_read"), sem("const_made"), sem("counts"), sem("dv0")
            prefix = sem("prefix")

            @block.sync
            def _(sp):
                def load(t, slot):
                    for src, lo, hi in zip(tile_rows(adj_by_row, t), (0, 1), (1, P)):
                        sp.dma_start(adj_rows[lo:hi, slot:slot + 1, :], src.rearrange("r q n -> q r n")
                                     ).then_inc(adj_in[slot], 16)

                load(0, 0)
                load(1, 1)
                with sp.Fori(1, RT // 2) as i:
                    for slot in range(2):
                        sp.wait_ge(adj_read, 2 * i - 1 + slot)
                        load(2 * i + slot, slot)

            @block.scalar
            def _(act):
                n = 0
                for L, kind in enumerate(KINDS):
                    pre = f"L{L}_gnn_"
                    if kind == "tf":
                        loads = [(w[L]["qkv"][:, k * D:(k + 1) * D], a[pre + m]) for k, m in enumerate(("Wq", "Wk", "Wv"))]
                        loads += [(w[L]["wo"][:], a[pre + "Wo"]), (w[L]["w1"][:], a[pre + "W1"]),
                                  (w[L]["w2"][:], a[pre + "W2"].rearrange("(c p) n -> p c n", p=P)),
                                  (w[L]["bias"][:, 0, :], a[pre + "bo"].rearrange("(a n) -> a n", a=1).broadcast_to([P, D])),
                                  (w[L]["bias"][:, 1, :], a[pre + "b2"].rearrange("(a n) -> a n", a=1).broadcast_to([P, D]))]
                        loads += [(w[L]["b1"][:, c:c + 1], a[pre + "b1"][c * P:(c + 1) * P].rearrange("(p a) -> p a", a=1))
                                  for c in range(FC)]
                        gb = ("ln1_g", "ln1_b", "ln2_g", "ln2_b")
                    else:
                        loads = [(w[L]["w"][:, 0:D], a[pre + "W"])]
                        loads += [(w[L]["av"][:, k:k + 1], a[pre + m].rearrange("(p a) -> p a", a=1))
                                  for k, m in enumerate(("a_src", "a_dst"))]
                        gb = ("ln_gamma", "ln_beta")
                    loads += [(w[L]["gb"][:, k, :], a[pre + m].rearrange("(a n) -> a n", a=1).broadcast_to([P, D]))
                              for k, m in enumerate(gb)]
                    for dst, src in loads:
                        act.dma_start(dst, src).then_inc(w_in, 16)
                        n += 16
                act.wait_ge(w_in, n)

            @block.gpsimd
            def _(g):
                g.memset(ones[:], 1.0)
                g.memset(eps_col[:], EPS)
                g.memset(capacity[:], float(CREST * P)).then_inc(const_made, 1)
                g.wait_ge(const_made, 1)
                g.memset(capacity[:, 0:1], float(CMAX * P))
                g.affine_select(out=ident[:], in_=ones[:], compare_op=ALU.is_equal, fill=0.0, base=0,
                                pattern=[[-1, P]], channel_multiplier=1)
                g.affine_select(out=below[:], in_=ones[:], compare_op=ALU.is_gt, fill=0.0, base=0,
                                pattern=[[1, P]], channel_multiplier=-1)
                g.affine_select(out=keep32.rearrange("p (t b) -> p t b", b=NBLK), in_=ones[:, 0:1].broadcast_to([P, RT * NBLK]).rearrange("p (t b) -> p t b", b=NBLK),
                                compare_op=ALU.is_gt, fill=0.0, base=0, pattern=[[0, RT], [1, NBLK]],
                                channel_multiplier=0)
                any_dt = dict(allow_small_or_imprecise_dtypes=True)
                g.iota(lane[:], pattern=[[1, P]], base=0, channel_multiplier=0, **any_dt)
                g.iota(edge_id[:], pattern=[[P, CMAX]], base=0, channel_multiplier=1, **any_dt)
                g.iota(tile_start[:], pattern=[[P, CMAX]], base=0, channel_multiplier=0, **any_dt)
                g.iota(table[:, :, COL_LOC:COL_LOC + 1], pattern=[[0, RT], [0, 1]], base=1, channel_multiplier=1, **any_dt)
                g.iota(table[:, :, COL_ROW:COL_ROW + 1], pattern=[[-1, RT], [0, 1]], base=RT - 1,
                       channel_multiplier=RT, **any_dt).then_inc(const_made, 1)
                g.wait_ge(const_made, 2)
                g.iota(table[0:1, :, COL_ROW:COL_ROW + 1], pattern=[[1, RT], [0, 1]], base=0,
                       channel_multiplier=0, **any_dt).then_inc(const_made, 1)

            @block.vector
            def _(v):
                ch = Chain(v, dv)
                def count(t, slot, times):
                    v.wait_ge(adj_in[slot], 32 * times + 32)
                    if not (isinstance(t, int) and t == 0):
                        v.wait_ge(adj_read, t)
                    ch.link(v.tensor_scalar(nz, adj_rows[:, slot, :], 0, None, ALU.not_equal))
                    v.tensor_reduce(block_sum[:, bass.ds(t, 1), :],
                                    nz.rearrange("p (a k j) -> p a k j", a=1, j=BLK), AX.X, ALU.add).then_inc(adj_read, 1)

                count(0, 0, 0)
                count(1, 1, 0)
                with v.Fori(1, RT // 2) as i:
                    ch.loop(i - 1, 2)
                    count(2 * i, 0, i)
                    count(2 * i + 1, 1, i)
                ch.end(RT // 2 - 1)
                v.wait_ge(adj_read, RT)
                v.wait_ge(const_made, 3)
                ch.link(v.tensor_tensor_scan(cum, keep32, block_sum.rearrange("p t k -> p (t k)"), 0.0, ALU.mult, ALU.add))
                cum3 = cum.rearrange("p (t k) -> p t k", t=RT)
                ch.link(v.tensor_copy(table[:, :, 0:NBLK], cum3))
                v.tensor_copy(deg, cum3[:, :, NBLK - 1]).then_inc(counts, 1)
                v.wait_ge(prefix, 1)
                v.tensor_copy(before, bank[0][:, 0:RT]).then_inc(dv, 1)
                ch.link(v.tensor_copy(total, bank[1][:, 0:RT]))
                ch.n += 1
                v.wait_ge(dv, ch.base + ch.n)
                v.tensor_copy(table[:, :, COL_OFS], before)
                bc = lambda x: x.rearrange("p (t a) -> p t a", a=1).broadcast_to([P, RT, CMAX])
                cc = tile_start[:].rearrange("p (a c) -> p a c", a=1).broadcast_to([P, RT, CMAX])
                ch.link(v.tensor_tensor(row_from[:], bc(before), cc, ALU.subtract))
                v.tensor_tensor(row_to[:], row_from[:], bc(deg), ALU.add)
                ch.link(v.tensor_tensor(over, total, capacity[:], ALU.subtract))
                ch.link(v.tensor_reduce(row_count, over, AX.X, ALU.max))
                ch.link(v.tensor_scalar(fits[:], row_count, 0.0, None, ALU.is_le))

            @block.tensor
            def _(pe):
                pe.wait_ge(counts, 1)
                pe.matmul(bank[0][:, 0:RT], below[:], deg, start=True, stop=True)
                pe.matmul(bank[1][:, 0:RT], ones[:], deg, start=True, stop=True).then_inc(prefix, 1)

        _, _, _, _, _, table, deg = carve((N,), (2, N), (RT, NBLK), (RT * NBLK,), (RT * NBLK,), (RT, TABW), (RT,))
        deg_end = (N + 2 * N + 3 * RT * NBLK + RT * TABW + RT)
        views = carve((deg_end,), (2, EMAX), (EMAX,), (CMAX, TABW), (CMAX,), (CMAX, NBLK), (CMAX, NBLK), (CMAX,),
                      (CMAX,), (2, CMAX), (2, CMAX), (2, CMAX), (2, CMAX, BLK), (CMAX, BLK), (CMAX, BLK), (CMAX, BLK),
                      (CMAX,), (CMAX,), (CMAX * BLK,), (EMAX,), (2, EMAX + P))
        (_, onehot, ge, tab, rank, le, part, blk, base, gidx, rank2, blk_base, ablk, nzb, cumb, leb, inner, col,
         keep64, iota_e, start_row) = views
        gidx, ablk = gidx.bitcast(I32), ablk.bitcast(I32)
        adj_blocks = a["adj"].rearrange("n (k j) -> (n k) j", j=BLK)
        with nc.Block() as block:
            oh_made, tab_ready, tab_read, gidx_ready = sem("oh_made"), sem("tab_ready"), sem("tab_read"), sem("gidx_ready")
            blk_in = [sem("blk_in0"), sem("blk_in1")]
            oh_kept = sem("oh_kept")
            blk_read, dv, k64_made = sem("blk_read"), sem("dv1"), sem("k64_made")
            start_made, start_clear = sem("start_made"), sem("start_clear")
            end_made, start_ready, start_out = sem("end_made"), sem("start_ready"), [sem("start_out0"), sem("start_out1")]

            @block.scalar
            def _(act):
                def step(t, slot, half):
                    act.wait_ge(oh_made, t + 1)
                    act.copy(spread_bits[:, bass.ds(t, 1), :, :].rearrange("p a c n -> p (a c n)"), onehot[:, slot, :]
                             ).then_inc(oh_kept, 1)
                    act.wait_ge(start_ready, t + 1)
                    act.wait_ge(start_clear, 1)
                    if not (isinstance(t, int) and t < 2):
                        act.wait_ge(start_out[slot], 16 * half)
                    for k in range(3):
                        lo, hi = k * 512, min((k + 1) * 512, EMAX)
                        ins = act.activation(start_row[0:1, slot, lo:hi], bank[1 + k][0:1, 0:hi - lo], ACT.Copy, scale=-BIG)
                    ins.then_inc(start_made, 1)

                step(0, 0, 0)
                step(1, 1, 0)
                with act.Fori(1, RT // 2) as i:
                    for slot in range(2):
                        step(2 * i + slot, slot, i)

            @block.gpsimd
            def _(g):
                g.affine_select(out=keep64.rearrange("p (t b) -> p t b", b=BLK), in_=ones[:, 0:1].broadcast_to([P, CMAX * BLK]).rearrange("p (t b) -> p t b", b=BLK),
                                compare_op=ALU.is_gt, fill=0.0, base=0, pattern=[[0, CMAX], [1, BLK]],
                                channel_multiplier=0)
                g.iota(iota_e, pattern=[[1, EMAX]], base=0, channel_multiplier=0,
                       allow_small_or_imprecise_dtypes=True).then_inc(k64_made, 1)
                with g.Fori(0, RT // 2) as i:
                    for slot in range(2):
                        hold(g, gidx_ready, 2 * i + slot + 1)
                        for c in range(CMAX):
                            g.indirect_dma_start(out=ablk[:, slot, c, :], out_offset=None, in_=adj_blocks,
                                                 in_offset=bass.IndirectOffsetOnAxis(ap=gidx[:, slot, c:c + 1], axis=0)
                                                 ).then_inc(blk_in[slot], 16)

            @block.tensor
            def _(pe):
                def step(t, slot):
                    pe.wait_ge(oh_made, t + 1)
                    if not (isinstance(t, int) and t < 2):
                        pe.wait_ge(tab_read, t - 1)
                    for c in range(CMAX):
                        mm = pe.matmul(bank[4 * slot][:, c * TABW:(c + 1) * TABW], onehot[:, slot, c * P:(c + 1) * P],
                                       table[:, bass.ds(t, 1), :].rearrange("p a n -> p (a n)"), start=True, stop=True)
                    mm.then_inc(tab_ready, 1)
                    pe.wait_ge(end_made, t + 1)
                    if not (isinstance(t, int) and t == 0):
                        pe.wait_ge(start_made, t)
                    for k in range(3):
                        lo, hi = k * 512, min((k + 1) * 512, EMAX)
                        mm = pe.matmul(bank[1 + k][0:1, 0:hi - lo], ones[:, 0:1], nz[:, lo:hi], start=True, stop=True)
                    mm.then_inc(start_ready, 1)

                step(0, 0)
                step(1, 1)
                with pe.Fori(1, RT // 2) as i:
                    for slot in range(2):
                        step(2 * i + slot, slot)

            @block.sync
            def _(sp):
                with sp.Fori(0, RT // 2) as i:
                    for slot in range(2):
                        sp.wait_ge(start_made, 2 * i + slot + 1)
                        sp.dma_start(starts[bass.ds(2 * i + slot, 1), :], start_row[0:1, slot, :]).then_inc(start_out[slot], 16)
                for slot in range(2):
                    sp.wait_ge(start_out[slot], 16 * (RT // 2))

            @block.vector
            def _(v):
                ch = Chain(v, dv)
                v.wait_ge(k64_made, 1)
                v.memset(start_row[0:1, :, :], -BIG).then_inc(start_clear, 1)

                def one_hot(t, slot):
                    row = lambda x: x[:, bass.ds(t, 1), 0]
                    if not (isinstance(t, int) and t < 2):
                        v.wait_ge(tab_ready, t - 1)
                        v.wait_ge(oh_kept, t - 1)
                    if not (isinstance(t, int) and t == 0):
                        v.wait_ge(oh_made, t)
                    ch.link(v.tensor_scalar(ge, iota_e, row(row_from), None, ALU.is_ge))
                    v.scalar_tensor_tensor(onehot[:, slot, :], iota_e, row(row_to), ge, ALU.is_lt, ALU.mult).then_inc(oh_made, 1)
                    if not (isinstance(t, int) and t == 0):
                        v.wait_ge(start_ready, t)
                    v.tensor_scalar(nz[:, 0:EMAX], iota_e, row(row_to), None, ALU.is_equal).then_inc(end_made, 1)

                def find_block(t, slot):
                    v.wait_ge(tab_ready, t + 1)
                    v.tensor_copy(tab, bank[4 * slot][:, 0:CMAX * TABW].rearrange("p (c n) -> p c n", c=CMAX)).then_inc(tab_read, 1)
                    v.wait_ge(tab_read, t + 1)
                    ch.link(v.tensor_tensor(rank, edge_id[:], tab[:, :, COL_OFS], ALU.subtract))
                    over32 = lambda x: x.rearrange("p (c a) -> p c a", a=1).broadcast_to([P, CMAX, NBLK])
                    ch.link(v.tensor_tensor(le, tab[:, :, 0:NBLK], over32(rank), ALU.is_le))
                    ch.link(v.tensor_tensor(part, tab[:, :, 0:NBLK], le, ALU.mult))
                    ch.link(v.tensor_reduce(base, part, AX.X, ALU.max))
                    ch.link(v.tensor_reduce(blk, le, AX.X, ALU.add))
                    v.tensor_tensor(rank2[:, slot, :], rank, base, ALU.subtract)
                    v.tensor_scalar(local_row[:, bass.ds(t, 1), :], tab[:, :, COL_LOC].rearrange("p (a c) -> p a c", a=1), -1.0, None, ALU.add)
                    ch.link(v.tensor_scalar(blk, blk, float(NBLK - 1), None, ALU.min))
                    v.tensor_scalar(blk_base[:, slot, :], blk, float(BLK), None, ALU.mult)
                    v.scalar_tensor_tensor(gidx[:, slot, :], tab[:, :, COL_ROW], float(NBLK), blk, ALU.mult, ALU.add
                                           ).then_inc(gidx_ready, 1)
                    v.wait_ge(gidx_ready, t + 1)
                    over = [P, CMAX, P]
                    v.tensor_tensor(select_bits[:, bass.ds(t, 1), :, :].rearrange("p a c r -> p (a c) r"),
                                    lane[:].rearrange("p (a r) -> p a r", a=1).broadcast_to(over),
                                    local_row[:, bass.ds(t, 1), :].rearrange("p a (c n) -> p (a c) n", n=1).broadcast_to(over),
                                    ALU.is_equal)

                def find_column(t, slot, half):
                    v.wait_ge(blk_in[slot], 16 * CMAX * (half + 1))
                    ch.link(v.tensor_scalar(nzb, ablk[:, slot], 0, None, ALU.not_equal))
                    flat = lambda x: x.rearrange("p c j -> p (c j)")
                    ch.link(v.tensor_tensor_scan(flat(cumb), keep64, flat(nzb), 0.0, ALU.mult, ALU.add))
                    over64 = lambda x: x.rearrange("p (c a) -> p c a", a=1).broadcast_to([P, CMAX, BLK])
                    ch.link(v.tensor_tensor(leb, cumb, over64(rank2[:, slot, :]), ALU.is_le))
                    ch.link(v.tensor_reduce(inner, leb, AX.X, ALU.add))
                    ch.link(v.tensor_tensor(col, inner, blk_base[:, slot, :], ALU.add))
                    v.tensor_scalar(neighbour[:, bass.ds(t, 1), :], col.rearrange("p (a c) -> p a c", a=1), float(N - 1), None, ALU.min)

                one_hot(0, 0)
                one_hot(1, 1)
                find_block(0, 0)
                with v.Fori(0, RT // 2 - 1) as i:
                    ch.loop(i, 2 * (1 + 6 + 5))
                    for slot in range(2):
                        one_hot(2 * i + 2 + slot, slot)
                        find_block(2 * i + 1 + slot, 1 - slot)
                        find_column(2 * i + slot, slot, i)
                ch.end(RT // 2 - 1)
                find_block(RT - 1, 1)
                find_column(RT - 2, 0, RT // 2 - 1)
                find_column(RT - 1, 1, RT // 2 - 1)

        def kept_rows(t):
            return [(xs[bass.ds(t, 1)].rearrange("r q n -> (r q) n"), 0, P)]

        def given_rows(t):
            return [(src.rearrange("r q b d -> (r q) b d"), lo, hi) for src, lo, hi in zip(tile_rows(x_by_row, t), (0, 1), (1, P))]

        def result_rows(t):
            return [(dst.rearrange("r q b d -> (r q) b d"), lo, hi) for dst, lo, hi in zip(tile_rows(out_by_row, t), (0, 1), (1, P))]

        for L in range(layers):
            x_rows = given_rows if L == 0 else kept_rows
            y_rows = result_rows if L == layers - 1 else kept_rows
            sems.renew()
            project(nc, sem, carve, bank, pair, w[L], KINDS[L], L, ident, tile_rows, x_rows, qq, kk_by_row, vv_by_row, si, sj_by_row)
            sems.renew()
            attend(nc, sem, carve, bank, pair, KINDS[L], L, neighbour, spread_bits, select_bits, ident,
                   starts, qq, kk, vv, si, sj, ao, fits, ones, adj_by_row, tile_rows)
            sems.renew()
            (post_gat if KINDS[L] == "gat" else post_tf)(nc, sem, carve, bank, w[L], L, ident, eps_col, x_rows, ao, y_rows)
        sems.renew()
        return nc


def project(nc, sem, carve, bank, pair, w, kind, L, ident, tile_rows, x_rows, qq, kk_by_row, vv_by_row, si, sj_by_row):
    tf = kind == "tf"
    x_tile, x_turned, stage, small, w_turned = carve((2, BD), (2, 4 * D), (2, 3, BD), (2, 2 * B), (D,))
    x_in = [sem(f"x_in{L}{s}") for s in range(2)]
    turned, x_copied, product = sem(f"turned{L}"), sem(f"x_copied{L}"), sem(f"product{L}")
    evac_v, evac_a = sem(f"evac_v{L}"), sem(f"evac_a{L}")
    out_sem = [sem(f"staged_out{L}{s}") for s in range(2)]
    wt, wt_copied, wa = sem(f"wt{L}"), sem(f"wt_copied{L}"), sem(f"wa{L}")
    stores = 5 if tf else 5
    GROUPS = 2 * RT

    with nc.Block() as block:
        @block.sync
        def _(sp):
            def load(t, slot):
                for src, lo, hi in x_rows(t):
                    dst = x_tile[lo:hi, slot, :]
                    sp.dma_start(dst if len(src.shape) == 2 else dst.rearrange("p (b d) -> p b d", b=B), src).then_inc(x_in[slot], 16)

            def store(t, slot):
                sp.wait_ge(evac_v, (4 if tf else 1) * (t + 1))
                sp.wait_ge(evac_a, (4 if tf else 1) * (t + 1))
                if tf:
                    sp.dma_start(qq[bass.ds(t, 1)].rearrange("r q n -> q r n"), stage[:, slot, 0:1, :]).then_inc(out_sem[slot], 16)
                    pieces = [(kk_by_row, stage[:, slot, 1, :]), (vv_by_row, stage[:, slot, 2, :])]
                else:
                    sp.dma_start(si[bass.ds(t, 1)].rearrange("r q n -> q r n"), small[:, slot:slot + 1, 0:B]).then_inc(out_sem[slot], 16)
                    pieces = [(vv_by_row, stage[:, slot, 2, :]), (sj_by_row, small[:, slot, B:2 * B])]
                for view, src in pieces:
                    for dst, lo, hi in zip(tile_rows(view, t), (0, 1), (1, P)):
                        sp.dma_start(dst.rearrange("r q n -> (r q) n"), src[lo:hi]).then_inc(out_sem[slot], 16)

            load(0, 0)
            load(1, 1)
            with sp.Fori(0, RT // 2 - 1) as i:
                for slot in range(2):
                    sp.wait_ge(turned, 2 * (2 * i + slot) + 2)
                    load(2 * i + slot + 2, slot)
                    store(2 * i + slot, slot)
            store(RT - 2, 0)
            store(RT - 1, 1)
            for slot in range(2):
                sp.wait_ge(out_sem[slot], 16 * stores * (RT // 2))

        @block.tensor
        def _(pe):
            if not tf:
                pe.transpose(bank[6][:, 0:D], w["w"][:, 0:D], ident[:]).then_inc(wt, 1)
                pe.wait_ge(wt_copied, 1)
                pe.matmul(bank[7][:, 0:2], w_turned, w["av"][:], start=True, stop=True).then_inc(wt, 1)
                pe.wait_ge(wa, 1)

            def turn(n, k, turn_no):
                slot, half = (k // 2) % 2, k % 2
                if k % 2 == 0:
                    pe.wait_ge(x_in[slot], 16 * len(x_rows(0)) * (turn_no + 1))
                if not (isinstance(n, int) and n < 2):
                    pe.wait_ge(x_copied, n - 1)
                for b in range(4):
                    at = (4 * half + b) * D
                    tr = pe.transpose(bank[half][:, b * P:(b + 1) * P], x_tile[:, slot, at:at + D], ident[:])
                tr.then_inc(turned, 1)

            def multiply(n, k):
                half = k % 2
                pe.wait_ge(x_copied, n + 1)
                for b in range(4):
                    lhs = x_turned[:, half, b * P:(b + 1) * P]
                    if tf:
                        if not (isinstance(n, int) and n == 0):
                            pe.wait_ge(evac_a if b % 2 else evac_v, 2 * n - 1 + b // 2)
                        pe.matmul(bank[2 + b][:, 0:3 * D], lhs, w["qkv"][:], start=True, stop=True).then_inc(product, 1)
                    else:
                        if b == 0 and not (isinstance(n, int) and n < 2):
                            pe.wait_ge(evac_a if half else evac_v, n // 2 if isinstance(n, int) else n_half[0])
                        at = 512 * (b // 2) + (D + 2) * (b % 2)
                        mm = pe.matmul(pair[1 + half][:, at:at + D + 2], lhs, w["w"][:], start=True, stop=True)
                if not tf:
                    mm.then_inc(product, 1)

            n_half = [0]
            turn(0, 0, 0)
            multiply_now = []
            for k in range(4):
                turn(k + 1, k + 1 if k < 3 else 0, 0 if k < 3 else 1)
                multiply(k, k)
            with pe.Fori(1, RT // 2 - 1) as i:
                for k in range(4):
                    n_half[0] = 2 * i + k // 2
                    turn(4 * i + k + 1, (k + 1) % 4, i if k < 3 else i + 1)
                    multiply(4 * i + k, k)
            for k in range(4):
                n = GROUPS - 4 + k
                if k < 3:
                    turn(n + 1, k + 1, RT // 2 - 1)
                multiply(n, k)

        def products(half):
            return pair[1 + half][:].rearrange("p (k n) -> p k n", k=2)[:, :, 0:2 * (D + 2)].rearrange("p k (j m) -> p k j m", j=2)

        def evacuate(eng, copy, n, k, done, uses, first):
            slot, half = (k // 2) % 2, k % 2
            mine = 1 if eng is nc.scalar else 0
            if tf:
                for b in (mine, mine + 2):
                    eng.wait_ge(product, 4 * n + b + 1)
                    if not first and half == 0 and b < 2:
                        eng.wait_ge(out_sem[slot], 16 * stores * uses)
                    at = (4 * half + b) * D
                    copy(stage[:, slot, :, at:at + D], bank[2 + b][:, 0:3 * D].rearrange("p (m d) -> p m d", m=3)).then_inc(done, 1)
            elif half == mine:
                eng.wait_ge(product, n + 1)
                if not first:
                    eng.wait_ge(out_sem[slot], 16 * stores * uses)
                for m in range(2):
                    copy(small[:, slot, m * B + 4 * half:m * B + 4 * half + 4].rearrange("p (k j) -> p k j", k=2),
                         products(half)[:, :, :, D + m])
                copy(stage[:, slot, 2, half * 4 * D:(half + 1) * 4 * D].rearrange("p (k j d) -> p k j d", k=2, j=2),
                     products(half)[:, :, :, 0:D]).then_inc(done, 1)

        @block.scalar
        def _(act):
            if not tf:
                act.wait_ge(wt, 1)
                act.copy(w_turned, bank[6][:, 0:D]).then_inc(wt_copied, 1)
                act.wait_ge(wt, 2)
                act.copy(w["w"][:, D:D + 2], bank[7][:, 0:2]).then_inc(wa, 1)

            def copy_turned(n, k):
                act.wait_ge(turned, n + 1)
                if not (isinstance(n, int) and n < 2):
                    act.wait_ge(product, (4 if tf else 1) * (n - 1))
                act.copy(x_turned[:, k % 2, :], bank[k % 2]).then_inc(x_copied, 1)

            copy_turned(0, 0)
            for k in range(4):
                copy_turned(k + 1, k + 1)
                evacuate(act, act.copy, k, k, evac_a, 0, True)
            with act.Fori(1, RT // 2 - 1) as i:
                for k in range(4):
                    copy_turned(4 * i + k + 1, k + 1)
                    evacuate(act, act.copy, 4 * i + k, k, evac_a, i, False)
            for k in range(4):
                n = GROUPS - 4 + k
                if k < 3:
                    copy_turned(n + 1, k + 1)
                evacuate(act, act.copy, n, k, evac_a, RT // 2 - 1, False)

        @block.vector
        def _(v):
            def turn(n, k, t, uses, first):
                evacuate(v, v.tensor_copy, n, k, evac_v, uses, first)

            for k in range(4):
                turn(k, k, k // 2, 0, True)
            with v.Fori(1, RT // 2) as i:
                for k in range(4):
                    turn(4 * i + k, k, 2 * i + k // 2, i, False)


def attend(nc, sem, carve, bank, pair, kind, L, neighbour, spread_bits, select_bits, ident,
           starts, qq, kk, vv, si, sj, ao, fits, ones, adj_by_row, tile_rows):
    by_edge = attend_by_edge(nc, sem, carve, bank, pair, kind, L, neighbour, spread_bits, select_bits, ident,
                             starts, qq, kk, vv, si, sj, ao)
    dense = attend_dense(nc, sem, carve, bank, pair, kind, L, ident, qq, kk, vv, si, sj, ao, ones, adj_by_row, tile_rows)

    def either(eng, edge_program, dense_program):
        fit = eng.value_load(fits[0:1, 0:1], min_val=0, max_val=1)
        with eng.If(fit == 1):
            edge_program(eng)
        with eng.Else():
            dense_program(eng)

    with nc.Block() as block:
        @block.gpsimd
        def _(g):
            either(g, by_edge[0], dense[0])

        @block.sync
        def _(sp):
            either(sp, by_edge[1], dense[1])

        @block.tensor
        def _(pe):
            either(pe, by_edge[2], dense[2])

        @block.scalar
        def _(act):
            either(act, by_edge[3], dense[3])

        @block.vector
        def _(v):
            either(v, by_edge[4], dense[4])


def attend_dense(nc, sem, carve, bank, pair, kind, L, ident, qq, kk, vv, si, sj, ao, ones, adj_by_row, tile_rows):
    tf = kind == "tf"
    H = HEADS if tf else 1
    W = D // H
    SCALE = float(HD) ** -0.5 if tf else 1.0
    KT = N // P
    (keys, values, keys_turned, masked, probs, probs_turned, bias, adj_rows, q_tile, q_heads, o_stage, head_mask, top,
     shift, den, q_pair, k_pair) = carve((KT, D), (KT, D), (N,), (N,), (N,), (N,), (N,), (N,), (D,), (HEADS, P), (D,),
                                         (HEADS,), (1,), (1,), (1,), (P,), (N,))
    adj_rows = adj_rows.bitcast(I32)
    new = lambda name: sem(f"{name}{L}")
    made, adj_in, kv_in, bias_made = new("d_made"), new("d_adj_in"), new("d_kv_in"), new("d_bias")
    k_tr, k_copied, q_tr, q_masked = new("d_k_tr"), new("d_k_copied"), new("d_q_tr"), new("d_q_masked")
    scored, read, biased, topped, shifted = new("d_scored"), new("d_read"), new("d_biased"), new("d_topped"), new("d_shifted")
    raised, p_tr, p_copied, summed = new("d_exp"), new("d_p_tr"), new("d_p_copied"), new("d_summed")
    den_step, o_made, o_out = new("d_den"), new("d_o"), new("d_o_out")
    loads = 3 if tf else 3

    def tiles(eng, per_tile, per_batch):
        with eng.Fori(0, RT) as t:
            per_tile(t)
            with eng.Fori(0, B) as b:
                per_batch(t, b, B * t + b)

    nothing = lambda t: None

    def gpsimd(g):
        g.affine_select(out=head_mask, in_=ones[:, 0:HEADS], compare_op=ALU.is_ge, fill=0.0, base=0,
                        pattern=[[-HD, HEADS]], channel_multiplier=1).then_inc(made, 1)
        g.wait_ge(made, 1)
        g.affine_select(out=head_mask, in_=head_mask, compare_op=ALU.is_ge, fill=0.0, base=HD - 1,
                        pattern=[[HD, HEADS]], channel_multiplier=-1)
        g.memset(q_pair[0:2, :], 1.0)
        g.memset(k_pair[0:2, :], 1.0).then_inc(made, 1)
        g.sem_inc(o_made, 1)
        g.sem_inc(p_copied, 1)
        g.sem_inc(raised, 1)
        g.sem_inc(o_out, 16)

    def sync(sp):
        sp.wait_ge(made, 2)

        def per_tile(t):
            sp.wait_ge(o_made, H * B * t + 1)
            for src, lo, hi in zip(tile_rows(adj_by_row, t), (0, 1), (1, P)):
                sp.dma_start(adj_rows[lo:hi, :], src.rearrange("r q n -> (r q) n")).then_inc(adj_in, 16)

        def per_batch(t, b, m):
            sp.wait_ge(o_made, H * m + 1)
            cols = bass.ds(b * D, D)
            by_tile = lambda x: x.rearrange("(k p) n -> p k n", p=P)
            sp.dma_start(values, by_tile(vv)[:, :, cols]).then_inc(kv_in, 16)
            if tf:
                sp.dma_start(keys, by_tile(kk)[:, :, cols]).then_inc(kv_in, 16)
                sp.dma_start(q_tile, qq[bass.ds(t, 1), :, cols].rearrange("r q n -> (r q) n")).then_inc(kv_in, 16)
            else:
                sp.dma_start(k_pair[1:2, :], sj.rearrange("n b -> b n")[bass.ds(b, 1), :], allow_slow_non_contiguous=True
                             ).then_inc(kv_in, 16)
                sp.dma_start(q_pair[0:1, :], si.rearrange("r q b -> r b q")[bass.ds(t, 1), bass.ds(b, 1), :].rearrange("r b q -> (r b) q"),
                             allow_slow_non_contiguous=True).then_inc(kv_in, 16)
            sp.wait_ge(o_made, H * (m + 1) + 1)
            sp.dma_start(ao[bass.ds(t, 1), :, cols].rearrange("r q n -> (r q) n"), o_stage).then_inc(o_out, 16)
        tiles(sp, per_tile, per_batch)
        sp.wait_ge(o_out, 16 * RT * B + 16)

    def tensor(pe):
        def per_batch(t, b, m):
            hold(pe, kv_in, 16 * loads * (m + 1))
            if tf:
                hold(pe, p_copied, 2 * H * m + 1)
                for k in range(KT):
                    tr = pe.transpose(bank[k // 4][:, (k % 4) * P:(k % 4 + 1) * P], keys[:, k, :], ident[:])
                tr.then_inc(k_tr, 1)
                pe.transpose(bank[5][:, 0:P], q_tile, ident[:]).then_inc(q_tr, 1)
            for h in range(H):
                n = H * m + h
                if tf:
                    pe.wait_ge(k_copied, 2 * m + 2)
                    pe.wait_ge(q_masked, m + 1)
                hold(pe, p_copied, 2 * n + 1)
                for k in range(4):
                    if tf:
                        mm = pe.matmul(bank[k], q_heads[:, h, :], keys_turned[:, k * 512:(k + 1) * 512], start=True, stop=True)
                    else:
                        mm = pe.matmul(bank[k], q_pair[0:2, :], k_pair[0:2, k * 512:(k + 1) * 512], start=True, stop=True)
                mm.then_inc(scored, 1)
                hold(pe, raised, n + 2)
                for k in range(KT):
                    tr = pe.transpose(bank[k // 4][:, (k % 4) * P:(k % 4 + 1) * P], probs[:, k * P:(k + 1) * P], ident[:])
                tr.then_inc(p_tr, 1)
                pe.wait_ge(o_made, n + 1)
                hold(pe, p_copied, 2 * n + 3)
                for k in range(KT):
                    mm = pe.matmul(bank[4][:, 0:W], probs_turned[:, k * P:(k + 1) * P], values[:, k, h * W:(h + 1) * W],
                                   start=(k == 0), stop=(k == KT - 1))
                mm.then_inc(summed, 1)
        tiles(pe, nothing, per_batch)

    def scalar(act):
        def per_batch(t, b, m):
            if tf:
                act.wait_ge(k_tr, m + 1)
                for k in range(2):
                    act.copy(keys_turned[:, k * 1024:(k + 1) * 1024], pair[k][:]).then_inc(k_copied, 1)
            for h in range(H):
                n = H * m + h
                if not tf:
                    act.wait_ge(scored, n + 1)
                    for k in range(2):
                        act.copy(masked[:, k * 1024:(k + 1) * 1024], pair[k][:]).then_inc(read, 1)
                act.wait_ge(shifted, n + 1)
                act.wait_ge(o_made, n + 1)
                act.activation(probs, masked, ACT.Exp, bias=shift, scale=SCALE, accum_out=den).then_inc(raised, 1)
                act.wait_ge(p_tr, n + 1)
                for k in range(2):
                    act.copy(probs_turned[:, k * 1024:(k + 1) * 1024], pair[k][:]).then_inc(p_copied, 1)
        tiles(act, nothing, per_batch)

    def vector(v):
        v.wait_ge(made, 2)

        def per_tile(t):
            v.wait_ge(adj_in, 32 * t + 32)
            v.wait_ge(o_made, H * B * t + 1)
            v.tensor_scalar(bias, adj_rows, 0, -BIG, ALU.is_equal, ALU.mult).then_inc(bias_made, 1)
            hold(v, bias_made, t + 1)

        def per_batch(t, b, m):
            if tf:
                v.wait_ge(q_tr, m + 1)
                v.tensor_tensor(q_heads, bank[5][:, 0:P].rearrange("p (a q) -> p a q", a=1).broadcast_to([P, HEADS, P]),
                                head_mask.rearrange("p (h a) -> p h a", a=1).broadcast_to([P, HEADS, P]), ALU.mult
                                ).then_inc(q_masked, 1)
            for h in range(H):
                n = H * m + h
                if tf:
                    v.wait_ge(scored, n + 1)
                    v.wait_ge(raised, n + 1)
                    for k in range(2):
                        cols = slice(k * 1024, (k + 1) * 1024)
                        v.tensor_tensor(masked[:, cols], pair[k][:], bias[:, cols], ALU.add).then_inc(biased, 1)
                    v.wait_ge(biased, 2 * n + 2)
                else:
                    v.wait_ge(read, 2 * n + 2)
                    v.scalar_tensor_tensor(masked, masked, SLOPE, masked, ALU.mult, ALU.max).then_inc(biased, 1)
                    v.wait_ge(biased, 2 * n + 1)
                    v.tensor_tensor(masked, masked, bias, ALU.add).then_inc(biased, 1)
                    v.wait_ge(biased, 2 * n + 2)
                v.tensor_reduce(top, masked, AX.X, ALU.max).then_inc(topped, 1)
                v.wait_ge(topped, n + 1)
                v.tensor_scalar(shift, top, -BIG / 2, -SCALE, ALU.max, ALU.mult).then_inc(shifted, 1)
                v.wait_ge(raised, n + 2)
                v.tensor_scalar(den, den, TINY, None, ALU.max).then_inc(den_step, 1)
                v.wait_ge(den_step, 2 * n + 1)
                v.reciprocal(den, den).then_inc(den_step, 1)
                v.wait_ge(den_step, 2 * n + 2)
                v.wait_ge(summed, n + 1)
                if h == 0:
                    v.wait_ge(o_out, 16 * m + 16)
                v.tensor_scalar(o_stage[:, h * W:(h + 1) * W], bank[4][:, 0:W], den, None, ALU.mult).then_inc(o_made, 1)
        tiles(v, per_tile, per_batch)

    return gpsimd, sync, tensor, scalar, vector


def attend_by_edge(nc, sem, carve, bank, pair, kind, L, neighbour, spread_bits, select_bits, ident,
                   starts, qq, kk, vv, si, sj, ao):
    tf = kind == "tf"
    G = B * HEADS if tf else B
    W = BD // G
    SCALE = float(HD) ** -0.5 if tf else 1.0
    K_RING, V_RING = (5, 5) if tf else (0, 10)
    WEIGHTED = 5
    LATE = 2 if tf else 3
    CHUNK = CMAX - CREST // 2
    (q_tile, k_ring, v_ring, prod, weighted_v, o_stage, spread, select, score, row_start, turned, row_max, prob, den,
     idx_k, idx_v, sj_edge, raw) = carve(
        (2, BD), (max(K_RING, 1), BD if tf else 1), (V_RING, BD), (2, BD if tf else 1), (WEIGHTED, BD), (2, BD), (2, CHUNK, P), (2, CHUNK, P), (CMAX, G),
        (EMAX + P,), (EMAX,), (EMAX,), (2, CMAX, G), (G,), (2, CMAX), (2, CMAX), (2, CMAX, 1 if tf else G), (CMAX, B))
    idx_k, idx_v = idx_k.bitcast(I32), idx_v.bitcast(I32)
    new = lambda name: sem(f"{name}{L}")
    q_in = [new("q_in0_"), new("q_in1_")]
    k_landed = [new(f"k_landed{r}_") for r in range(K_RING)]
    v_landed = [new(f"v_landed{r}_") for r in range(V_RING)]
    sj_in = [new("sj_in0_"), new("sj_in1_")]
    start_in, idx_k_made, idx_v_made = new("start_in"), new("idx_k_made"), new("idx_v_made")
    spread_made, spread_q, prod_made, score_made = new("spread_made"), new("spread_q"), new("prod_made"), new("score_made")
    raw_made = new("raw_made")
    tp_full, tp_read = new("tp_full"), new("tp_read")
    scan_fwd, scan_back, shifted, prob_ready = new("scan_fwd"), new("scan_back"), new("shifted"), new("prob_ready")
    select_made, weighted, summed = new("select_made"), new("weighted"), new("summed")
    den_step, o_ready, o_out = new("den_step"), new("o_ready"), [new("o_out0_"), new("o_out1_")]
    zero = lambda t: isinstance(t, int) and t == 0
    g0 = first_edge_tile
    GROUP_S, GROUP_P = 4, 8

    sums_at = lambda par: pair[2] if tf else pair[1 + par]
    den_at = lambda par: bank[7][:, 0:G] if tf else bank[(1, 7)[par]][:, 0:G]

    def has(t, lag=0):
        return not isinstance(t, int) or 0 <= t - lag < RT

    def cut(t):
        return CHUNK if zero(t) else CREST // 2

    def slot_of(t, c, ring):
        if zero(t):
            return c % ring, c // ring
        return (CMAX + c) % ring, (CREST // ring) * (t - 1) + (CMAX + c) // ring

    def steps(eng, step):
        for t in range(6):
            step(t, t % 2, t // 2)
        with eng.Fori(3, RT // 2 - 1) as i:
            step(2 * i, 0, i)
            step(2 * i + 1, 1, i)
        for t in range(RT - 2, RT + LATE):
            step(t, t % 2, t // 2)

    def turn_of_scores(t, k):
        return 5 * t + 1 + k

    def turn_of_probs(t, m):
        return 5 * t + 4 + m

    def width(t):
        return max(edge_tiles(t) if has(t) else 0, edge_tiles(t - 2) if has(t, 2) else 0)

    def gpsimd(g):
        def step(t, par, half):
            where = lambda idx, c: bass.IndirectOffsetOnAxis(ap=idx[:, par, c:c + 1], axis=0)
            if has(t):
                if has(t, 2):
                    if tf:
                        hold(g, prod_made, g0(t - 1))
                    else:
                        hold(g, raw_made, t - 1)
                g.tensor_copy(idx_k[:, par:par + 1, :], neighbour[:, bass.ds(t, 1), :]).then_inc(idx_k_made, 1)
                hold(g, idx_k_made, t + 1)
            if has(t, 2):
                if has(t, 4):
                    hold(g, weighted, g0(t - 3))
                g.tensor_copy(idx_v[:, par:par + 1, :], neighbour[:, bass.ds(t - 2, 1), :]).then_inc(idx_v_made, 1)
                hold(g, idx_v_made, t - 1)
            for c in range(width(t)):
                if has(t) and c < edge_tiles(t):
                    if tf:
                        slot, _ = slot_of(t, c, K_RING)
                        if not (zero(t) and c < K_RING):
                            hold(g, prod_made, g0(t) + c - K_RING + 1)
                        g.indirect_dma_start(out=k_ring[:, slot, :], out_offset=None, in_=kk, in_offset=where(idx_k, c)
                                             ).then_inc(k_landed[slot], 16)
                    else:
                        g.indirect_dma_start(out=sj_edge[:, par, c, :], out_offset=None, in_=sj, in_offset=where(idx_k, c)
                                             ).then_inc(sj_in[par], 16)
                if has(t, 2) and c < edge_tiles(t - 2):
                    u = t - 2
                    slot, _ = slot_of(u, c, V_RING)
                    if not (zero(u) and c < V_RING):
                        hold(g, weighted, g0(u) + c - V_RING + 1)
                    g.indirect_dma_start(out=v_ring[:, slot, :], out_offset=None, in_=vv, in_offset=where(idx_v, c)
                                         ).then_inc(v_landed[slot], 16)
        steps(g, step)

    def sync(sp):
        def load_q(t, par):
            dst, src = (q_tile[:, par, :], qq) if tf else (q_tile[:, par, 0:B], si)
            sp.dma_start(dst, src[bass.ds(t, 1)].rearrange("r q n -> (r q) n")).then_inc(q_in[par], 16)

        def store(t, par):
            sp.wait_ge(o_ready, t + 1)
            sp.dma_start(ao[bass.ds(t, 1)].rearrange("r q n -> (r q) n"), o_stage[:, par, :]).then_inc(o_out[par], 16)

        def step(t, par, half):
            if has(t, -1):
                if has(t, 1):
                    sp.wait_ge(spread_q, g0(t))
                load_q(t + 1, 1 - par)
            if has(t, LATE + 1):
                store(t - LATE - 1, (par + LATE + 1) % 2)
            if has(t):
                if has(t, 1):
                    sp.wait_ge(scan_back, t)
                sp.dma_start(row_start[0:G, :], starts[bass.ds(t, 1), :].broadcast_to([G, EMAX + P])).then_inc(start_in, 16)

        load_q(0, 0)
        steps(sp, step)
        store(RT - 1, 1)
        for s in range(2):
            sp.wait_ge(o_out[s], 16 * (RT // 2))

    def tensor(pe):
        def turn_scores(t, k):
            lo, hi = k * GROUP_S, min((k + 1) * GROUP_S, edge_tiles(t))
            pe.wait_ge(score_made, g0(t) + hi if tf else t + 1)
            if not (zero(t) and k == 0):
                hold(pe, tp_read, turn_of_scores(t, k) - 1)
            for c in range(lo, hi):
                tr = pe.transpose(bank[6][0:G, (c - lo) * P:(c - lo + 1) * P], score[:, c, :], ident[:])
            tr.then_inc(tp_full, 1)

        def turn_probs(t, m):
            lo, hi = m * GROUP_P, min((m + 1) * GROUP_P, edge_tiles(t))
            pe.wait_ge(prob_ready, t + 1)
            hold(pe, tp_read, turn_of_probs(t, m) - 1)
            for c in range(lo, hi):
                tr = pe.transpose(bank[6][:, (c - lo) * G:(c - lo + 1) * G], turned[0:G, c * P:(c + 1) * P], ident[0:G, 0:G])
            tr.then_inc(tp_full, 1)

        def spread_queries(t, c, par, half):
            h = int(c >= cut(t))
            if c == 0:
                pe.wait_ge(q_in[par], 16 * half + 16)
            if c in (0, cut(t)):
                pe.wait_ge(spread_made, 2 * t + h + 1)
            lhs = spread[:, h, c - h * cut(t), :]
            if tf:
                slot = slot_of(t, c, 2)[0]
                if not (zero(t) and c < 2):
                    pe.wait_ge(prod_made, g0(t) + c - 1)
                for k in range(2):
                    mm = pe.matmul(pair[slot][:, k * 512:(k + 1) * 512], lhs, q_tile[:, par, k * 512:(k + 1) * 512],
                                   start=True, stop=True)
                mm.then_inc(spread_q, 1)
            else:
                if c == 0 and has(t, 1):
                    pe.wait_ge(raw_made, t)
                pe.matmul(bank[0][:, c * B:(c + 1) * B], lhs, q_tile[:, par, 0:B], start=True, stop=True).then_inc(spread_q, 1)

        def sum_values(t, c, par):
            h = int(c >= cut(t))
            if c == 0 and has(t, LATE - 1):
                pe.wait_ge(o_ready, t - LATE + 2)
            if c in (0, cut(t)):
                pe.wait_ge(select_made, 2 * t + h + 1)
            pe.wait_ge(weighted, g0(t) + c + 1)
            slot = slot_of(t, c, WEIGHTED)[0]
            lhs = select[:, h, c - h * cut(t), :]
            ends = dict(start=(c == 0), stop=(c == edge_tiles(t) - 1))
            for k in range(2):
                pe.matmul(sums_at(par)[:, k * 512:(k + 1) * 512], lhs, weighted_v[:, slot, k * 512:(k + 1) * 512], **ends)
            pe.matmul(den_at(par), lhs, prob[:, par, c, :], **ends).then_inc(summed, 1)

        def step(t, par, half):
            ahead = 2 if tf else CMAX
            if has(t):
                for c in range(min(ahead, edge_tiles(t))):
                    spread_queries(t, c, par, half)
            if tf and has(t, 1):
                turn_scores(t - 1, 2)
            for c in range(CMAX):
                if has(t, 2) and c < edge_tiles(t - 2):
                    sum_values(t - 2, c, par)
                if has(t) and c + ahead < edge_tiles(t):
                    spread_queries(t, c + ahead, par, half)
                if has(t, 1) and c in (3, 4):
                    turn_probs(t - 1, c - 3)
                if has(t) and tf and c in (5, 8):
                    turn_scores(t, int(c == 8))
                if has(t) and not tf and c in (6, 7, 8):
                    turn_scores(t, c - 6)
        steps(pe, step)

    def scalar(act):
        def copy_scores(t, k):
            lo, hi = k * GROUP_S, min((k + 1) * GROUP_S, edge_tiles(t))
            act.wait_ge(tp_full, turn_of_scores(t, k))
            act.copy(turned[0:G, lo * P:hi * P], bank[6][0:G, 0:(hi - lo) * P]).then_inc(tp_read, 1)

        def widen(t, h, bits, wide, used, made):
            if not zero(t):
                act.wait_ge(used, g0(t - 1) + (edge_tiles(t - 1) if h else cut(t - 1)))
            lo, hi = (cut(t), edge_tiles(t)) if h else (0, cut(t))
            act.copy(wide[:, h:h + 1, 0:hi - lo, :], bits[:, bass.ds(t, 1), lo:hi, :]).then_inc(made, 1)

        def step(t, par, half):
            if tf and has(t, 1):
                copy_scores(t - 1, 2)
            if has(t):
                widen(t, 1, spread_bits, spread, spread_q, spread_made)
            if has(t, 2):
                widen(t - 2, 1, select_bits, select, summed, select_made)
            if has(t, 1):
                u, s, C = t - 1, 1 - par, edge_tiles(t - 1)
                act.wait_ge(shifted, u + 1)
                act.activation(turned[0:G, 0:C * P], turned[0:G, 0:C * P], ACT.Exp, scale=SCALE).then_inc(prob_ready, 1)
                for m in range(2):
                    lo, hi = m * GROUP_P, min((m + 1) * GROUP_P, C)
                    act.wait_ge(tp_full, turn_of_probs(u, m))
                    if m == 0 and has(u, 2):
                        act.wait_ge(summed, g0(u - 1))
                    act.copy(prob[:, s, lo:hi, :], bank[6][:, 0:(hi - lo) * G].rearrange("p (c g) -> p c g", g=G)).then_inc(tp_read, 1)
            if has(t, -1):
                widen(t + 1, 0, spread_bits, spread, spread_q, spread_made)
            if has(t, 1):
                widen(t - 1, 0, select_bits, select, summed, select_made)
            if has(t):
                for k in range(2 if tf else 3):
                    copy_scores(t, k)

        widen(0, 0, spread_bits, spread, spread_q, spread_made)
        steps(act, step)

    def vector(v):
        def product(t, c):
            slot, (k_slot, used) = slot_of(t, c, 2)[0], slot_of(t, c, K_RING)
            v.wait_ge(k_landed[k_slot], 16 * used + 16)
            v.wait_ge(spread_q, g0(t) + c + 1)
            if not (zero(t) and c < 2):
                v.wait_ge(score_made, g0(t) + c - 1)
            v.tensor_tensor(prod[:, slot, :], pair[slot][:], k_ring[:, k_slot, :], ALU.mult).then_inc(prod_made, 1)

        def score_of(t, c):
            slot = slot_of(t, c, 2)[0]
            v.wait_ge(prod_made, g0(t) + c + 1)
            if has(t, 1) and c in (0, 2 * GROUP_S):
                v.wait_ge(tp_full, turn_of_scores(t - 1, 1 + c // (2 * GROUP_S)))
            v.tensor_reduce(score[:, c, :], prod[:, slot, :].rearrange("p (g w) -> p g w", w=W), AX.X, ALU.add
                            ).then_inc(score_made, 1)

        def scores_gat(t, par, half):
            C = edge_tiles(t)
            v.wait_ge(spread_q, g0(t) + C)
            v.wait_ge(sj_in[par], 16 * (CREST * (half + 1) + (CMAX - CREST if par == 0 else 0)))
            if not zero(t):
                v.wait_ge(score_made, t)
                v.wait_ge(tp_full, turn_of_scores(t - 1, 2))
            v.tensor_tensor(raw[:, 0:C, :], bank[0][:, 0:C * B].rearrange("p (c b) -> p c b", b=B),
                            sj_edge[:, par, 0:C, :], ALU.add).then_inc(raw_made, 1)
            v.wait_ge(raw_made, t + 1)
            v.scalar_tensor_tensor(score[:, 0:C, :], raw[:, 0:C, :], SLOPE, raw[:, 0:C, :], ALU.mult, ALU.max
                                   ).then_inc(score_made, 1)

        def shift(t):
            E = edge_tiles(t) * P
            v.wait_ge(tp_read, turn_of_scores(t, 2))
            v.wait_ge(start_in, 16 * t + 16)
            if not zero(t):
                v.wait_ge(shifted, t)
            v.tensor_tensor_scan(row_max[0:G, 0:E], row_start[0:G, 0:E], turned[0:G, 0:E], -BIG, ALU.add, ALU.max
                                 ).then_inc(scan_fwd, 1)
            v.wait_ge(scan_fwd, t + 1)
            back = row_max[0:G, 0:E][:, ::-1]
            v.tensor_tensor_scan(back, row_start[0:G, 1:E + 1][:, ::-1], back, -BIG, ALU.add, ALU.max
                                 ).then_inc(scan_back, 1)
            v.wait_ge(scan_back, t + 1)
            v.tensor_tensor(turned[0:G, 0:E], turned[0:G, 0:E], row_max[0:G, 0:E], ALU.subtract).then_inc(shifted, 1)

        def weigh(t, c, par):
            slot, (v_slot, used) = slot_of(t, c, WEIGHTED)[0], slot_of(t, c, V_RING)
            if c == 0:
                v.wait_ge(tp_read, turn_of_probs(t, 1))
            if not (zero(t) and c < WEIGHTED):
                v.wait_ge(summed, g0(t) + c - WEIGHTED + 1)
            v.wait_ge(v_landed[v_slot], 16 * used + 16)
            v.tensor_tensor(weighted_v[:, slot, :].rearrange("p (g w) -> p g w", w=W),
                            v_ring[:, v_slot, :].rearrange("p (g w) -> p g w", w=W),
                            prob[:, par, c, :].rearrange("p (g a) -> p g a", a=1).broadcast_to([P, G, W]), ALU.mult
                            ).then_inc(weighted, 1)

        def divide(t, par, uses):
            v.wait_ge(summed, g0(t) + edge_tiles(t))
            if not zero(t):
                v.wait_ge(o_ready, t)
            v.tensor_scalar(den, den_at(par), TINY, None, ALU.max).then_inc(den_step, 1)
            v.wait_ge(den_step, 2 * t + 1)
            v.reciprocal(den, den).then_inc(den_step, 1)
            v.wait_ge(den_step, 2 * t + 2)
            if has(t, 2):
                v.wait_ge(o_out[par], 16 * uses)
            v.tensor_tensor(o_stage[:, par, :].rearrange("p (g w) -> p g w", w=W), sums_at(par)[:].rearrange("p (g w) -> p g w", w=W),
                            den.rearrange("p (g a) -> p g a", a=1).broadcast_to([P, G, W]), ALU.mult).then_inc(o_ready, 1)

        def step(t, par, half):
            if tf:
                if has(t, 2):
                    weigh(t - 2, 0, par)
                for c in range(CMAX):
                    if has(t) and c < edge_tiles(t):
                        product(t, c)
                    if has(t, 2) and c + 1 < edge_tiles(t - 2):
                        weigh(t - 2, c + 1, par)
                    if has(t) and c < edge_tiles(t):
                        score_of(t, c)
                    if has(t, 1) and c == 1:
                        shift(t - 1)
            else:
                for c in range(CMAX):
                    if has(t, 2) and c < edge_tiles(t - 2):
                        weigh(t - 2, c, par)
                    if has(t, 1) and c == 2:
                        shift(t - 1)
                    if has(t, LATE) and c == 4:
                        divide(t - LATE, 1 - par, half + (par - LATE) // 2)
                    if has(t) and c == 5:
                        scores_gat(t, par, half)
            if tf and has(t, LATE):
                divide(t - LATE, par, half - 1)
        steps(v, step)

    return gpsimd, sync, tensor, scalar, vector


def post_gat(nc, sem, carve, bank, w, L, ident, eps_col, x_rows, ao, y_rows):
    x_tile, o_tile, y, normal, z, moved_z, stats, mv, sd, rs, shift = carve(
        (2, BD), (2, BD), (2, BD), (2, BD), (2, BD), (2, BD), (B, 6), (2, B, 2), (2, B), (2, B), (2, B))
    new = lambda name: sem(f"{name}{L}")
    x_in, o_in = [new("px0_"), new("px1_")], [new("po0_"), new("po1_")]
    stored = [new("st0_"), new("st1_")]
    y_made, stats_made, moments, roots, inverse, factors = new("y_made"), new("stats_made"), new("moments"), new("roots"), new("inverse"), new("factors")
    normed, scaled, moved = new("normed"), new("scaled"), new("moved")
    x_loads, stores = len(x_rows(0)), len(y_rows(0))

    def turns(eng, turn):
        for k in range(4):
            turn(k, k % 2, k // 2)
        with eng.Fori(2, RT // 2 - 1) as i:
            turn(2 * i, 0, i)
            turn(2 * i + 1, 1, i)
        for k in range(RT - 2, RT + 3):
            turn(k, k % 2, k // 2)

    def has(k, lag=0):
        return not isinstance(k, int) or 0 <= k - lag < RT

    as3 = lambda x: x.rearrange("p (b d) -> p b d", b=B)
    with nc.Block() as block:
        @block.sync
        def _(sp):
            def load(t, par):
                for src, lo, hi in x_rows(t):
                    sp.dma_start(x_tile[lo:hi, par, :] if len(src.shape) == 2 else as3(x_tile[lo:hi, par, :]), src
                                 ).then_inc(x_in[par], 16)
                sp.dma_start(o_tile[:, par, :], ao[bass.ds(t, 1)].rearrange("r q n -> (r q) n")).then_inc(o_in[par], 16)

            def turn(k, par, i):
                if has(k, -2):
                    sp.wait_ge(y_made, k + 1)
                    load(k + 2, par)
                if has(k, 3):
                    sp.wait_ge(moved, k - 2)
                    for dst, lo, hi in y_rows(k - 3):
                        src = moved_z[lo:hi, 1 - par, :]
                        sp.dma_start(dst, src if len(dst.shape) == 2 else as3(src)).then_inc(stored[1 - par], 16)

            load(0, 0)
            load(1, 1)
            turns(sp, turn)
            for s in range(2):
                sp.wait_ge(stored[s], 16 * stores * (RT // 2))

        @block.scalar
        def _(act):
            def turn(k, par, i):
                if has(k, 1):
                    t, s = k - 1, 1 - par
                    act.wait_ge(factors, k)
                    if has(t, 2):
                        act.wait_ge(scaled, t - 1)
                    for b in range(B):
                        ins = act.activation(normal[:, s, b * D:(b + 1) * D], y[:, s, b * D:(b + 1) * D], ACT.Identity,
                                             bias=shift[:, s, b:b + 1], scale=rs[:, s, b:b + 1])
                    ins.then_inc(normed, 1)
                if has(k):
                    act.wait_ge(moments, k + 1)
                    if has(k, 2):
                        act.wait_ge(inverse, k - 1)
                    act.activation(sd[:, par, :], mv[:, par, :, 1], ACT.Sqrt, bias=eps_col[:, 0:1]).then_inc(roots, 1)
            turns(act, turn)

        @block.vector
        def _(v):
            def turn(k, par, i):
                if has(k, 1):
                    s = 1 - par
                    v.wait_ge(roots, k)
                    v.reciprocal(rs[:, s, :], sd[:, s, :]).then_inc(inverse, 1)
                    v.wait_ge(inverse, k)
                    v.scalar_tensor_tensor(shift[:, s, :], mv[:, s, :, 0], -1.0, rs[:, s, :], ALU.mult, ALU.mult
                                           ).then_inc(factors, 1)
                if has(k):
                    v.wait_ge(x_in[par], 16 * x_loads * (i + 1))
                    v.wait_ge(o_in[par], 16 * i + 16)
                    if has(k, 2):
                        v.wait_ge(normed, k - 1)
                    if has(k, 1):
                        v.wait_ge(moments, k)
                    v.tensor_tensor(y[:, par, :], x_tile[:, par, :], o_tile[:, par, :], ALU.add).then_inc(y_made, 1)
                    v.wait_ge(y_made, k + 1)
                    for b in range(B):
                        ins = v.bn_stats(stats[:, b, :], y[:, par, b * D:(b + 1) * D])
                    ins.then_inc(stats_made, 1)
                    hold(v, stats_made, k + 1)
                    for b in range(B):
                        ins = v.bn_aggr(mv[:, par, b, :], stats[:, b, :])
                    ins.then_inc(moments, 1)
                if has(k, 2):
                    v.wait_ge(normed, k - 1)
                    if has(k, 4):
                        v.wait_ge(moved, k - 3)
                    v.tensor_tensor(as3(z[:, par, :]), as3(normal[:, par, :]), w["gb"][:, 0:1, :].broadcast_to([P, B, D]),
                                    ALU.mult).then_inc(scaled, 1)
            turns(v, turn)

        @block.gpsimd
        def _(g):
            def turn(k, par, i):
                if has(k, 2):
                    g.wait_ge(scaled, k - 1)
                    if has(k, 4):
                        g.wait_ge(stored[par], 16 * stores * (i - 1) if not isinstance(k, int) else 16 * stores * (k // 2 - 1))
                    g.tensor_tensor(as3(moved_z[:, par, :]), as3(z[:, par, :]), w["gb"][:, 1:2, :].broadcast_to([P, B, D]),
                                    ALU.add).then_inc(moved, 1)
            turns(g, turn)


def post_tf(nc, sem, carve, bank, w, L, ident, eps_col, x_rows, ao, y_rows):
    GW = 4 * D
    GROUPS = 2 * RT
    (x_tile, o_tile, o_turned, xb, y1, normal1, z1, x1, x1_turned, hidden, x1b, y2, normal2, z2, x2, stats1, stats2, mv1,
     mv2, sd1, sd2, rs1, rs2, shift1, shift2) = carve(
        (4, GW), (4, GW), (2, GW), (2, GW), (2, GW), (2, GW), (2, GW), (4, GW), (2, GW), (2, FC, GW), (4, GW), (2, GW),
        (2, GW), (2, GW), (4, GW), (4, 6), (4, 6), (2, 4, 2), (2, 4, 2), (2, 4), (2, 4), (2, 4), (2, 4), (2, 4), (2, 4))
    new = lambda name: sem(f"{name}{L}")
    x_in, o_in = [new(f"fx{s}_") for s in range(2)], [new(f"fo{s}_") for s in range(2)]
    o_tr, o_copied, o_prod = new("o_tr"), new("o_copied"), new("o_prod")
    x1_tr, x1_copied, h_prod, h_relu, y2_prod = new("x1_tr"), new("x1_copied"), new("h_prod"), new("h_relu"), new("y2_prod")
    xb_made, x1_made, x1b_made, x2_made = new("xb_made"), new("x1_made"), new("x1b_made"), new("x2_made")
    norm_sems = lambda m: [new(f"{name}{m}_") for name in ("y_made", "stats_made", "moments", "roots", "inverse", "factors", "normed", "scaled")]
    norm1, norm2 = norm_sems(1), norm_sems(2)
    y1_made, _, m1, r1, inverse1, f1, normed1, scaled1 = norm1
    y2_made, _, m2, r2, inverse2, f2, normed2, scaled2 = norm2
    stored = [new(f"fst{s}_") for s in range(2)]
    x_loads, stores = len(x_rows(0)), len(y_rows(0))

    def turns(eng, turn):
        for k in range(8):
            turn(k, k % 4, k // 4)
        with eng.Fori(2, GROUPS // 4 - 1) as i:
            for j in range(4):
                turn(4 * i + j, j, i)
        for k in range(GROUPS - 4, GROUPS + 6):
            turn(k, k % 4, k // 4)

    def has(k, lag=0):
        return not isinstance(k, int) or 0 <= k - lag < GROUPS

    as3 = lambda x: x.rearrange("p (b d) -> p b d", b=4)
    row = lambda r: r.broadcast_to([P, 4, D])

    with nc.Block() as block:
        @block.sync
        def _(sp):
            def turn(k, j, i):
                if has(k, 5) and (j - 5) % 2 == 1:
                    s4 = (j - 5) % 4
                    t = 2 * i + (j - 5) // 2
                    sp.wait_ge(x2_made, k - 4)
                    tile_in = x2[:, s4 - 1:s4 + 1, :].rearrange("p h n -> p (h n)")
                    for dst, lo, hi in y_rows(t):
                        sp.dma_start(dst, tile_in[lo:hi]).then_inc(stored[s4 // 2], 16)
            turns(sp, turn)
            for s in range(2):
                sp.wait_ge(stored[s], 16 * stores * (RT // 2))

        @block.tensor
        def _(pe):
            def turn_o(n, j, i):
                if j % 2 == 0:
                    pe.wait_ge(o_in[j // 2], 16 * i + 16)
                if has(n, 1):
                    pe.wait_ge(o_copied, n)
                for b in range(4):
                    tr = pe.transpose(bank[0][:, b * P:(b + 1) * P], o_tile[:, j, b * D:(b + 1) * D], ident[:])
                tr.then_inc(o_tr, 1)

            def turn(k, j, i):
                if has(k):
                    pe.wait_ge(o_copied, k + 1)
                    if has(k, 1):
                        pe.wait_ge(y1_made, k)
                    for b in range(4):
                        mm = pe.matmul(bank[1][:, b * D:(b + 1) * D], o_turned[:, j % 2, b * P:(b + 1) * P], w["wo"][:],
                                       start=True, stop=True)
                    mm.then_inc(o_prod, 1)
                if has(k, 2):
                    n, s = k - 2, (j - 2) % 4
                    pe.wait_ge(x1_made, n + 1)
                    if has(n, 1):
                        pe.wait_ge(x1_copied, n)
                    for b in range(4):
                        tr = pe.transpose(bank[2][:, b * P:(b + 1) * P], x1[:, s, b * D:(b + 1) * D], ident[:])
                    tr.then_inc(x1_tr, 1)
                if has(k, 3):
                    n, s = k - 3, (j - 3) % 2
                    pe.wait_ge(h_relu, FC * n + FC)
                    if has(n, 1):
                        pe.wait_ge(y2_made, n)
                    for b in range(4):
                        for c in range(FC):
                            mm = pe.matmul(bank[5][:, b * D:(b + 1) * D], hidden[:, s, c, b * P:(b + 1) * P], w["w2"][:, c, :],
                                           start=(c == 0), stop=(c == FC - 1))
                    mm.then_inc(y2_prod, 1)
                if has(k, -1):
                    turn_o(k + 1, (j + 1) % 4, i + (j + 1) // 4)
                if has(k, 2):
                    n, s = k - 2, (j - 2) % 2
                    pe.wait_ge(x1_copied, n + 1)
                    for c in range(FC):
                        if has(n, 1):
                            pe.wait_ge(h_relu, FC * (n - 1) + c + 1)
                        pe.matmul(bank[3 + c], w["w1"][:, c * P:(c + 1) * P], x1_turned[:, s, :], start=True, stop=True
                                  ).then_inc(h_prod, 1)

            turn_o(0, 0, 0)
            turns(pe, turn)

        @block.scalar
        def _(act):
            def load(n, j, t):
                par = j // 2
                if has(n, 4):
                    act.wait_ge(y1_made, n - 2)
                    act.wait_ge(xb_made, n - 2)
                    act.wait_ge(o_tr, n - 2)
                for src, lo, hi in x_rows(t):
                    act.dma_start(x_tile[lo:hi, j:j + 2, :].rearrange("p h n -> p (h n)"), src).then_inc(x_in[par], 16)
                act.dma_start(o_tile[:, j:j + 2, :], ao[bass.ds(t, 1)].rearrange("r q (h n) -> q (r h) n", h=2)).then_inc(o_in[par], 16)

            def copy_o(n, j):
                act.wait_ge(o_tr, n + 1)
                if has(n, 2):
                    act.wait_ge(o_prod, n - 1)
                act.copy(o_turned[:, j % 2, :], bank[0]).then_inc(o_copied, 1)

            def normalise(n, s, y, normal, rs, shift, sems):
                factors, normed, scaled = sems[5:]
                act.wait_ge(factors, n + 1)
                if has(n, 2):
                    act.wait_ge(scaled, n - 1)
                for b in range(4):
                    ins = act.activation(normal[:, s, b * D:(b + 1) * D], y[:, s, b * D:(b + 1) * D], ACT.Identity,
                                         bias=shift[:, s, b:b + 1], scale=rs[:, s, b:b + 1])
                ins.then_inc(normed, 1)

            def root(n, s, sd, mv, sems):
                moments, roots, inverse = sems[2:5]
                act.wait_ge(moments, n + 1)
                if has(n, 2):
                    act.wait_ge(inverse, n - 1)
                act.activation(sd[:, s, :], mv[:, s, :, 1], ACT.Sqrt, bias=eps_col[:, 0:1]).then_inc(roots, 1)

            def turn(k, j, i):
                if has(k, -2) and has(k, 1) and j % 2 == 0:
                    load(k + 2, (j + 2) % 4, 2 * i + (j + 2) // 2)
                if has(k, 1):
                    normalise(k - 1, (j - 1) % 2, y1, normal1, rs1, shift1, norm1)
                if has(k, 2):
                    n, s = k - 2, j % 2
                    act.wait_ge(x1_tr, n + 1)
                    if has(n, 2):
                        act.wait_ge(h_prod, FC * (n - 1))
                    act.copy(x1_turned[:, s, :], bank[2]).then_inc(x1_copied, 1)
                if has(k, 4):
                    normalise(k - 4, j % 2, y2, normal2, rs2, shift2, norm2)
                if has(k):
                    root(k, j % 2, sd1, mv1, norm1)
                if has(k, -1):
                    copy_o(k + 1, j + 1)
                if has(k, 2):
                    n, s = k - 2, j % 2
                    if has(n, 2):
                        act.wait_ge(y2_prod, n - 1)
                    for c in range(FC):
                        act.wait_ge(h_prod, FC * n + c + 1)
                        act.activation(hidden[:, s, c, :], bank[3 + c], ACT.Relu, bias=w["b1"][:, c:c + 1]).then_inc(h_relu, 1)
                if has(k, 3):
                    root(k - 3, (j - 3) % 2, sd2, mv2, norm2)

            load(0, 0, 0)
            load(2, 2, 1)
            copy_o(0, 0)
            turns(act, turn)

        @block.vector
        def _(v):
            def factors(n, s, sd, mv, rs, shift, sems):
                _, _, _, roots, inverse, made, normed, _ = sems
                v.wait_ge(roots, n + 1)
                if has(n, 2):
                    v.wait_ge(normed, n - 1)
                v.reciprocal(rs[:, s, :], sd[:, s, :]).then_inc(inverse, 1)
                v.wait_ge(inverse, n + 1)
                v.scalar_tensor_tensor(shift[:, s, :], mv[:, s, :, 0], -1.0, rs[:, s, :], ALU.mult, ALU.mult).then_inc(made, 1)

            def add_and_moments(n, s, y, product, addend, stats, mv, sems):
                y_made, stats_made, moments, _, _, _, normed, _ = sems
                if has(n, 2):
                    v.wait_ge(normed, n - 1)
                if has(n, 1):
                    v.wait_ge(moments, n)
                v.tensor_tensor(y[:, s, :], product, addend, ALU.add).then_inc(y_made, 1)
                v.wait_ge(y_made, n + 1)
                for b in range(4):
                    ins = v.bn_stats(stats[:, b, :], y[:, s, b * D:(b + 1) * D])
                ins.then_inc(stats_made, 1)
                hold(v, stats_made, n + 1)
                for b in range(4):
                    ins = v.bn_aggr(mv[:, s, b, :], stats[:, b, :])
                ins.then_inc(moments, 1)

            def scale(n, s, z, normal, gamma, sems, z_used):
                normed, scaled = sems[6:]
                v.wait_ge(normed, n + 1)
                if has(n, 2):
                    v.wait_ge(z_used, n - 1)
                v.tensor_tensor(as3(z[:, s, :]), as3(normal[:, s, :]), row(w["gb"][:, gamma:gamma + 1, :]), ALU.mult
                                ).then_inc(scaled, 1)

            def turn(k, j, i):
                if has(k, 1):
                    factors(k - 1, (j - 1) % 2, sd1, mv1, rs1, shift1, norm1)
                if has(k, 4):
                    factors(k - 4, j % 2, sd2, mv2, rs2, shift2, norm2)
                if has(k):
                    v.wait_ge(o_prod, k + 1)
                    v.wait_ge(xb_made, k + 1)
                    add_and_moments(k, j % 2, y1, bank[1], xb[:, j % 2, :], stats1, mv1, norm1)
                if has(k, 1):
                    scale(k - 1, (j - 1) % 2, z1, normal1, 0, norm1, x1_made)
                if has(k, 3):
                    n, s = k - 3, (j - 3) % 2
                    v.wait_ge(y2_prod, n + 1)
                    v.wait_ge(x1b_made, n + 1)
                    add_and_moments(n, s, y2, bank[5], x1b[:, (j - 3) % 4, :], stats2, mv2, norm2)
                if has(k, 4):
                    scale(k - 4, j % 2, z2, normal2, 2, norm2, x2_made)
            turns(v, turn)

        @block.gpsimd
        def _(g):
            def add_bo(n, j, i):
                if j % 2 == 0:
                    g.wait_ge(x_in[j // 2], 16 * x_loads * (i + 1))
                if has(n, 2):
                    g.wait_ge(y1_made, n - 1)
                g.tensor_tensor(as3(xb[:, j % 2, :]), as3(x_tile[:, j, :]), row(w["bias"][:, 0:1, :]), ALU.add).then_inc(xb_made, 1)

            def turn(k, j, i):
                if has(k, 1):
                    n, s, s4 = k - 1, (j - 1) % 2, (j - 1) % 4
                    g.wait_ge(scaled1, n + 1)
                    if has(n, 4):
                        g.wait_ge(x1_tr, n - 3)
                        g.wait_ge(x1b_made, n - 3)
                    g.tensor_tensor(as3(x1[:, s4, :]), as3(z1[:, s, :]), row(w["gb"][:, 1:2, :]), ALU.add).then_inc(x1_made, 1)
                    g.wait_ge(x1_made, n + 1)
                    if has(n, 4):
                        g.wait_ge(y2_made, n - 3)
                    g.tensor_tensor(as3(x1b[:, s4, :]), as3(x1[:, s4, :]), row(w["bias"][:, 1:2, :]), ALU.add).then_inc(x1b_made, 1)
                if has(k, -1):
                    add_bo(k + 1, (j + 1) % 4, i + (j + 1) // 4)
                if has(k, 4):
                    n, s, s4 = k - 4, j % 2, j % 4
                    g.wait_ge(scaled2, n + 1)
                    if has(n, 4) and s4 % 2 == 0:
                        g.wait_ge(stored[s4 // 2], 16 * stores * (i - 1))
                    g.tensor_tensor(as3(x2[:, s4, :]), as3(z2[:, s, :]), row(w["gb"][:, 3:4, :]), ALU.add).then_inc(x2_made, 1)

            add_bo(0, 0, 0)
            turns(g, turn)


_INS = ['x', 'adj'] + [f'L{L}_gnn_{n}' for L in (0, 3) for n in ('W', 'a_src', 'a_dst', 'ln_gamma', 'ln_beta')] + \
       [f'L{L}_gnn_{n}' for L in (1, 2) for n in ('Wq', 'Wk', 'Wv', 'Wo', 'bo', 'ln1_g', 'ln1_b', 'W1', 'b1', 'W2', 'b2',
                                                  'ln2_g', 'ln2_b')]


def kernel(**inputs):
    import numpy as _np
    import concourse.bacc as _bacc
    from concourse import mybir as _mybir
    from concourse.bass_utils import run_bass_kernel_spmd as _run

    nc = _bacc.Bacc("TRN2", target_bir_lowering=False, num_devices=1)
    arrays, args = {}, {}
    for name in _INS:
        x = _np.ascontiguousarray(inputs[name])
        arrays[f"in_{name}_dram"] = x
        args[name] = nc.dram_tensor(f"in_{name}_dram", x.shape, _mybir.dt.from_np(x.dtype), kind="ExternalInput").ap()
    out = nc.dram_tensor("out_0_dram", (B, N, D), _mybir.dt.float32, kind="ExternalOutput").ap()
    build(nc, args, out)
    r = _run(nc, [arrays], core_ids=[0])
    return r.results[0]["out_0_dram"]
```

```python
import concourse.bass as bass
from concourse import mybir
from contextlib import ExitStack

F32 = mybir.dt.float32
I32 = mybir.dt.int32
BF16 = mybir.dt.bfloat16
ONE_HOT = mybir.dt.uint8
ALU = mybir.AluOpType
ACT = mybir.ActivationFunctionType
AX = mybir.AxisListType

P = 128
B, N, D = 8, 2048, 128
RT = N // P
BD = B * D
HEADS, HD = 8, 16
FFN = 2 * D
FC = FFN // P
CMAX = 11
CREST = 10
EMAX = CMAX * P
BLK = 64
NBLK = N // BLK
COL_OFS, COL_ROW, COL_LOC = NBLK, NBLK + 1, NBLK + 2
TABW = NBLK + 3
ARENA = 33792
APART = 13312
BIG = 1.0e30
TINY = 1.0e-30
SLOPE = 0.2
EPS = 1e-5
KINDS = ("gat", "tf", "tf", "gat")


class Chain:

    def __init__(self, eng, sem):
        self.eng, self.sem, self.base, self.n = eng, sem, 0, 0

    def link(self, ins):
        ins.then_inc(self.sem, 1)
        self.n += 1
        self.eng.wait_ge(self.sem, self.base + self.n)

    def loop(self, i, per):
        self.start, self.per = self.base + self.n, per
        self.base, self.n = self.start + i * per, 0

    def end(self, turns):
        assert self.n == self.per, (self.n, self.per)
        self.base, self.n = self.start + turns * self.per, 0


class Semaphores:

    def __init__(self, nc):
        self.nc, self.made = nc, {}

    def get(self, name):
        if name not in self.made:
            self.made[name] = self.nc.alloc_semaphore(name)
        return self.made[name]

    def renew(self):
        if self.made:
            self.nc.clear_and_free_semaphores(list(self.made.values()))
            self.nc.all_engine_barrier()
        self.made = {}


def hold(eng, sem, value):
    eng.wait_ge(sem, value)
    eng.nop(nofuse=True)


def first_edge_tile(t):
    return 0 if isinstance(t, int) and t == 0 else CMAX + CREST * (t - 1)


def edge_tiles(t):
    return CMAX if isinstance(t, int) and t == 0 else CREST


def build(nc, a, out, layers=4):
    ctx = ExitStack()
    with ctx:
        def sb(name, shape, dt=F32):
            return ctx.enter_context(nc.sbuf_tensor(name, shape, dt))

        def ps(name, shape):
            return ctx.enter_context(nc.psum_tensor(name, shape, F32))

        sems = Semaphores(nc)
        sem = sems.get

        xs = nc.dram_tensor("xs", (RT, P, BD), F32).ap()
        ao = nc.dram_tensor("ao", (RT, P, BD), F32).ap()
        qq = nc.dram_tensor("qq", (RT, P, BD), F32).ap()
        si = nc.dram_tensor("si", (RT, P, B), F32).ap()
        kk = nc.dram_tensor("kk", (N, BD), F32).ap()
        vv = nc.dram_tensor("vv", (N, BD), F32).ap()
        sj = nc.dram_tensor("sj", (N, B), F32).ap()
        starts = nc.dram_tensor("starts", (RT, EMAX + P), F32).ap()

        ident = sb("ident", [P, P])
        ones = sb("ones", [P, P])
        below = sb("below", [P, P])
        lane = sb("lane", [P, P])
        edge_id = sb("edge_id", [P, CMAX])
        tile_start = sb("tile_start", [P, CMAX])
        capacity = sb("capacity", [P, RT])
        fits = sb("fits", [P, 1], I32)
        neighbour = sb("neighbour", [P, RT, CMAX], I32)
        row_from = sb("row_from", [P, RT, CMAX])
        row_to = sb("row_to", [P, RT, CMAX])
        spread_bits = sb("spread_bits", [P, RT, CMAX, P], ONE_HOT)
        select_bits = sb("select_bits", [P, RT, CMAX, P], ONE_HOT)
        w = {}
        for L, kind in enumerate(KINDS):
            if kind == "tf":
                w[L] = dict(qkv=sb(f"wqkv{L}", [P, 3 * D]), wo=sb(f"wo{L}", [P, D]), w1=sb(f"w1{L}", [P, FFN]),
                            w2=sb(f"w2{L}", [P, FC, D]), b1=sb(f"b1{L}", [P, FC]), bias=sb(f"bias{L}", [P, 2, D]),
                            gb=sb(f"gb{L}", [P, 4, D]))
            else:
                w[L] = dict(w=sb(f"w{L}", [P, D + 2]), av=sb(f"av{L}", [P, 2]), gb=sb(f"gb{L}", [P, 2, D]))
        eps_col = sb("eps_col", [P, 1])

        arena = sb("arena", [P, ARENA])

        def carve(*shapes):
            at, views = 0, []
            for shape in shapes:
                size = 1
                for s in shape:
                    size *= s
                v = arena[:, at:at + size]
                if len(shape) == 2:
                    v = v.rearrange("p (a b) -> p a b", a=shape[0])
                if len(shape) == 3:
                    v = v.rearrange("p (a b c) -> p a b c", a=shape[0], b=shape[1])
                views.append(v)
                at += size
            assert at <= ARENA, at
            return views

        bank = [ps(f"bank{i}", [P, 4 * P]) if i in (6, 7) else None for i in range(8)]
        pair = [ps(f"pair{i}", [P, 8 * P]) for i in range(3)]
        bank[0], bank[1] = pair[0][:, 0:512], pair[0][:, 512:1024]
        bank[2], bank[3] = pair[1][:, 0:512], pair[1][:, 512:1024]
        bank[4], bank[5] = pair[2][:, 0:512], pair[2][:, 512:1024]

        x_by_row = a["x"].rearrange("b (q r) d -> r q b d", r=RT)
        out_by_row = out.rearrange("b (q r) d -> r q b d", r=RT)
        adj_by_row = a["adj"].rearrange("(q r) n -> r q n", r=RT)
        kk_by_row = kk.rearrange("(q r) n -> r q n", r=RT)
        vv_by_row = vv.rearrange("(q r) n -> r q n", r=RT)
        sj_by_row = sj.rearrange("(q r) n -> r q n", r=RT)

        def tile_rows(view, t):
            return (view[bass.ds(t, 1), 0:1], view[bass.ds(RT - 1 - t, 1), 1:P])

        def kept_rows(t):
            return [(xs[bass.ds(t, 1)].rearrange("r q n -> (r q) n"), 0, P)]

        def given_rows(t):
            return [(src.rearrange("r q b d -> (r q) b d"), lo, hi) for src, lo, hi in zip(tile_rows(x_by_row, t), (0, 1), (1, P))]

        def result_rows(t):
            return [(dst.rearrange("r q b d -> (r q) b d"), lo, hi) for dst, lo, hi in zip(tile_rows(out_by_row, t), (0, 1), (1, P))]

        def projection(L, x_rows, made=None):
            return project(nc, sem, carve, bank, pair, w[L], KINDS[L], L, ident, tile_rows, x_rows, qq, kk_by_row, vv_by_row,
                           si, sj_by_row, made)

        row_count, = carve((1,))
        nz, adj_rows, block_sum, cum, keep32, table, deg, before, total, over = carve(
            (N,), (2, N), (RT, NBLK), (RT * NBLK,), (RT * NBLK,), (RT, TABW), (RT,), (RT,), (RT,), (RT,))
        adj_rows = adj_rows.bitcast(I32)
        first = projection(0, given_rows)
        with nc.Block() as block:
            first_w_in, w_in, weights_ready = sem("first_w_in"), sem("w_in"), sem("weights_ready")
            adj_in = [sem("adj_in0"), sem("adj_in1")]
            adj_read, const_made, counts, dv = sem("adj_read"), sem("const_made"), sem("counts"), sem("dv0")
            prefix = sem("prefix")

            @block.sync
            def _(sp):
                first.sync(sp)

            @block.scalar
            def _(act):
                n = [0] * len(KINDS)
                for L, kind in enumerate(KINDS):
                    pre = f"L{L}_gnn_"
                    if kind == "tf":
                        loads = [(w[L]["qkv"][:, k * D:(k + 1) * D], a[pre + m]) for k, m in enumerate(("Wq", "Wk", "Wv"))]
                        loads += [(w[L]["wo"][:], a[pre + "Wo"]), (w[L]["w1"][:], a[pre + "W1"]),
                                  (w[L]["w2"][:], a[pre + "W2"].rearrange("(c p) n -> p c n", p=P)),
                                  (w[L]["bias"][:, 0, :], a[pre + "bo"].rearrange("(a n) -> a n", a=1).broadcast_to([P, D])),
                                  (w[L]["bias"][:, 1, :], a[pre + "b2"].rearrange("(a n) -> a n", a=1).broadcast_to([P, D]))]
                        loads += [(w[L]["b1"][:, c:c + 1], a[pre + "b1"][c * P:(c + 1) * P].rearrange("(p a) -> p a", a=1))
                                  for c in range(FC)]
                        gb = ("ln1_g", "ln1_b", "ln2_g", "ln2_b")
                    else:
                        loads = [(w[L]["w"][:, 0:D], a[pre + "W"])]
                        loads += [(w[L]["av"][:, k:k + 1], a[pre + m].rearrange("(p a) -> p a", a=1))
                                  for k, m in enumerate(("a_src", "a_dst"))]
                        gb = ("ln_gamma", "ln_beta")
                    loads += [(w[L]["gb"][:, k, :], a[pre + m].rearrange("(a n) -> a n", a=1).broadcast_to([P, D]))
                              for k, m in enumerate(gb)]
                    for dst, src in loads:
                        act.dma_start(dst, src).then_inc(w_in if L else first_w_in, 16)
                        n[L] += 16
                act.wait_ge(first_w_in, n[0])
                act.sem_inc(weights_ready, 1)
                first.scalar(act)
                act.wait_ge(w_in, sum(n[1:]))

            @block.gpsimd
            def _(g):
                g.memset(ones[:], 1.0)
                g.memset(eps_col[:], EPS)
                g.memset(capacity[:], float(CREST * P)).then_inc(const_made, 1)
                g.wait_ge(const_made, 1)
                g.memset(capacity[:, 0:1], float(CMAX * P))
                g.affine_select(out=ident[:], in_=ones[:], compare_op=ALU.is_equal, fill=0.0, base=0,
                                pattern=[[-1, P]], channel_multiplier=1)
                g.affine_select(out=below[:], in_=ones[:], compare_op=ALU.is_gt, fill=0.0, base=0,
                                pattern=[[1, P]], channel_multiplier=-1)
                g.affine_select(out=keep32.rearrange("p (t b) -> p t b", b=NBLK), in_=ones[:, 0:1].broadcast_to([P, RT * NBLK]).rearrange("p (t b) -> p t b", b=NBLK),
                                compare_op=ALU.is_gt, fill=0.0, base=0, pattern=[[0, RT], [1, NBLK]],
                                channel_multiplier=0)
                any_dt = dict(allow_small_or_imprecise_dtypes=True)
                g.iota(lane[:], pattern=[[1, P]], base=0, channel_multiplier=0, **any_dt)
                g.iota(edge_id[:], pattern=[[P, CMAX]], base=0, channel_multiplier=1, **any_dt)
                g.iota(tile_start[:], pattern=[[P, CMAX]], base=0, channel_multiplier=0, **any_dt)
                g.iota(table[:, :, COL_LOC:COL_LOC + 1], pattern=[[0, RT], [0, 1]], base=1, channel_multiplier=1, **any_dt)
                g.iota(table[:, :, COL_ROW:COL_ROW + 1], pattern=[[-1, RT], [0, 1]], base=RT - 1,
                       channel_multiplier=RT, **any_dt).then_inc(const_made, 1)
                def load(t, slot):
                    for src, lo, hi in zip(tile_rows(adj_by_row, t), (0, 1), (1, P)):
                        g.dma_start(adj_rows[lo:hi, slot:slot + 1, :], src.rearrange("r q n -> q r n")
                                    ).then_inc(adj_in[slot], 16)

                load(0, 0)
                load(1, 1)
                g.wait_ge(const_made, 2)
                g.iota(table[0:1, :, COL_ROW:COL_ROW + 1], pattern=[[1, RT], [0, 1]], base=0,
                       channel_multiplier=0, **any_dt).then_inc(const_made, 1)
                with g.Fori(1, RT // 2) as i:
                    for slot in range(2):
                        hold(g, adj_read, 2 * i - 1 + slot)
                        load(2 * i + slot, slot)

            @block.vector
            def _(v):
                ch = Chain(v, dv)
                def count(t, slot, times):
                    v.wait_ge(adj_in[slot], 32 * times + 32)
                    if not (isinstance(t, int) and t == 0):
                        v.wait_ge(adj_read, t)
                    ch.link(v.tensor_scalar(nz, adj_rows[:, slot, :], 0, None, ALU.not_equal))
                    v.tensor_reduce(block_sum[:, bass.ds(t, 1), :],
                                    nz.rearrange("p (a k j) -> p a k j", a=1, j=BLK), AX.X, ALU.add).then_inc(adj_read, 1)

                count(0, 0, 0)
                count(1, 1, 0)
                with v.Fori(1, RT // 2) as i:
                    ch.loop(i - 1, 2)
                    count(2 * i, 0, i)
                    count(2 * i + 1, 1, i)
                ch.end(RT // 2 - 1)
                v.wait_ge(adj_read, RT)
                v.wait_ge(const_made, 3)
                ch.link(v.tensor_tensor_scan(cum, keep32, block_sum.rearrange("p t k -> p (t k)"), 0.0, ALU.mult, ALU.add))
                cum3 = cum.rearrange("p (t k) -> p t k", t=RT)
                ch.link(v.tensor_copy(table[:, :, 0:NBLK], cum3))
                v.tensor_copy(deg, cum3[:, :, NBLK - 1]).then_inc(counts, 1)
                v.wait_ge(prefix, 1)
                v.tensor_copy(before, bank[6][:, 0:RT]).then_inc(dv, 1)
                ch.link(v.tensor_copy(total, bank[7][:, 0:RT]))
                ch.n += 1
                v.wait_ge(dv, ch.base + ch.n)
                v.tensor_copy(table[:, :, COL_OFS], before)
                bc = lambda x: x.rearrange("p (t a) -> p t a", a=1).broadcast_to([P, RT, CMAX])
                cc = tile_start[:].rearrange("p (a c) -> p a c", a=1).broadcast_to([P, RT, CMAX])
                ch.link(v.tensor_tensor(row_from[:], bc(before), cc, ALU.subtract))
                v.tensor_tensor(row_to[:], row_from[:], bc(deg), ALU.add)
                ch.link(v.tensor_tensor(over, total, capacity[:], ALU.subtract))
                ch.link(v.tensor_reduce(row_count, over, AX.X, ALU.max))
                ch.link(v.tensor_scalar(fits[:], row_count, 0.0, None, ALU.is_le))

            @block.tensor
            def _(pe):
                pe.wait_ge(const_made, 3)
                pe.wait_ge(weights_ready, 1)
                first.tensor(pe)
                pe.wait_ge(counts, 1)
                pe.matmul(bank[6][:, 0:RT], below[:], deg, start=True, stop=True)
                pe.matmul(bank[7][:, 0:RT], ones[:], deg, start=True, stop=True).then_inc(prefix, 1)

        _, _, _, _, _, table, deg = carve((N,), (2, N), (RT, NBLK), (RT * NBLK,), (RT * NBLK,), (RT, TABW), (RT,))
        deg_end = (N + 2 * N + 3 * RT * NBLK + RT * TABW + RT)
        views = carve((deg_end,), (2, EMAX), (EMAX,), (CMAX, TABW), (CMAX,), (CMAX, NBLK), (CMAX, NBLK), (CMAX,),
                      (CMAX,), (2, CMAX), (2, CMAX), (2, CMAX), (2, CMAX, BLK), (CMAX, BLK), (CMAX, BLK), (CMAX, BLK),
                      (CMAX,), (CMAX,), (CMAX * BLK,), (EMAX,), (2, EMAX + P), (2, CMAX), (CMAX, P))
        (_, onehot, ge, tab, rank, le, part, blk, base, gidx, rank2, blk_base, ablk, nzb, cumb, leb, inner, col,
         keep64, iota_e, start_row, minus_row, distance) = views
        gidx, ablk = gidx.bitcast(I32), ablk.bitcast(I32)
        adj_blocks = a["adj"].rearrange("n (k j) -> (n k) j", j=BLK)
        with nc.Block() as block:
            oh_made, tab_ready, tab_read, gidx_ready = sem("oh_made"), sem("tab_ready"), sem("tab_read"), sem("gidx_ready")
            blk_in = [sem("blk_in0"), sem("blk_in1")]
            oh_kept, select_kept, distance_made = sem("oh_kept"), sem("select_kept"), sem("distance_made")
            dv, k64_made = sem("dv1"), sem("k64_made")
            start_made, start_clear = sem("start_made"), sem("start_clear")
            end_made, start_ready, start_out = sem("end_made"), sem("start_ready"), [sem("start_out0"), sem("start_out1")]

            @block.scalar
            def _(act):
                def step(t, slot, half):
                    act.wait_ge(oh_made, t + 1)
                    act.copy(spread_bits[:, bass.ds(t, 1), :, :].rearrange("p a c n -> p (a c n)"), onehot[:, slot, :]
                             ).then_inc(oh_kept, 1)
                    act.wait_ge(start_ready, t + 1)
                    act.wait_ge(start_clear, 1)
                    if not (isinstance(t, int) and t < 2):
                        act.wait_ge(start_out[slot], 16 * half)
                    for k in range(3):
                        lo, hi = k * 512, min((k + 1) * 512, EMAX)
                        ins = act.activation(start_row[0:1, slot, lo:hi], bank[1 + k][0:1, 0:hi - lo], ACT.Copy, scale=-BIG)
                    ins.then_inc(start_made, 1)
                    act.wait_ge(gidx_ready, t + 1)
                    if not (isinstance(t, int) and t == 0):
                        act.wait_ge(select_kept, t + 1)
                    for c in range(CMAX):
                        ins = act.activation(distance[:, c, :], lane[:], ACT.Abs, bias=minus_row[:, slot, c:c + 1])
                    ins.then_inc(distance_made, 1)
                    act.wait_ge(distance_made, t + 1)
                    act.activation(select_bits[:, bass.ds(t, 1), :, :].rearrange("p a c n -> p (a c) n"), distance, ACT.Relu,
                                   bias=1.0, scale=-1.0).then_inc(select_kept, 1)

                act.sem_inc(select_kept, 1)
                step(0, 0, 0)
                step(1, 1, 0)
                with act.Fori(1, RT // 2) as i:
                    for slot in range(2):
                        step(2 * i + slot, slot, i)

            @block.gpsimd
            def _(g):
                g.affine_select(out=keep64.rearrange("p (t b) -> p t b", b=BLK), in_=ones[:, 0:1].broadcast_to([P, CMAX * BLK]).rearrange("p (t b) -> p t b", b=BLK),
                                compare_op=ALU.is_gt, fill=0.0, base=0, pattern=[[0, CMAX], [1, BLK]],
                                channel_multiplier=0)
                g.iota(iota_e, pattern=[[1, EMAX]], base=0, channel_multiplier=0,
                       allow_small_or_imprecise_dtypes=True).then_inc(k64_made, 1)
                with g.Fori(0, RT // 2) as i:
                    for slot in range(2):
                        hold(g, gidx_ready, 2 * i + slot + 1)
                        for c in range(CMAX):
                            g.indirect_dma_start(out=ablk[:, slot, c, :], out_offset=None, in_=adj_blocks,
                                                 in_offset=bass.IndirectOffsetOnAxis(ap=gidx[:, slot, c:c + 1], axis=0)
                                                 ).then_inc(blk_in[slot], 16)

            @block.tensor
            def _(pe):
                def step(t, slot):
                    pe.wait_ge(oh_made, t + 1)
                    if not (isinstance(t, int) and t < 2):
                        pe.wait_ge(tab_read, t - 1)
                    for c in range(CMAX):
                        mm = pe.matmul(bank[4 * slot][:, c * TABW:(c + 1) * TABW], onehot[:, slot, c * P:(c + 1) * P],
                                       table[:, bass.ds(t, 1), :].rearrange("p a n -> p (a n)"), start=True, stop=True)
                    mm.then_inc(tab_ready, 1)
                    pe.wait_ge(end_made, t + 1)
                    if not (isinstance(t, int) and t == 0):
                        pe.wait_ge(start_made, t)
                    for k in range(3):
                        lo, hi = k * 512, min((k + 1) * 512, EMAX)
                        mm = pe.matmul(bank[1 + k][0:1, 0:hi - lo], ones[:, 0:1], nz[:, lo:hi], start=True, stop=True)
                    mm.then_inc(start_ready, 1)

                step(0, 0)
                step(1, 1)
                with pe.Fori(1, RT // 2) as i:
                    for slot in range(2):
                        step(2 * i + slot, slot)

            @block.sync
            def _(sp):
                with sp.Fori(0, RT // 2) as i:
                    for slot in range(2):
                        sp.wait_ge(start_made, 2 * i + slot + 1)
                        sp.dma_start(starts[bass.ds(2 * i + slot, 1), :], start_row[0:1, slot, :]).then_inc(start_out[slot], 16)
                for slot in range(2):
                    sp.wait_ge(start_out[slot], 16 * (RT // 2))

            @block.vector
            def _(v):
                ch = Chain(v, dv)
                v.wait_ge(k64_made, 1)
                v.memset(start_row[0:1, :, :], -BIG).then_inc(start_clear, 1)

                def one_hot(t, slot):
                    row = lambda x: x[:, bass.ds(t, 1), 0]
                    if not (isinstance(t, int) and t < 2):
                        v.wait_ge(tab_ready, t - 1)
                        v.wait_ge(oh_kept, t - 1)
                    if not (isinstance(t, int) and t == 0):
                        v.wait_ge(oh_made, t)
                    ch.link(v.tensor_scalar(ge, iota_e, row(row_from), None, ALU.is_ge))
                    v.scalar_tensor_tensor(onehot[:, slot, :], iota_e, row(row_to), ge, ALU.is_lt, ALU.mult).then_inc(oh_made, 1)
                    if not (isinstance(t, int) and t == 0):
                        v.wait_ge(start_ready, t)
                    v.tensor_scalar(nz[:, 0:EMAX], iota_e, row(row_to), None, ALU.is_equal).then_inc(end_made, 1)

                def find_block(t, slot):
                    v.wait_ge(tab_ready, t + 1)
                    if not (isinstance(t, int) and t == 0):
                        v.wait_ge(gidx_ready, t)
                    v.tensor_copy(tab, bank[4 * slot][:, 0:CMAX * TABW].rearrange("p (c n) -> p c n", c=CMAX)).then_inc(tab_read, 1)
                    v.wait_ge(tab_read, t + 1)
                    ch.link(v.tensor_tensor(rank, edge_id[:], tab[:, :, COL_OFS], ALU.subtract))
                    over32 = lambda x: x.rearrange("p (c a) -> p c a", a=1).broadcast_to([P, CMAX, NBLK])
                    ch.link(v.tensor_tensor(le, tab[:, :, 0:NBLK], over32(rank), ALU.is_le))
                    ch.link(v.tensor_tensor(part, tab[:, :, 0:NBLK], le, ALU.mult))
                    ch.link(v.tensor_reduce(base, part, AX.X, ALU.max))
                    ch.link(v.tensor_reduce(blk, le, AX.X, ALU.add))
                    v.tensor_tensor(rank2[:, slot, :], rank, base, ALU.subtract)
                    if not (isinstance(t, int) and t < 2):
                        v.wait_ge(select_kept, t)
                    v.tensor_scalar(minus_row[:, slot, :], tab[:, :, COL_LOC], -1.0, 1.0, ALU.mult, ALU.add)
                    ch.link(v.tensor_scalar(blk, blk, float(NBLK - 1), None, ALU.min))
                    v.tensor_scalar(blk_base[:, slot, :], blk, float(BLK), None, ALU.mult)
                    v.scalar_tensor_tensor(gidx[:, slot, :], tab[:, :, COL_ROW], float(NBLK), blk, ALU.mult, ALU.add
                                           ).then_inc(gidx_ready, 1)

                def find_column(t, slot, half):
                    v.wait_ge(blk_in[slot], 16 * CMAX * (half + 1))
                    ch.link(v.tensor_scalar(nzb, ablk[:, slot], 0, None, ALU.not_equal))
                    flat = lambda x: x.rearrange("p c j -> p (c j)")
                    ch.link(v.tensor_tensor_scan(flat(cumb), keep64, flat(nzb), 0.0, ALU.mult, ALU.add))
                    over64 = lambda x: x.rearrange("p (c a) -> p c a", a=1).broadcast_to([P, CMAX, BLK])
                    ch.link(v.tensor_tensor(leb, cumb, over64(rank2[:, slot, :]), ALU.is_le))
                    ch.link(v.tensor_reduce(inner, leb, AX.X, ALU.add))
                    ch.link(v.tensor_tensor(col, inner, blk_base[:, slot, :], ALU.add))
                    v.tensor_scalar(neighbour[:, bass.ds(t, 1), :], col.rearrange("p (a c) -> p a c", a=1), float(N - 1), None, ALU.min)

                one_hot(0, 0)
                one_hot(1, 1)
                find_block(0, 0)
                with v.Fori(0, RT // 2 - 1) as i:
                    ch.loop(i, 2 * (1 + 6 + 5))
                    for slot in range(2):
                        find_block(2 * i + 1 + slot, 1 - slot)
                        one_hot(2 * i + 2 + slot, slot)
                        find_column(2 * i + slot, slot, i)
                ch.end(RT // 2 - 1)
                find_block(RT - 1, 1)
                find_column(RT - 2, 0, RT // 2 - 1)
                find_column(RT - 1, 1, RT // 2 - 1)

        for L in range(layers):
            x_rows = given_rows if L == 0 else kept_rows
            y_rows = result_rows if L == layers - 1 else kept_rows
            sems.renew()
            if L > 0 and KINDS[L - 1] == "tf":
                mine = projection(L, x_rows)
                with nc.Block() as block:
                    @block.sync
                    def _(sp):
                        mine.sync(sp)

                    @block.tensor
                    def _(pe):
                        mine.tensor(pe)

                    @block.scalar
                    def _(act):
                        mine.scalar(act)

                    if KINDS[L] == "tf":
                        @block.vector
                        def _(v):
                            mine.vector(v)
                sems.renew()
            attend(nc, sem, carve, bank, pair, KINDS[L], L, neighbour, spread_bits, select_bits, ident,
                   starts, qq, kk, vv, si, sj, ao, fits, ones, adj_by_row, tile_rows)
            sems.renew()
            if KINDS[L] == "gat":
                weave = (lambda made: projection(L + 1, None, made)) if L + 1 < layers else None
                post_gat(nc, sem, carve, bank, w[L], L, ident, eps_col, x_rows, ao, y_rows, weave)
            else:
                post_tf(nc, sem, carve, bank, w[L], L, ident, eps_col, x_rows, ao, y_rows)
        sems.renew()
        return nc


class Projection:

    def __init__(self, turned, store, all_stored, copy_turned, sync=None, tensor=None, scalar=None, vector=None,
                 evacuate_a=None, evacuate_v=None):
        self.turned, self.store, self.all_stored, self.copy_turned = turned, store, all_stored, copy_turned
        self.sync, self.tensor, self.scalar, self.vector = sync, tensor, scalar, vector
        self.evacuate_a, self.evacuate_v = evacuate_a, evacuate_v


def project(nc, sem, carve, bank, pair, w, kind, L, ident, tile_rows, x_rows, qq, kk_by_row, vv_by_row, si, sj_by_row,
            made=None):
    tf = kind == "tf"
    _, x_tile, x_turned, stage, small, w_turned = carve((APART,), (2, BD), (2, 4 * D), (2, 3, BD), (2, 2 * B), (D,))
    if made:
        x_tile, tiles_made = made
    x_in = [sem(f"x_in{L}{s}") for s in range(2)]
    turned, x_copied, product = sem(f"turned{L}"), sem(f"x_copied{L}"), sem(f"product{L}")
    evac_v, evac_a = sem(f"evac_v{L}"), sem(f"evac_a{L}")
    out_sem = [sem(f"staged_out{L}{s}") for s in range(2)]
    wt, wt_copied, wa = sem(f"wt{L}"), sem(f"wt_copied{L}"), sem(f"wa{L}")
    stores = 5
    GROUPS = 2 * RT

    def store(sp, t, slot):
        if tf:
            sp.wait_ge(evac_v, 4 * (t + 1))
        sp.wait_ge(evac_a, (4 if tf else 2) * (t + 1))
        if tf:
            sp.dma_start(qq[bass.ds(t, 1)].rearrange("r q n -> q r n"), stage[:, slot, 0:1, :]).then_inc(out_sem[slot], 16)
            pieces = [(kk_by_row, stage[:, slot, 1, :]), (vv_by_row, stage[:, slot, 2, :])]
        else:
            sp.dma_start(si[bass.ds(t, 1)].rearrange("r q n -> q r n"), small[:, slot:slot + 1, 0:B]).then_inc(out_sem[slot], 16)
            pieces = [(vv_by_row, stage[:, slot, 2, :]), (sj_by_row, small[:, slot, B:2 * B])]
        for view, src in pieces:
            for dst, lo, hi in zip(tile_rows(view, t), (0, 1), (1, P)):
                sp.dma_start(dst.rearrange("r q n -> (r q) n"), src[lo:hi]).then_inc(out_sem[slot], 16)

    def all_stored(sp):
        for slot in range(2):
            sp.wait_ge(out_sem[slot], 16 * stores * (RT // 2))

    def sync(sp):
        def load(t, slot):
            for src, lo, hi in x_rows(t):
                dst = x_tile[lo:hi, slot, :]
                sp.dma_start(dst if len(src.shape) == 2 else dst.rearrange("p (b d) -> p b d", b=B), src).then_inc(x_in[slot], 16)

        load(0, 0)
        load(1, 1)
        with sp.Fori(0, RT // 2 - 1) as i:
            for slot in range(2):
                sp.wait_ge(turned, 2 * (2 * i + slot) + 2)
                load(2 * i + slot + 2, slot)
                store(sp, 2 * i + slot, slot)
        store(sp, RT - 2, 0)
        store(sp, RT - 1, 1)
        all_stored(sp)

    def tensor(pe):
        if not tf:
            pe.transpose(bank[6][:, 0:D], w["w"][:, 0:D], ident[:]).then_inc(wt, 1)
            pe.wait_ge(wt_copied, 1)
            pe.matmul(bank[7][:, 0:2], w_turned, w["av"][:], start=True, stop=True).then_inc(wt, 1)
            pe.wait_ge(wa, 1)

        def turn(n, k, turn_no):
            slot, half = (k // 2) % 2, k % 2
            if k % 2 == 0 and made:
                pe.wait_ge(tiles_made, 2 * turn_no + slot + 1)
            elif k % 2 == 0:
                pe.wait_ge(x_in[slot], 16 * len(x_rows(0)) * (turn_no + 1))
            if not (isinstance(n, int) and n < 2):
                pe.wait_ge(x_copied, n - 1)
            for b in range(4):
                at = (4 * half + b) * D
                tr = pe.transpose(bank[half][:, b * P:(b + 1) * P], x_tile[:, slot, at:at + D], ident[:])
            tr.then_inc(turned, 1)

        def multiply(n, k):
            half = k % 2
            pe.wait_ge(x_copied, n + 1)
            for b in range(4):
                lhs = x_turned[:, half, b * P:(b + 1) * P]
                if tf:
                    if not (isinstance(n, int) and n == 0):
                        pe.wait_ge(evac_a if b % 2 else evac_v, 2 * n - 1 + b // 2)
                    pe.matmul(bank[2 + b][:, 0:3 * D], lhs, w["qkv"][:], start=True, stop=True).then_inc(product, 1)
                else:
                    if b == 0 and not (isinstance(n, int) and n < 2):
                        pe.wait_ge(evac_a, n - 1)
                    at = 512 * (b // 2) + (D + 2) * (b % 2)
                    mm = pe.matmul(pair[1 + half][:, at:at + D + 2], lhs, w["w"][:], start=True, stop=True)
            if not tf:
                mm.then_inc(product, 1)

        turn(0, 0, 0)
        for k in range(4):
            turn(k + 1, k + 1 if k < 3 else 0, 0 if k < 3 else 1)
            multiply(k, k)
        with pe.Fori(1, RT // 2 - 1) as i:
            for k in range(4):
                turn(4 * i + k + 1, (k + 1) % 4, i if k < 3 else i + 1)
                multiply(4 * i + k, k)
        for k in range(4):
            n = GROUPS - 4 + k
            if k < 3:
                turn(n + 1, k + 1, RT // 2 - 1)
            multiply(n, k)

    def products(half):
        return pair[1 + half][:].rearrange("p (k n) -> p k n", k=2)[:, :, 0:2 * (D + 2)].rearrange("p k (j m) -> p k j m", j=2)

    def evacuate(eng, copy, n, k, done, uses, first):
        slot, half = (k // 2) % 2, k % 2
        mine = 1 if eng is nc.scalar else 0
        if tf:
            for b in (mine, mine + 2):
                eng.wait_ge(product, 4 * n + b + 1)
                if not first and half == 0 and b < 2:
                    eng.wait_ge(out_sem[slot], 16 * stores * uses)
                at = (4 * half + b) * D
                copy(stage[:, slot, :, at:at + D], bank[2 + b][:, 0:3 * D].rearrange("p (m d) -> p m d", m=3)).then_inc(done, 1)
        else:
            eng.wait_ge(product, n + 1)
            if not first:
                eng.wait_ge(out_sem[slot], 16 * stores * uses)
            for m in range(2):
                copy(small[:, slot, m * B + 4 * half:m * B + 4 * half + 4].rearrange("p (k j) -> p k j", k=2),
                     products(half)[:, :, :, D + m])
            copy(stage[:, slot, 2, half * 4 * D:(half + 1) * 4 * D].rearrange("p (k j d) -> p k j d", k=2, j=2),
                 products(half)[:, :, :, 0:D]).then_inc(done, 1)

    def copy_turned(act, n, k):
        act.wait_ge(turned, n + 1)
        if not (isinstance(n, int) and n < 2):
            act.wait_ge(product, (4 if tf else 1) * (n - 1))
        act.copy(x_turned[:, k % 2, :], bank[k % 2]).then_inc(x_copied, 1)

    def scalar(act):
        if not tf:
            act.wait_ge(wt, 1)
            act.copy(w_turned, bank[6][:, 0:D]).then_inc(wt_copied, 1)
            act.wait_ge(wt, 2)
            act.copy(w["w"][:, D:D + 2], bank[7][:, 0:2]).then_inc(wa, 1)

        copy_turned(act, 0, 0)
        for k in range(4):
            copy_turned(act, k + 1, k + 1)
            evacuate(act, act.copy, k, k, evac_a, 0, True)
        with act.Fori(1, RT // 2 - 1) as i:
            for k in range(4):
                copy_turned(act, 4 * i + k + 1, k + 1)
                evacuate(act, act.copy, 4 * i + k, k, evac_a, i, False)
        for k in range(4):
            n = GROUPS - 4 + k
            if k < 3:
                copy_turned(act, n + 1, k + 1)
            evacuate(act, act.copy, n, k, evac_a, RT // 2 - 1, False)

    def vector(v):
        def turn(n, k, t, uses, first):
            evacuate(v, v.tensor_copy, n, k, evac_v, uses, first)

        for k in range(4):
            turn(k, k, k // 2, 0, True)
        with v.Fori(1, RT // 2) as i:
            for k in range(4):
                turn(4 * i + k, k, 2 * i + k // 2, i, False)

    return Projection(sync=sync, tensor=tensor, scalar=scalar, vector=vector, store=store, all_stored=all_stored,
                      copy_turned=copy_turned, turned=turned,
                      evacuate_a=lambda n, k, uses, first: evacuate(nc.scalar, nc.scalar.copy, n, k, evac_a, uses, first),
                      evacuate_v=lambda n, k, uses, first: evacuate(nc.vector, nc.vector.tensor_copy, n, k, evac_v, uses, first))


def attend(nc, sem, carve, bank, pair, kind, L, neighbour, spread_bits, select_bits, ident,
           starts, qq, kk, vv, si, sj, ao, fits, ones, adj_by_row, tile_rows):
    by_edge = attend_by_edge(nc, sem, carve, bank, pair, kind, L, neighbour, spread_bits, select_bits, ident,
                             starts, qq, kk, vv, si, sj, ao)
    dense = attend_dense(nc, sem, carve, bank, pair, kind, L, ident, qq, kk, vv, si, sj, ao, ones, adj_by_row, tile_rows)

    def either(eng, edge_program, dense_program):
        fit = eng.value_load(fits[0:1, 0:1], min_val=0, max_val=1)
        with eng.If(fit == 1):
            edge_program(eng)
        with eng.Else():
            dense_program(eng)

    with nc.Block() as block:
        @block.gpsimd
        def _(g):
            either(g, by_edge[0], dense[0])

        @block.sync
        def _(sp):
            either(sp, by_edge[1], dense[1])

        @block.tensor
        def _(pe):
            either(pe, by_edge[2], dense[2])

        @block.scalar
        def _(act):
            either(act, by_edge[3], dense[3])

        @block.vector
        def _(v):
            either(v, by_edge[4], dense[4])


def attend_dense(nc, sem, carve, bank, pair, kind, L, ident, qq, kk, vv, si, sj, ao, ones, adj_by_row, tile_rows):
    tf = kind == "tf"
    H = HEADS if tf else 1
    W = D // H
    SCALE = float(HD) ** -0.5 if tf else 1.0
    KT = N // P
    (keys, values, keys_turned, masked, probs, probs_turned, bias, adj_rows, q_tile, q_heads, o_stage, head_mask, top,
     shift, den, q_pair, k_pair) = carve((KT, D), (KT, D), (N,), (N,), (N,), (N,), (N,), (N,), (D,), (HEADS, P), (D,),
                                         (HEADS,), (1,), (1,), (1,), (P,), (N,))
    adj_rows = adj_rows.bitcast(I32)
    new = lambda name: sem(f"{name}{L}")
    made, adj_in, kv_in, bias_made = new("d_made"), new("d_adj_in"), new("d_kv_in"), new("d_bias")
    k_tr, k_copied, q_tr, q_masked = new("d_k_tr"), new("d_k_copied"), new("d_q_tr"), new("d_q_masked")
    scored, read, biased, topped, shifted = new("d_scored"), new("d_read"), new("d_biased"), new("d_topped"), new("d_shifted")
    raised, p_tr, p_copied, summed = new("d_exp"), new("d_p_tr"), new("d_p_copied"), new("d_summed")
    den_step, o_made, o_out = new("d_den"), new("d_o"), new("d_o_out")
    loads = 3

    def tiles(eng, per_tile, per_batch):
        with eng.Fori(0, RT) as t:
            per_tile(t)
            with eng.Fori(0, B) as b:
                per_batch(t, b, B * t + b)

    nothing = lambda t: None

    def gpsimd(g):
        g.affine_select(out=head_mask, in_=ones[:, 0:HEADS], compare_op=ALU.is_ge, fill=0.0, base=0,
                        pattern=[[-HD, HEADS]], channel_multiplier=1).then_inc(made, 1)
        g.wait_ge(made, 1)
        g.affine_select(out=head_mask, in_=head_mask, compare_op=ALU.is_ge, fill=0.0, base=HD - 1,
                        pattern=[[HD, HEADS]], channel_multiplier=-1)
        g.memset(q_pair[0:2, :], 1.0)
        g.memset(k_pair[0:2, :], 1.0).then_inc(made, 1)
        g.sem_inc(o_made, 1)
        g.sem_inc(p_copied, 1)
        g.sem_inc(raised, 1)
        g.sem_inc(o_out, 16)

    def sync(sp):
        sp.wait_ge(made, 2)

        def per_tile(t):
            sp.wait_ge(o_made, H * B * t + 1)
            for src, lo, hi in zip(tile_rows(adj_by_row, t), (0, 1), (1, P)):
                sp.dma_start(adj_rows[lo:hi, :], src.rearrange("r q n -> (r q) n")).then_inc(adj_in, 16)

        def per_batch(t, b, m):
            sp.wait_ge(o_made, H * m + 1)
            cols = bass.ds(b * D, D)
            by_tile = lambda x: x.rearrange("(k p) n -> p k n", p=P)
            sp.dma_start(values, by_tile(vv)[:, :, cols]).then_inc(kv_in, 16)
            if tf:
                sp.dma_start(keys, by_tile(kk)[:, :, cols]).then_inc(kv_in, 16)
                sp.dma_start(q_tile, qq[bass.ds(t, 1), :, cols].rearrange("r q n -> (r q) n")).then_inc(kv_in, 16)
            else:
                sp.dma_start(k_pair[1:2, :], sj.rearrange("n b -> b n")[bass.ds(b, 1), :], allow_slow_non_contiguous=True
                             ).then_inc(kv_in, 16)
                sp.dma_start(q_pair[0:1, :], si.rearrange("r q b -> r b q")[bass.ds(t, 1), bass.ds(b, 1), :].rearrange("r b q -> (r b) q"),
                             allow_slow_non_contiguous=True).then_inc(kv_in, 16)
            sp.wait_ge(o_made, H * (m + 1) + 1)
            sp.dma_start(ao[bass.ds(t, 1), :, cols].rearrange("r q n -> (r q) n"), o_stage).then_inc(o_out, 16)
        tiles(sp, per_tile, per_batch)
        sp.wait_ge(o_out, 16 * RT * B + 16)

    def tensor(pe):
        def per_batch(t, b, m):
            hold(pe, kv_in, 16 * loads * (m + 1))
            if tf:
                hold(pe, p_copied, 2 * H * m + 1)
                for k in range(KT):
                    tr = pe.transpose(bank[k // 4][:, (k % 4) * P:(k % 4 + 1) * P], keys[:, k, :], ident[:])
                tr.then_inc(k_tr, 1)
                pe.transpose(bank[5][:, 0:P], q_tile, ident[:]).then_inc(q_tr, 1)
            for h in range(H):
                n = H * m + h
                if tf:
                    pe.wait_ge(k_copied, 2 * m + 2)
                    pe.wait_ge(q_masked, m + 1)
                hold(pe, p_copied, 2 * n + 1)
                for k in range(4):
                    if tf:
                        mm = pe.matmul(bank[k], q_heads[:, h, :], keys_turned[:, k * 512:(k + 1) * 512], start=True, stop=True)
                    else:
                        mm = pe.matmul(bank[k], q_pair[0:2, :], k_pair[0:2, k * 512:(k + 1) * 512], start=True, stop=True)
                mm.then_inc(scored, 1)
                hold(pe, raised, n + 2)
                for k in range(KT):
                    tr = pe.transpose(bank[k // 4][:, (k % 4) * P:(k % 4 + 1) * P], probs[:, k * P:(k + 1) * P], ident[:])
                tr.then_inc(p_tr, 1)
                pe.wait_ge(o_made, n + 1)
                hold(pe, p_copied, 2 * n + 3)
                for k in range(KT):
                    mm = pe.matmul(bank[4][:, 0:W], probs_turned[:, k * P:(k + 1) * P], values[:, k, h * W:(h + 1) * W],
                                   start=(k == 0), stop=(k == KT - 1))
                mm.then_inc(summed, 1)
        tiles(pe, nothing, per_batch)

    def scalar(act):
        def per_batch(t, b, m):
            if tf:
                act.wait_ge(k_tr, m + 1)
                for k in range(2):
                    act.copy(keys_turned[:, k * 1024:(k + 1) * 1024], pair[k][:]).then_inc(k_copied, 1)
            for h in range(H):
                n = H * m + h
                if not tf:
                    act.wait_ge(scored, n + 1)
                    for k in range(2):
                        act.copy(masked[:, k * 1024:(k + 1) * 1024], pair[k][:]).then_inc(read, 1)
                act.wait_ge(shifted, n + 1)
                act.wait_ge(o_made, n + 1)
                act.activation(probs, masked, ACT.Exp, bias=shift, scale=SCALE, accum_out=den).then_inc(raised, 1)
                act.wait_ge(p_tr, n + 1)
                for k in range(2):
                    act.copy(probs_turned[:, k * 1024:(k + 1) * 1024], pair[k][:]).then_inc(p_copied, 1)
        tiles(act, nothing, per_batch)

    def vector(v):
        v.wait_ge(made, 2)

        def per_tile(t):
            v.wait_ge(adj_in, 32 * t + 32)
            v.wait_ge(o_made, H * B * t + 1)
            v.tensor_scalar(bias, adj_rows, 0, -BIG, ALU.is_equal, ALU.mult).then_inc(bias_made, 1)
            hold(v, bias_made, t + 1)

        def per_batch(t, b, m):
            if tf:
                v.wait_ge(q_tr, m + 1)
                v.tensor_tensor(q_heads, bank[5][:, 0:P].rearrange("p (a q) -> p a q", a=1).broadcast_to([P, HEADS, P]),
                                head_mask.rearrange("p (h a) -> p h a", a=1).broadcast_to([P, HEADS, P]), ALU.mult
                                ).then_inc(q_masked, 1)
            for h in range(H):
                n = H * m + h
                if tf:
                    v.wait_ge(scored, n + 1)
                    v.wait_ge(raised, n + 1)
                    for k in range(2):
                        cols = slice(k * 1024, (k + 1) * 1024)
                        v.tensor_tensor(masked[:, cols], pair[k][:], bias[:, cols], ALU.add).then_inc(biased, 1)
                    v.wait_ge(biased, 2 * n + 2)
                else:
                    v.wait_ge(read, 2 * n + 2)
                    v.scalar_tensor_tensor(masked, masked, SLOPE, masked, ALU.mult, ALU.max).then_inc(biased, 1)
                    v.wait_ge(biased, 2 * n + 1)
                    v.tensor_tensor(masked, masked, bias, ALU.add).then_inc(biased, 1)
                    v.wait_ge(biased, 2 * n + 2)
                v.tensor_reduce(top, masked, AX.X, ALU.max).then_inc(topped, 1)
                v.wait_ge(topped, n + 1)
                v.tensor_scalar(shift, top, -BIG / 2, -SCALE, ALU.max, ALU.mult).then_inc(shifted, 1)
                v.wait_ge(raised, n + 2)
                v.tensor_scalar(den, den, TINY, None, ALU.max).then_inc(den_step, 1)
                v.wait_ge(den_step, 2 * n + 1)
                v.reciprocal(den, den).then_inc(den_step, 1)
                v.wait_ge(den_step, 2 * n + 2)
                v.wait_ge(summed, n + 1)
                if h == 0:
                    v.wait_ge(o_out, 16 * m + 16)
                v.tensor_scalar(o_stage[:, h * W:(h + 1) * W], bank[4][:, 0:W], den, None, ALU.mult).then_inc(o_made, 1)
        tiles(v, per_tile, per_batch)

    return gpsimd, sync, tensor, scalar, vector


def attend_by_edge(nc, sem, carve, bank, pair, kind, L, neighbour, spread_bits, select_bits, ident,
                   starts, qq, kk, vv, si, sj, ao):
    tf = kind == "tf"
    G = B * HEADS if tf else B
    W = BD // G
    SCALE = float(HD) ** -0.5 if tf else 1.0
    K_RING, V_RING = (5, 5) if tf else (0, 10)
    WEIGHTED = 5
    LATE = 2 if tf else 3
    Q_PARTS = 3
    BY_POOL = (2, 5, 7) if tf else ()
    CHUNK = CMAX - CREST // 2
    (q_tile, q_parts, k_ring, v_ring, prod, weighted_v, o_stage, spread, select, score, row_start, turned, row_max, prob, den,
     idx_k, idx_v, sj_edge, raw) = carve(
        (1 if tf else 2, BD), (2, Q_PARTS, BD // 2 if tf else 1), (max(K_RING, 1), BD if tf else 1), (V_RING, BD),
        (2, BD if tf else 1), (WEIGHTED, BD), (2, BD), (2, CHUNK, P // 2 if tf else P), (2, CHUNK, P), (CMAX, G),
        (EMAX + P,), (EMAX,), (EMAX,), (2, CMAX, G), (G,), (2, CMAX), (2, CMAX), (2, CMAX, 1 if tf else G), (CMAX, B))
    if tf:
        q_parts, spread = q_parts.bitcast(BF16), spread.bitcast(BF16)
    idx_k, idx_v = idx_k.bitcast(I32), idx_v.bitcast(I32)
    new = lambda name: sem(f"{name}{L}")
    q_in = [new("q_in0_"), new("q_in1_")]
    k_landed = [new(f"k_landed{r}_") for r in range(K_RING)]
    v_landed = [new(f"v_landed{r}_") for r in range(V_RING)]
    sj_in = [new("sj_in0_"), new("sj_in1_")]
    q_high, q_rest, q_mid, q_split = new("q_high"), new("q_rest"), new("q_mid"), new("q_split")
    start_in, idx_k_made, idx_v_made = new("start_in"), new("idx_k_made"), new("idx_v_made")
    spread_made, spread_q, prod_made, score_made = new("spread_made"), new("spread_q"), new("prod_made"), new("score_made")
    raw_made = new("raw_made")
    tp_full, tp_read = new("tp_full"), new("tp_read")
    scan_fwd, scan_back, shifted, prob_ready = new("scan_fwd"), new("scan_back"), new("shifted"), new("prob_ready")
    select_made, weighed_v, weighed_g, summed = new("select_made"), new("weighed_v"), new("weighed_g"), new("summed")
    den_step, o_ready, o_out = new("den_step"), new("o_ready"), [new("o_out0_"), new("o_out1_")]
    zero = lambda t: isinstance(t, int) and t == 0
    g0 = first_edge_tile
    GROUP_S, GROUP_P = 4, 8

    sums_at = lambda par: pair[2] if tf else pair[1 + par]
    den_at = lambda par: bank[7][:, 0:G] if tf else bank[(1, 7)[par]][:, 0:G]

    def has(t, lag=0):
        return not isinstance(t, int) or 0 <= t - lag < RT

    def cut(t):
        return CHUNK if zero(t) else CREST // 2

    def slot_of(t, c, ring):
        if zero(t):
            return c % ring, c // ring
        return (CMAX + c) % ring, (CREST // ring) * (t - 1) + (CMAX + c) // ring

    def weighed(t, c):
        by_pool = sum(x <= c for x in BY_POOL)
        if c in BY_POOL:
            return weighed_g, len(BY_POOL) * t + by_pool
        before = 0 if zero(t) else CMAX - CREST + (CREST - len(BY_POOL)) * t
        return weighed_v, before + c + 1 - by_pool

    def hold_weighed(eng, t, c):
        hold(eng, *weighed(t, c))

    def hold_all_weighed(eng, t):
        last = edge_tiles(t) - 1
        assert last not in BY_POOL
        hold_weighed(eng, t, last)
        if BY_POOL:
            hold_weighed(eng, t, BY_POOL[-1])

    def weigh(eng, t, c, par, done):
        slot, (v_slot, used) = slot_of(t, c, WEIGHTED)[0], slot_of(t, c, V_RING)
        if c == 0 or c == min(BY_POOL, default=0):
            eng.wait_ge(tp_read, turn_of_probs(t, 1))
        if not (zero(t) and c < WEIGHTED):
            eng.wait_ge(summed, g0(t) + c - WEIGHTED + 1)
        eng.wait_ge(v_landed[v_slot], 16 * used + 16)
        eng.tensor_tensor(weighted_v[:, slot, :].rearrange("p (g w) -> p g w", w=W),
                          v_ring[:, v_slot, :].rearrange("p (g w) -> p g w", w=W),
                          prob[:, par, c, :].rearrange("p (g a) -> p g a", a=1).broadcast_to([P, G, W]), ALU.mult
                          ).then_inc(done, 1)

    def steps(eng, step):
        for t in range(6):
            step(t, t % 2, t // 2)
        with eng.Fori(3, RT // 2 - 1) as i:
            step(2 * i, 0, i)
            step(2 * i + 1, 1, i)
        for t in range(RT - 2, RT + LATE):
            step(t, t % 2, t // 2)

    def turn_of_scores(t, k):
        return 5 * t + 1 + k

    def turn_of_probs(t, m):
        return 5 * t + 4 + m

    def width(t):
        return max(edge_tiles(t) if has(t) else 0, edge_tiles(t - 2) if has(t, 2) else 0)

    def gpsimd(g):
        def step(t, par, half):
            where = lambda idx, c: bass.IndirectOffsetOnAxis(ap=idx[:, par, c:c + 1], axis=0)
            if has(t):
                if has(t, 2):
                    if tf:
                        hold(g, prod_made, g0(t - 1))
                    else:
                        hold(g, raw_made, t - 1)
                g.tensor_copy(idx_k[:, par:par + 1, :], neighbour[:, bass.ds(t, 1), :]).then_inc(idx_k_made, 1)
                hold(g, idx_k_made, t + 1)
            if has(t, 2):
                if has(t, 4):
                    hold_all_weighed(g, t - 4)
                g.tensor_copy(idx_v[:, par:par + 1, :], neighbour[:, bass.ds(t - 2, 1), :]).then_inc(idx_v_made, 1)
                hold(g, idx_v_made, t - 1)
            for c in range(width(t)):
                if tf and has(t, -1) and c == 4:
                    rest(t + 1, 1 - par)
                if tf and has(t, -1) and c == 6:
                    low(t + 1, 1 - par)
                if has(t) and c < edge_tiles(t):
                    if tf:
                        slot, _ = slot_of(t, c, K_RING)
                        if not (zero(t) and c < K_RING):
                            hold(g, prod_made, g0(t) + c - K_RING + 1)
                        g.indirect_dma_start(out=k_ring[:, slot, :], out_offset=None, in_=kk, in_offset=where(idx_k, c)
                                             ).then_inc(k_landed[slot], 16)
                    else:
                        g.indirect_dma_start(out=sj_edge[:, par, c, :], out_offset=None, in_=sj, in_offset=where(idx_k, c)
                                             ).then_inc(sj_in[par], 16)
                if has(t, 2) and c < edge_tiles(t - 2):
                    u = t - 2
                    slot, _ = slot_of(u, c, V_RING)
                    if c >= V_RING:
                        hold_weighed(g, u, c - V_RING)
                    elif not zero(u):
                        hold_weighed(g, u - 1, c - V_RING + edge_tiles(u - 1))
                    g.indirect_dma_start(out=v_ring[:, slot, :], out_offset=None, in_=vv, in_offset=where(idx_v, c)
                                         ).then_inc(v_landed[slot], 16)
                if has(t, 2) and c - 2 in BY_POOL:
                    weigh(g, t - 2, c - 2, par, weighed_g)

        def rest(t, par):
            g.wait_ge(q_high, t + 1)
            g.tensor_tensor(q_tile[:, 0, :], q_tile[:, 0, :], q_parts[:, par, 0, :], ALU.subtract).then_inc(q_rest, 1)

        def low(t, par):
            g.wait_ge(q_mid, t + 1)
            g.tensor_tensor(q_parts[:, par, 2, :], q_tile[:, 0, :], q_parts[:, par, 1, :], ALU.subtract).then_inc(q_split, 1)

        if tf:
            rest(0, 0)
            low(0, 0)
        steps(g, step)

    def sync(sp):
        def load_q(t, par):
            dst, src = (q_tile[:, 0, :], qq) if tf else (q_tile[:, par, 0:B], si)
            sp.dma_start(dst, src[bass.ds(t, 1)].rearrange("r q n -> (r q) n")).then_inc(q_in[0 if tf else par], 16)

        def store(t, par):
            sp.wait_ge(o_ready, t + 1)
            sp.dma_start(ao[bass.ds(t, 1)].rearrange("r q n -> (r q) n"), o_stage[:, par, :]).then_inc(o_out[par], 16)

        def step(t, par, half):
            if has(t, -1):
                if tf:
                    sp.wait_ge(q_split, t + 1)
                elif has(t, 1):
                    sp.wait_ge(spread_q, g0(t))
                load_q(t + 1, 1 - par)
            if has(t, LATE + 1):
                store(t - LATE - 1, (par + LATE + 1) % 2)
            if has(t):
                if has(t, 1):
                    sp.wait_ge(scan_back, t)
                sp.dma_start(row_start[0:G, :], starts[bass.ds(t, 1), :].broadcast_to([G, EMAX + P])).then_inc(start_in, 16)

        load_q(0, 0)
        steps(sp, step)
        store(RT - 1, 1)
        for s in range(2):
            sp.wait_ge(o_out[s], 16 * (RT // 2))

    def tensor(pe):
        def turn_scores(t, k):
            lo, hi = k * GROUP_S, min((k + 1) * GROUP_S, edge_tiles(t))
            pe.wait_ge(score_made, g0(t) + hi if tf else t + 1)
            if not (zero(t) and k == 0):
                hold(pe, tp_read, turn_of_scores(t, k) - 1)
            for c in range(lo, hi):
                tr = pe.transpose(bank[6][0:G, (c - lo) * P:(c - lo + 1) * P], score[:, c, :], ident[:])
            tr.then_inc(tp_full, 1)

        def turn_probs(t, m):
            lo, hi = m * GROUP_P, min((m + 1) * GROUP_P, edge_tiles(t))
            pe.wait_ge(prob_ready, t + 1)
            hold(pe, tp_read, turn_of_probs(t, m) - 1)
            for c in range(lo, hi):
                tr = pe.transpose(bank[6][:, (c - lo) * G:(c - lo + 1) * G], turned[0:G, c * P:(c + 1) * P], ident[0:G, 0:G])
            tr.then_inc(tp_full, 1)

        def spread_queries(t, c, par, half):
            h = int(c >= cut(t))
            if c == 0:
                if tf:
                    pe.wait_ge(q_split, t + 1)
                else:
                    pe.wait_ge(q_in[par], 16 * half + 16)
            if c in (0, cut(t)):
                pe.wait_ge(spread_made, 2 * t + h + 1)
            lhs = spread[:, h, c - h * cut(t), :]
            if tf:
                slot = slot_of(t, c, 2)[0]
                if not (zero(t) and c < 2):
                    pe.wait_ge(prod_made, g0(t) + c - 1)
                for k in range(2):
                    for part in range(Q_PARTS):
                        mm = pe.matmul(pair[slot][:, k * 512:(k + 1) * 512], lhs, q_parts[:, par, part, k * 512:(k + 1) * 512],
                                       start=(part == 0), stop=(part == Q_PARTS - 1))
                mm.then_inc(spread_q, 1)
            else:
                if c == 0 and has(t, 1):
                    pe.wait_ge(raw_made, t)
                pe.matmul(bank[0][:, c * B:(c + 1) * B], lhs, q_tile[:, par, 0:B], start=True, stop=True).then_inc(spread_q, 1)

        def sum_values(t, c, par):
            h = int(c >= cut(t))
            if c == 0 and has(t, LATE - 1):
                pe.wait_ge(o_ready, t - LATE + 2)
            if c in (0, cut(t)):
                pe.wait_ge(select_made, 2 * t + h + 1)
            pe.wait_ge(*weighed(t, c))
            slot = slot_of(t, c, WEIGHTED)[0]
            lhs = select[:, h, c - h * cut(t), :]
            ends = dict(start=(c == 0), stop=(c == edge_tiles(t) - 1))
            for k in range(2):
                pe.matmul(sums_at(par)[:, k * 512:(k + 1) * 512], lhs, weighted_v[:, slot, k * 512:(k + 1) * 512], **ends)
            pe.matmul(den_at(par), lhs, prob[:, par, c, :], **ends).then_inc(summed, 1)

        def step(t, par, half):
            ahead = 2 if tf else CMAX
            if has(t):
                for c in range(min(ahead, edge_tiles(t))):
                    spread_queries(t, c, par, half)
            if tf and has(t, 1):
                turn_scores(t - 1, 2)
            for c in range(CMAX):
                if has(t, 2) and c < edge_tiles(t - 2):
                    sum_values(t - 2, c, par)
                if has(t) and c + ahead < edge_tiles(t):
                    spread_queries(t, c + ahead, par, half)
                turn_at = 5 if tf else 3
                if has(t, 1) and c in (turn_at, turn_at + 1):
                    turn_probs(t - 1, c - turn_at)
                if has(t) and tf and c in (7, 8):
                    turn_scores(t, c - 7)
                if has(t) and not tf and c in (6, 7, 8):
                    turn_scores(t, c - 6)
        steps(pe, step)

    def scalar(act):
        def copy_scores(t, k):
            lo, hi = k * GROUP_S, min((k + 1) * GROUP_S, edge_tiles(t))
            act.wait_ge(tp_full, turn_of_scores(t, k))
            act.copy(turned[0:G, lo * P:hi * P], bank[6][0:G, 0:(hi - lo) * P]).then_inc(tp_read, 1)

        def widen(t, h, bits, wide, used, made):
            if not zero(t):
                act.wait_ge(used, g0(t - 1) + (edge_tiles(t - 1) if h else cut(t - 1)))
            lo, hi = (cut(t), edge_tiles(t)) if h else (0, cut(t))
            act.copy(wide[:, h:h + 1, 0:hi - lo, :], bits[:, bass.ds(t, 1), lo:hi, :]).then_inc(made, 1)

        def high(t, par):
            act.wait_ge(q_in[0], 16 * t + 16)
            if has(t, 2):
                act.wait_ge(spread_q, g0(t - 1))
            act.copy(q_parts[:, par, 0, :], q_tile[:, 0, :]).then_inc(q_high, 1)

        def middle(t, par):
            act.wait_ge(q_rest, t + 1)
            act.copy(q_parts[:, par, 1, :], q_tile[:, 0, :]).then_inc(q_mid, 1)

        def step(t, par, half):
            if tf and has(t, 1):
                copy_scores(t - 1, 2)
            if has(t):
                widen(t, 1, spread_bits, spread, spread_q, spread_made)
            if has(t, 2):
                widen(t - 2, 1, select_bits, select, summed, select_made)
            if tf and has(t, -1):
                high(t + 1, 1 - par)
                middle(t + 1, 1 - par)
            if has(t, 1):
                u, s, C = t - 1, 1 - par, edge_tiles(t - 1)
                act.wait_ge(shifted, u + 1)
                act.activation(turned[0:G, 0:C * P], turned[0:G, 0:C * P], ACT.Exp, scale=SCALE).then_inc(prob_ready, 1)
                for m in range(2):
                    lo, hi = m * GROUP_P, min((m + 1) * GROUP_P, C)
                    act.wait_ge(tp_full, turn_of_probs(u, m))
                    if m == 0 and has(u, 2):
                        act.wait_ge(summed, g0(u - 1))
                    act.copy(prob[:, s, lo:hi, :], bank[6][:, 0:(hi - lo) * G].rearrange("p (c g) -> p c g", g=G)).then_inc(tp_read, 1)
            if has(t):
                for k in range(2 if tf else 3):
                    copy_scores(t, k)
            if has(t, -1):
                widen(t + 1, 0, spread_bits, spread, spread_q, spread_made)
            if has(t, 1):
                widen(t - 1, 0, select_bits, select, summed, select_made)

        widen(0, 0, spread_bits, spread, spread_q, spread_made)
        if tf:
            high(0, 0)
            middle(0, 0)
        steps(act, step)

    def vector(v):
        def product(t, c):
            slot, (k_slot, used) = slot_of(t, c, 2)[0], slot_of(t, c, K_RING)
            v.wait_ge(k_landed[k_slot], 16 * used + 16)
            v.wait_ge(spread_q, g0(t) + c + 1)
            if not (zero(t) and c < 2):
                v.wait_ge(score_made, g0(t) + c - 1)
            v.tensor_tensor(prod[:, slot, :], pair[slot][:], k_ring[:, k_slot, :], ALU.mult).then_inc(prod_made, 1)

        def score_of(t, c):
            slot = slot_of(t, c, 2)[0]
            v.wait_ge(prod_made, g0(t) + c + 1)
            if has(t, 1) and c in (0, 2 * GROUP_S):
                v.wait_ge(tp_full, turn_of_scores(t - 1, 1 + c // (2 * GROUP_S)))
            v.tensor_reduce(score[:, c, :], prod[:, slot, :].rearrange("p (g w) -> p g w", w=W), AX.X, ALU.add
                            ).then_inc(score_made, 1)

        def scores_gat(t, par, half):
            C = edge_tiles(t)
            v.wait_ge(spread_q, g0(t) + C)
            v.wait_ge(sj_in[par], 16 * (CREST * (half + 1) + (CMAX - CREST if par == 0 else 0)))
            if not zero(t):
                v.wait_ge(score_made, t)
                v.wait_ge(tp_full, turn_of_scores(t - 1, 2))
            v.tensor_tensor(raw[:, 0:C, :], bank[0][:, 0:C * B].rearrange("p (c b) -> p c b", b=B),
                            sj_edge[:, par, 0:C, :], ALU.add).then_inc(raw_made, 1)
            v.wait_ge(raw_made, t + 1)
            v.scalar_tensor_tensor(score[:, 0:C, :], raw[:, 0:C, :], SLOPE, raw[:, 0:C, :], ALU.mult, ALU.max
                                   ).then_inc(score_made, 1)

        def shift_1(t):
            E = edge_tiles(t) * P
            v.wait_ge(tp_read, turn_of_scores(t, 2))
            v.wait_ge(start_in, 16 * t + 16)
            if not zero(t):
                v.wait_ge(shifted, t)
            v.tensor_tensor_scan(row_max[0:G, 0:E], row_start[0:G, 0:E], turned[0:G, 0:E], -BIG, ALU.add, ALU.max
                                 ).then_inc(scan_fwd, 1)

        def shift_2(t):
            E = edge_tiles(t) * P
            v.wait_ge(scan_fwd, t + 1)
            back = row_max[0:G, 0:E][:, ::-1]
            v.tensor_tensor_scan(back, row_start[0:G, 1:E + 1][:, ::-1], back, -BIG, ALU.add, ALU.max
                                 ).then_inc(scan_back, 1)

        def shift_3(t):
            E = edge_tiles(t) * P
            v.wait_ge(scan_back, t + 1)
            v.tensor_tensor(turned[0:G, 0:E], turned[0:G, 0:E], row_max[0:G, 0:E], ALU.subtract).then_inc(shifted, 1)

        def divide(t, par, uses):
            v.wait_ge(summed, g0(t) + edge_tiles(t))
            if not zero(t):
                v.wait_ge(o_ready, t)
            v.tensor_scalar(den, den_at(par), TINY, None, ALU.max).then_inc(den_step, 1)
            v.wait_ge(den_step, 2 * t + 1)
            v.reciprocal(den, den).then_inc(den_step, 1)
            v.wait_ge(den_step, 2 * t + 2)
            if has(t, 2):
                v.wait_ge(o_out[par], 16 * uses)
            v.tensor_tensor(o_stage[:, par, :].rearrange("p (g w) -> p g w", w=W), sums_at(par)[:].rearrange("p (g w) -> p g w", w=W),
                            den.rearrange("p (g a) -> p g a", a=1).broadcast_to([P, G, W]), ALU.mult).then_inc(o_ready, 1)

        def step(t, par, half):
            if tf:
                if has(t, 2):
                    weigh(v, t - 2, 0, par, weighed_v)
                for c in range(CMAX):
                    if has(t) and c < edge_tiles(t):
                        product(t, c)
                    if has(t, 2) and c + 1 < edge_tiles(t - 2) and c + 1 not in BY_POOL:
                        weigh(v, t - 2, c + 1, par, weighed_v)
                    if has(t) and c < edge_tiles(t):
                        score_of(t, c)
                    if has(t, 1) and c in (1, 2, 3):
                        (shift_1, shift_2, shift_3)[c - 1](t - 1)
            else:
                for c in range(CMAX):
                    if has(t, 2) and c < edge_tiles(t - 2):
                        weigh(v, t - 2, c, par, weighed_v)
                    if has(t, 1) and c == 2:
                        for piece in (shift_1, shift_2, shift_3):
                            piece(t - 1)
                    if has(t, LATE) and c == 5:
                        divide(t - LATE, 1 - par, half + (par - LATE) // 2)
                    if has(t) and c == 5:
                        scores_gat(t, par, half)
            if tf and has(t, LATE):
                divide(t - LATE, par, half - 1)
        steps(v, step)

    return gpsimd, sync, tensor, scalar, vector


def post_gat(nc, sem, carve, bank, w, L, ident, eps_col, x_rows, ao, y_rows, weave):
    x_tile, o_tile, y, normal, z, moved_z, stats, mv, sd, rs, shift = carve(
        (2, BD), (2, BD), (2, BD), (2, BD), (2, BD), (2, BD), (B, 6), (2, B, 2), (2, B), (2, B), (2, B))
    new = lambda name: sem(f"{name}{L}")
    x_in, o_in = [new("px0_"), new("px1_")], [new("po0_"), new("po1_")]
    stored = [new("st0_"), new("st1_")]
    y_made, stats_made, moments, roots, inverse, factors = new("y_made"), new("stats_made"), new("moments"), new("roots"), new("inverse"), new("factors")
    normed, scaled, moved = new("normed"), new("scaled"), new("moved")
    x_loads, stores = len(x_rows(0)), len(y_rows(0))
    following = weave((moved_z, moved)) if weave else None

    def turns(eng, turn):
        for k in range(6):
            turn(k, k % 2, k // 2)
        with eng.Fori(3, RT // 2 - 1) as i:
            turn(2 * i, 0, i)
            turn(2 * i + 1, 1, i)
        for k in range(RT - 2, RT + 4):
            turn(k, k % 2, k // 2)

    def has(k, lag=0):
        return not isinstance(k, int) or 0 <= k - lag < RT

    def evacuations(k, par, i, evacuate, copy_turned=None):
        for half in range(2):
            if copy_turned and has(k, 3):
                copy_turned(2 * (k - 3) + half, 2 * (1 - par) + half)
            lag = 4 - half
            if has(k, lag):
                evacuate(2 * (k - lag) + 1 - half, 2 * ((par + lag) % 2) + 1 - half, i + (par - lag) // 2,
                         isinstance(k, int) and k - lag < 2)

    as3 = lambda x: x.rearrange("p (b d) -> p b d", b=B)
    with nc.Block() as block:
        @block.sync
        def _(sp):
            def load(t, par):
                for src, lo, hi in x_rows(t):
                    sp.dma_start(x_tile[lo:hi, par, :] if len(src.shape) == 2 else as3(x_tile[lo:hi, par, :]), src
                                 ).then_inc(x_in[par], 16)
                sp.dma_start(o_tile[:, par, :], ao[bass.ds(t, 1)].rearrange("r q n -> (r q) n")).then_inc(o_in[par], 16)

            def turn(k, par, i):
                if has(k, -2):
                    sp.wait_ge(y_made, k + 1)
                    load(k + 2, par)
                if has(k, 3):
                    sp.wait_ge(moved, k - 2)
                    for dst, lo, hi in y_rows(k - 3):
                        src = moved_z[lo:hi, 1 - par, :]
                        sp.dma_start(dst, src if len(dst.shape) == 2 else as3(src)).then_inc(stored[1 - par], 16)

                if following and has(k, 4):
                    following.store(sp, k - 4, par)

            load(0, 0)
            load(1, 1)
            turns(sp, turn)
            for s in range(2):
                sp.wait_ge(stored[s], 16 * stores * (RT // 2))
            if following:
                following.all_stored(sp)

        if following:
            @block.tensor
            def _(pe):
                following.tensor(pe)

        @block.scalar
        def _(act):
            def turn(k, par, i):
                if has(k, 1):
                    t, s = k - 1, 1 - par
                    act.wait_ge(factors, k)
                    if has(t, 2):
                        act.wait_ge(scaled, t - 1)
                    for b in range(B):
                        ins = act.activation(normal[:, s, b * D:(b + 1) * D], y[:, s, b * D:(b + 1) * D], ACT.Identity,
                                             bias=shift[:, s, b:b + 1], scale=rs[:, s, b:b + 1])
                    ins.then_inc(normed, 1)
                if has(k):
                    act.wait_ge(moments, k + 1)
                    if has(k, 2):
                        act.wait_ge(inverse, k - 1)
                    act.activation(sd[:, par, :], mv[:, par, :, 1], ACT.Sqrt, bias=eps_col[:, 0:1]).then_inc(roots, 1)
                if following:
                    evacuations(k, par, i, following.evacuate_a, lambda n, group: following.copy_turned(act, n, group))
            turns(act, turn)

        @block.vector
        def _(v):
            def turn(k, par, i):
                if has(k, 1):
                    s = 1 - par
                    v.wait_ge(roots, k)
                    v.reciprocal(rs[:, s, :], sd[:, s, :]).then_inc(inverse, 1)
                    v.wait_ge(inverse, k)
                    v.scalar_tensor_tensor(shift[:, s, :], mv[:, s, :, 0], -1.0, rs[:, s, :], ALU.mult, ALU.mult
                                           ).then_inc(factors, 1)
                if has(k):
                    v.wait_ge(x_in[par], 16 * x_loads * (i + 1))
                    v.wait_ge(o_in[par], 16 * i + 16)
                    if has(k, 2):
                        v.wait_ge(normed, k - 1)
                    if has(k, 1):
                        v.wait_ge(moments, k)
                    v.tensor_tensor(y[:, par, :], x_tile[:, par, :], o_tile[:, par, :], ALU.add).then_inc(y_made, 1)
                    v.wait_ge(y_made, k + 1)
                    for b in range(B):
                        ins = v.bn_stats(stats[:, b, :], y[:, par, b * D:(b + 1) * D])
                    ins.then_inc(stats_made, 1)
                    hold(v, stats_made, k + 1)
                    for b in range(B):
                        ins = v.bn_aggr(mv[:, par, b, :], stats[:, b, :])
                    ins.then_inc(moments, 1)
                if has(k, 2):
                    v.wait_ge(normed, k - 1)
                    if has(k, 4):
                        v.wait_ge(moved, k - 3)
                    v.tensor_tensor(as3(z[:, par, :]), as3(normal[:, par, :]), w["gb"][:, 0:1, :].broadcast_to([P, B, D]),
                                    ALU.mult).then_inc(scaled, 1)
                if following:
                    evacuations(k, par, i, following.evacuate_v)
            turns(v, turn)

        @block.gpsimd
        def _(g):
            def turn(k, par, i):
                if has(k, 2):
                    g.wait_ge(scaled, k - 1)
                    if has(k, 4):
                        g.wait_ge(stored[par], 16 * stores * (i - 1))
                        if following:
                            g.wait_ge(following.turned, 2 * (k - 4) + 2)
                    g.tensor_tensor(as3(moved_z[:, par, :]), as3(z[:, par, :]), w["gb"][:, 1:2, :].broadcast_to([P, B, D]),
                                    ALU.add).then_inc(moved, 1)
            turns(g, turn)


def post_tf(nc, sem, carve, bank, w, L, ident, eps_col, x_rows, ao, y_rows):
    GW = 4 * D
    GROUPS = 2 * RT
    (x_tile, o_tile, o_turned, xb, y1, normal1, z1, x1, x1_turned, hidden, x1b, y2, normal2, z2, x2, stats1, stats2, mv1,
     mv2, sd1, sd2, rs1, rs2, shift1, shift2) = carve(
        (4, GW), (4, GW), (2, GW), (2, GW), (2, GW), (2, GW), (2, GW), (4, GW), (2, GW), (2, FC, GW), (4, GW), (2, GW),
        (2, GW), (2, GW), (4, GW), (4, 6), (4, 6), (2, 4, 2), (2, 4, 2), (2, 4), (2, 4), (2, 4), (2, 4), (2, 4), (2, 4))
    new = lambda name: sem(f"{name}{L}")
    x_in, o_in = [new(f"fx{s}_") for s in range(2)], [new(f"fo{s}_") for s in range(2)]
    o_tr, o_copied, o_prod = new("o_tr"), new("o_copied"), new("o_prod")
    x1_tr, x1_copied, h_prod, h_relu, y2_prod = new("x1_tr"), new("x1_copied"), new("h_prod"), new("h_relu"), new("y2_prod")
    xb_made, x1_made, x1b_made, x2_made = new("xb_made"), new("x1_made"), new("x1b_made"), new("x2_made")
    norm_sems = lambda m: [new(f"{name}{m}_") for name in ("y_made", "stats_made", "moments", "roots", "inverse", "factors", "normed", "scaled")]
    norm1, norm2 = norm_sems(1), norm_sems(2)
    y1_made, scaled1 = norm1[0], norm1[-1]
    y2_made, scaled2 = norm2[0], norm2[-1]
    stored = [new(f"fst{s}_") for s in range(2)]
    x_loads, stores = len(x_rows(0)), len(y_rows(0))

    def turns(eng, turn):
        for k in range(8):
            turn(k, k % 4, k // 4)
        with eng.Fori(2, GROUPS // 4 - 1) as i:
            for j in range(4):
                turn(4 * i + j, j, i)
        for k in range(GROUPS - 4, GROUPS + 6):
            turn(k, k % 4, k // 4)

    def has(k, lag=0):
        return not isinstance(k, int) or 0 <= k - lag < GROUPS

    as3 = lambda x: x.rearrange("p (b d) -> p b d", b=4)
    row = lambda r: r.broadcast_to([P, 4, D])

    with nc.Block() as block:
        @block.sync
        def _(sp):
            def turn(k, j, i):
                if has(k, 5) and (j - 5) % 2 == 1:
                    s4 = (j - 5) % 4
                    t = 2 * i + (j - 5) // 2
                    sp.wait_ge(x2_made, k - 4)
                    tile_in = x2[:, s4 - 1:s4 + 1, :].rearrange("p h n -> p (h n)")
                    for dst, lo, hi in y_rows(t):
                        sp.dma_start(dst, tile_in[lo:hi]).then_inc(stored[s4 // 2], 16)
            turns(sp, turn)
            for s in range(2):
                sp.wait_ge(stored[s], 16 * stores * (RT // 2))

        @block.tensor
        def _(pe):
            def turn_o(n, j, i):
                if j % 2 == 0:
                    pe.wait_ge(o_in[j // 2], 16 * i + 16)
                if has(n, 1):
                    pe.wait_ge(o_copied, n)
                for b in range(4):
                    tr = pe.transpose(bank[0][:, b * P:(b + 1) * P], o_tile[:, j, b * D:(b + 1) * D], ident[:])
                tr.then_inc(o_tr, 1)

            def turn(k, j, i):
                if has(k):
                    pe.wait_ge(o_copied, k + 1)
                    if has(k, 1):
                        pe.wait_ge(y1_made, k)
                    for b in range(4):
                        mm = pe.matmul(bank[1][:, b * D:(b + 1) * D], o_turned[:, j % 2, b * P:(b + 1) * P], w["wo"][:],
                                       start=True, stop=True)
                    mm.then_inc(o_prod, 1)
                if has(k, 2):
                    n, s = k - 2, (j - 2) % 4
                    pe.wait_ge(x1_made, n + 1)
                    if has(n, 1):
                        pe.wait_ge(x1_copied, n)
                    for b in range(4):
                        tr = pe.transpose(bank[2][:, b * P:(b + 1) * P], x1[:, s, b * D:(b + 1) * D], ident[:])
                    tr.then_inc(x1_tr, 1)
                if has(k, 3):
                    n, s = k - 3, (j - 3) % 2
                    pe.wait_ge(h_relu, FC * n + FC)
                    if has(n, 1):
                        pe.wait_ge(y2_made, n)
                    for b in range(4):
                        for c in range(FC):
                            mm = pe.matmul(bank[5][:, b * D:(b + 1) * D], hidden[:, s, c, b * P:(b + 1) * P], w["w2"][:, c, :],
                                           start=(c == 0), stop=(c == FC - 1))
                    mm.then_inc(y2_prod, 1)
                if has(k, -1):
                    turn_o(k + 1, (j + 1) % 4, i + (j + 1) // 4)
                if has(k, 2):
                    n, s = k - 2, (j - 2) % 2
                    pe.wait_ge(x1_copied, n + 1)
                    for c in range(FC):
                        if has(n, 1):
                            pe.wait_ge(h_relu, FC * (n - 1) + c + 1)
                        pe.matmul(bank[3 + c], w["w1"][:, c * P:(c + 1) * P], x1_turned[:, s, :], start=True, stop=True
                                  ).then_inc(h_prod, 1)

            turn_o(0, 0, 0)
            turns(pe, turn)

        @block.scalar
        def _(act):
            def load(n, j, t):
                par = j // 2
                if has(n, 4):
                    act.wait_ge(y1_made, n - 2)
                    act.wait_ge(xb_made, n - 2)
                    act.wait_ge(o_tr, n - 2)
                for src, lo, hi in x_rows(t):
                    act.dma_start(x_tile[lo:hi, j:j + 2, :].rearrange("p h n -> p (h n)"), src).then_inc(x_in[par], 16)
                act.dma_start(o_tile[:, j:j + 2, :], ao[bass.ds(t, 1)].rearrange("r q (h n) -> q (r h) n", h=2)).then_inc(o_in[par], 16)

            def copy_o(n, j):
                act.wait_ge(o_tr, n + 1)
                if has(n, 2):
                    act.wait_ge(o_prod, n - 1)
                act.copy(o_turned[:, j % 2, :], bank[0]).then_inc(o_copied, 1)

            def normalise(n, s, y, normal, rs, shift, sems):
                factors, normed, scaled = sems[5:]
                act.wait_ge(factors, n + 1)
                if has(n, 2):
                    act.wait_ge(scaled, n - 1)
                for b in range(4):
                    ins = act.activation(normal[:, s, b * D:(b + 1) * D], y[:, s, b * D:(b + 1) * D], ACT.Identity,
                                         bias=shift[:, s, b:b + 1], scale=rs[:, s, b:b + 1])
                ins.then_inc(normed, 1)

            def root(n, s, sd, mv, sems):
                moments, roots, inverse = sems[2:5]
                act.wait_ge(moments, n + 1)
                if has(n, 2):
                    act.wait_ge(inverse, n - 1)
                act.activation(sd[:, s, :], mv[:, s, :, 1], ACT.Sqrt, bias=eps_col[:, 0:1]).then_inc(roots, 1)

            def turn(k, j, i):
                if has(k, -2) and has(k, 1) and j % 2 == 0:
                    load(k + 2, (j + 2) % 4, 2 * i + (j + 2) // 2)
                if has(k, 1):
                    normalise(k - 1, (j - 1) % 2, y1, normal1, rs1, shift1, norm1)
                if has(k, 2):
                    n, s = k - 2, j % 2
                    act.wait_ge(x1_tr, n + 1)
                    if has(n, 2):
                        act.wait_ge(h_prod, FC * (n - 1))
                    act.copy(x1_turned[:, s, :], bank[2]).then_inc(x1_copied, 1)
                if has(k, 4):
                    normalise(k - 4, j % 2, y2, normal2, rs2, shift2, norm2)
                if has(k):
                    root(k, j % 2, sd1, mv1, norm1)
                if has(k, -1):
                    copy_o(k + 1, j + 1)
                if has(k, 2):
                    n, s = k - 2, j % 2
                    if has(n, 2):
                        act.wait_ge(y2_prod, n - 1)
                    for c in range(FC):
                        act.wait_ge(h_prod, FC * n + c + 1)
                        act.activation(hidden[:, s, c, :], bank[3 + c], ACT.Relu, bias=w["b1"][:, c:c + 1]).then_inc(h_relu, 1)
                if has(k, 3):
                    root(k - 3, (j - 3) % 2, sd2, mv2, norm2)

            load(0, 0, 0)
            load(2, 2, 1)
            copy_o(0, 0)
            turns(act, turn)

        @block.vector
        def _(v):
            def factors(n, s, sd, mv, rs, shift, sems):
                _, _, _, roots, inverse, made, normed, _ = sems
                v.wait_ge(roots, n + 1)
                if has(n, 2):
                    v.wait_ge(normed, n - 1)
                v.reciprocal(rs[:, s, :], sd[:, s, :]).then_inc(inverse, 1)
                v.wait_ge(inverse, n + 1)
                v.scalar_tensor_tensor(shift[:, s, :], mv[:, s, :, 0], -1.0, rs[:, s, :], ALU.mult, ALU.mult).then_inc(made, 1)

            def add_and_moments(n, s, y, product, addend, stats, mv, sems):
                y_made, stats_made, moments, _, _, _, normed, _ = sems
                if has(n, 2):
                    v.wait_ge(normed, n - 1)
                if has(n, 1):
                    v.wait_ge(moments, n)
                v.tensor_tensor(y[:, s, :], product, addend, ALU.add).then_inc(y_made, 1)
                v.wait_ge(y_made, n + 1)
                for b in range(4):
                    ins = v.bn_stats(stats[:, b, :], y[:, s, b * D:(b + 1) * D])
                ins.then_inc(stats_made, 1)
                hold(v, stats_made, n + 1)
                for b in range(4):
                    ins = v.bn_aggr(mv[:, s, b, :], stats[:, b, :])
                ins.then_inc(moments, 1)

            def scale(n, s, z, normal, gamma, sems, z_used):
                normed, scaled = sems[6:]
                v.wait_ge(normed, n + 1)
                if has(n, 2):
                    v.wait_ge(z_used, n - 1)
                v.tensor_tensor(as3(z[:, s, :]), as3(normal[:, s, :]), row(w["gb"][:, gamma:gamma + 1, :]), ALU.mult
                                ).then_inc(scaled, 1)

            def turn(k, j, i):
                if has(k, 1):
                    factors(k - 1, (j - 1) % 2, sd1, mv1, rs1, shift1, norm1)
                if has(k, 4):
                    factors(k - 4, j % 2, sd2, mv2, rs2, shift2, norm2)
                if has(k):
                    v.wait_ge(o_prod, k + 1)
                    v.wait_ge(xb_made, k + 1)
                    add_and_moments(k, j % 2, y1, bank[1], xb[:, j % 2, :], stats1, mv1, norm1)
                if has(k, 1):
                    scale(k - 1, (j - 1) % 2, z1, normal1, 0, norm1, x1_made)
                if has(k, 3):
                    n, s = k - 3, (j - 3) % 2
                    v.wait_ge(y2_prod, n + 1)
                    v.wait_ge(x1b_made, n + 1)
                    add_and_moments(n, s, y2, bank[5], x1b[:, (j - 3) % 4, :], stats2, mv2, norm2)
                if has(k, 4):
                    scale(k - 4, j % 2, z2, normal2, 2, norm2, x2_made)
            turns(v, turn)

        @block.gpsimd
        def _(g):
            def add_bo(n, j, i):
                if j % 2 == 0:
                    g.wait_ge(x_in[j // 2], 16 * x_loads * (i + 1))
                if has(n, 2):
                    g.wait_ge(y1_made, n - 1)
                g.tensor_tensor(as3(xb[:, j % 2, :]), as3(x_tile[:, j, :]), row(w["bias"][:, 0:1, :]), ALU.add).then_inc(xb_made, 1)

            def turn(k, j, i):
                if has(k, -1):
                    add_bo(k + 1, (j + 1) % 4, i + (j + 1) // 4)
                if has(k, 1):
                    n, s, s4 = k - 1, (j - 1) % 2, (j - 1) % 4
                    g.wait_ge(scaled1, n + 1)
                    if has(n, 4):
                        g.wait_ge(x1_tr, n - 3)
                        g.wait_ge(x1b_made, n - 3)
                    g.tensor_tensor(as3(x1[:, s4, :]), as3(z1[:, s, :]), row(w["gb"][:, 1:2, :]), ALU.add).then_inc(x1_made, 1)
                    g.wait_ge(x1_made, n + 1)
                    if has(n, 4):
                        g.wait_ge(y2_made, n - 3)
                    g.tensor_tensor(as3(x1b[:, s4, :]), as3(x1[:, s4, :]), row(w["bias"][:, 1:2, :]), ALU.add).then_inc(x1b_made, 1)
                if has(k, 4):
                    n, s, s4 = k - 4, j % 2, j % 4
                    g.wait_ge(scaled2, n + 1)
                    if has(n, 4) and s4 % 2 == 0:
                        g.wait_ge(stored[s4 // 2], 16 * stores * (i - 1))
                    g.tensor_tensor(as3(x2[:, s4, :]), as3(z2[:, s, :]), row(w["gb"][:, 3:4, :]), ALU.add).then_inc(x2_made, 1)

            add_bo(0, 0, 0)
            turns(g, turn)


_INS = ['x', 'adj'] + [f'L{L}_gnn_{n}' for L in (0, 3) for n in ('W', 'a_src', 'a_dst', 'ln_gamma', 'ln_beta')] + \
       [f'L{L}_gnn_{n}' for L in (1, 2) for n in ('Wq', 'Wk', 'Wv', 'Wo', 'bo', 'ln1_g', 'ln1_b', 'W1', 'b1', 'W2', 'b2',
                                                  'ln2_g', 'ln2_b')]


def kernel(**inputs):
    import numpy as _np
    import concourse.bacc as _bacc
    from concourse import mybir as _mybir
    from concourse.bass_utils import run_bass_kernel_spmd as _run

    nc = _bacc.Bacc("TRN2", target_bir_lowering=False, num_devices=1)
    arrays, args = {}, {}
    for name in _INS:
        x = _np.ascontiguousarray(inputs[name])
        arrays[f"in_{name}_dram"] = x
        args[name] = nc.dram_tensor(f"in_{name}_dram", x.shape, _mybir.dt.from_np(x.dtype), kind="ExternalInput").ap()
    out = nc.dram_tensor("out_0_dram", (B, N, D), _mybir.dt.float32, kind="ExternalOutput").ap()
    build(nc, args, out)
    r = _run(nc, [arrays], core_ids=[0])
    return r.results[0]["out_0_dram"]
```
